# Optimizing a Trainium2 kernel written in Bass

```python
import numpy as np
import jax
import jax.numpy as jnp

def _softmax(x, axis=-1):
    return jax.nn.softmax(x, axis=axis)

def _gelu(x):
    return jax.nn.gelu(x, approximate=True)

def _silu(x):
    return jax.nn.silu(x)

def _sigmoid(x):
    return jax.nn.sigmoid(x)

def _layernorm(x, axis=-1, eps=1e-05):
    m = jnp.mean(x, axis=axis, keepdims=True)
    v = jnp.var(x, axis=axis, keepdims=True)
    return (x - m) / jnp.sqrt(v + eps)

def _scatter_add(tgt, idx, src, axis=0):
    return tgt.at[idx].add(src)

def _segment_sum(src, seg, n):
    return jax.ops.segment_sum(src, seg, n)
kernel_name = 'mk_xattn_ffn_d2_seqx_r8_a1fc9b'

def setup_inputs(seed: int=0):
    np.random.seed(seed)
    _w = jnp.asarray

    def _rec_inputs():
        import jax
        import jax.numpy as jnp
        _rk = jax.random.key(seed)
        x = -0.0002928 + 1 * jax.random.normal(jax.random.fold_in(_rk, 1), (4, 512, 128), jnp.float32)
        _lenS = 512 - jax.random.randint(jax.random.fold_in(_rk, 7), (4,), 0, max(1, 512 // 4) + 1, jnp.int32)
        _lenS2 = 77 - jax.random.randint(jax.random.fold_in(_rk, 8), (4,), 0, max(1, 77 // 4) + 1, jnp.int32)
        _ctx_1024P = jax.random.normal(jax.random.fold_in(_rk, 11), (4, 16, 128), jnp.float32)
        _ctx_1024c = jax.random.dirichlet(jax.random.fold_in(_rk, 511), 0.3 * jnp.ones((16,), jnp.float32), (4, 77))
        _ctx_1024t = jnp.einsum('bsk,bkd->bsd', _ctx_1024c, _ctx_1024P)
        _ctx_1024t = _ctx_1024t * jax.lax.rsqrt(jnp.mean(jnp.square(_ctx_1024t)) + 1e-12) * 0.953939
        ctx_1024 = -1.39393e-06 + 0.999914 * (_ctx_1024t + 0.3 * jax.random.normal(jax.random.fold_in(_rk, 611), (4, 77, 128), jnp.float32))
        _validS = jnp.arange(512)[None, :] < _lenS[:, None]
        _validS2 = jnp.arange(77)[None, :] < _lenS2[:, None]
        _causal = jnp.tril(jnp.ones((512, 512), dtype=bool))
        mask_BxS2_ik0 = jnp.where(jnp.broadcast_to(_validS2[:, :], (4, 77)), 0, 1).astype(jnp.int32)
        return (x, ctx_1024, mask_BxS2_ik0)
    x, ctx_1024, mask_BxS2_ik0 = _rec_inputs()

    def _L0_xattn_setup():
        import jax, jax.numpy as jnp
        import numpy as np
        DIM = 128
        NUM_HEADS = 16
        HEAD_DIM = DIM // NUM_HEADS
        EPS = 1e-06
        SCALE = HEAD_DIM ** (-0.5)

        def _rmsnorm(x, w):
            dt = x.dtype
            xf = x.astype(jnp.float32)
            var = jnp.mean(xf * xf, axis=-1, keepdims=True)
            return w * (xf * jax.lax.rsqrt(var + EPS)).astype(dt)

        def _heads(x, B):
            return x.reshape(B, -1, NUM_HEADS, HEAD_DIM).transpose(0, 2, 1, 3)
        key = jax.random.key(seed)
        ks = jax.random.split(key, 12)
        B, Lq, Lk = (2, 256, 256)
        inp = {'query': jax.random.normal(ks[0], (B, Lq, DIM), dtype=jnp.float32), 'key': jax.random.normal(ks[1], (B, Lk, DIM), dtype=jnp.float32), 'value': jax.random.normal(ks[2], (B, Lk, DIM), dtype=jnp.float32), 'attention_mask': jax.random.randint(ks[3], (B, Lk), 0, 2, dtype=jnp.int32), 'Wq': jax.random.normal(ks[4], (DIM, DIM), dtype=jnp.float32) * 0.02, 'bq': jnp.zeros((DIM,), dtype=jnp.float32), 'Wk': jax.random.normal(ks[5], (DIM, DIM), dtype=jnp.float32) * 0.02, 'bk': jnp.zeros((DIM,), dtype=jnp.float32), 'Wv': jax.random.normal(ks[6], (DIM, DIM), dtype=jnp.float32) * 0.02, 'bv': jnp.zeros((DIM,), dtype=jnp.float32), 'Wo': jax.random.normal(ks[7], (DIM, DIM), dtype=jnp.float32) * 0.02, 'bo': jnp.zeros((DIM,), dtype=jnp.float32), 'q_norm_w': jnp.ones((HEAD_DIM,), dtype=jnp.float32), 'k_norm_w': jnp.ones((HEAD_DIM,), dtype=jnp.float32)}
        return inp
    _L0_xattn_all = _L0_xattn_setup()
    _L0_xattn_in = {k: v for k, v in _L0_xattn_all.items() if k in ('Wq', 'bq', 'Wk', 'bk', 'Wv', 'bv', 'Wo', 'bo', 'q_norm_w', 'k_norm_w')}
    del _L0_xattn_all

    def _L0_ffn_setup():
        import jax, jax.numpy as jnp
        import numpy as np
        DIM = 128
        HIDDEN = 384
        SCALE = 1.0 / 127.0

        def _dequant(w_int, dtype):
            return w_int.astype(dtype) * jnp.asarray(SCALE, dtype)
        key = jax.random.key(seed)
        k_x, k_g, k_u, k_d = jax.random.split(key, 4)
        x = jax.random.normal(k_x, (4, 256, DIM), dtype=jnp.float32)
        w_gate = jax.random.randint(k_g, (HIDDEN, DIM), -127, 128, dtype=jnp.int32)
        w_up = jax.random.randint(k_u, (HIDDEN, DIM), -127, 128, dtype=jnp.int32)
        w_down = jax.random.randint(k_d, (DIM, HIDDEN), -127, 128, dtype=jnp.int32)
        return {'x': x, 'w_gate': w_gate, 'w_up': w_up, 'w_down': w_down}
    _L0_ffn_all = _L0_ffn_setup()
    _L0_ffn_in = {k: v for k, v in _L0_ffn_all.items() if k in ('w_gate', 'w_up', 'w_down')}
    del _L0_ffn_all

    def _L1_xattn_setup():
        import jax, jax.numpy as jnp
        import numpy as np
        from jax import lax
        BIG = jnp.float32(1e+30)

        def _pairwise_euclidean(a, b):
            aa = jnp.sum(a * a, axis=-1)[:, None]
            bb = jnp.sum(b * b, axis=-1)[None, :]
            ab = a @ b.T
            return jnp.sqrt(jnp.maximum(aa + bb - 2.0 * ab, 0.0))

        def _dtw_cost(D):
            row0 = jnp.cumsum(D[0])

            def row_step(prev_row, d_row):
                first = d_row[0] + prev_row[0]

                def col_step(left, inp):
                    d_ij, up, diag = inp
                    r = d_ij + jnp.minimum(jnp.minimum(up, left), diag)
                    return (r, r)
                _, rest = lax.scan(col_step, first, (d_row[1:], prev_row[1:], prev_row[:-1]))
                row = jnp.concatenate([first[None], rest])
                return (row, row)
            _, rows = lax.scan(row_step, row0, D[1:])
            return jnp.concatenate([row0[None], rows], axis=0)

        def _backtrack(R, T1, T2):
            L = T1 + T2 - 1

            def step(carry, _):
                i, j, done = carry
                valid = jnp.logical_not(done)
                cd = jnp.where((i > 0) & (j > 0), R[jnp.maximum(i - 1, 0), jnp.maximum(j - 1, 0)], BIG)
                cu = jnp.where(i > 0, R[jnp.maximum(i - 1, 0), j], BIG)
                cl = jnp.where(j > 0, R[i, jnp.maximum(j - 1, 0)], BIG)
                choice = jnp.argmin(jnp.stack([cd, cu, cl]))
                ni = jnp.where(choice <= 1, i - 1, i)
                nj = jnp.where((choice == 0) | (choice == 2), j - 1, j)
                at_origin = (i == 0) & (j == 0)
                ni = jnp.where(at_origin, 0, ni)
                nj = jnp.where(at_origin, 0, nj)
                return ((ni, nj, done | at_origin), (i, j, valid))
            init = (jnp.int32(T1 - 1), jnp.int32(T2 - 1), jnp.bool_(False))
            _, (i_idx, j_idx, valid) = lax.scan(step, init, None, length=L)
            return (i_idx, j_idx, valid)

        def _align_one(small, large):
            T_small, d = small.shape
            T_large = large.shape[0]
            D = _pairwise_euclidean(small, large)
            R = _dtw_cost(D)
            i_idx, j_idx, valid = _backtrack(R, T_small, T_large)
            contrib = small[i_idx] * valid[:, None].astype(small.dtype)
            expanded = jnp.zeros((T_large, d), dtype=small.dtype).at[j_idx].add(contrib)
            return expanded
        key = jax.random.key(seed)
        k1, k2 = jax.random.split(key)
        teacher = jax.random.normal(k1, (16, 50, 128), dtype=jnp.float32)
        student = jax.random.normal(k2, (16, 75, 128), dtype=jnp.float32)
        return {'teacher_features': teacher, 'student_features': student}
    _L1_xattn_all = _L1_xattn_setup()
    _L1_xattn_in = {k: v for k, v in _L1_xattn_all.items() if k in ()}
    del _L1_xattn_all

    def _L1_ffn_setup():
        import jax, jax.numpy as jnp
        import numpy as np
        B, S, H = (1, 128, 128)
        E, I = (8, 256)
        JITTER_EPS = 0.01

        def _sparse_mixer_top2(scores, jitter_eps):
            vals, idx = jax.lax.top_k(scores, 2)
            neg_inf = jnp.array(-jnp.inf, scores.dtype)
            t1 = vals[:, :1]
            f1 = jnp.maximum(jnp.abs(scores), t1)
            m1 = (t1 - scores) / f1 > 2 * jitter_eps
            p1 = jax.nn.softmax(jnp.where(m1, neg_inf, scores), axis=-1)
            mult1 = jnp.take_along_axis(p1, idx[:, :1], axis=-1)
            t2 = vals[:, 1:2]
            f2 = jnp.maximum(jnp.abs(scores), t2)
            m2 = (t2 - scores) / f2 > 2 * jitter_eps
            rows = jnp.arange(scores.shape[0])[:, None]
            s2 = scores.at[rows, idx[:, :1]].set(neg_inf)
            p2 = jax.nn.softmax(jnp.where(m2, neg_inf, s2), axis=-1)
            mult2 = jnp.take_along_axis(p2, idx[:, 1:2], axis=-1)
            return (jnp.concatenate([mult1, mult2], axis=-1), idx)
        key = jax.random.key(seed)
        ks = jax.random.split(key, 5)
        s_h = 1.0 / np.sqrt(H)
        s_i = 1.0 / np.sqrt(I)
        return {'hidden_states': jax.random.normal(ks[0], (B, S, H), jnp.float32), 'gate_w': jax.random.normal(ks[1], (E, H), jnp.float32) * s_h, 'w1': jax.random.normal(ks[2], (E, I, H), jnp.float32) * s_h, 'w2': jax.random.normal(ks[3], (E, H, I), jnp.float32) * s_i, 'w3': jax.random.normal(ks[4], (E, I, H), jnp.float32) * s_h}
    _L1_ffn_all = _L1_ffn_setup()
    _L1_ffn_in = {k: v for k, v in _L1_ffn_all.items() if k in ('gate_w', 'w1', 'w2', 'w3')}
    del _L1_ffn_all
    return {'x': x, 'ctx_1024': ctx_1024, 'mask_BxS2_ik0': mask_BxS2_ik0, 'L0_xattn_Wq': _L0_xattn_in['Wq'], 'L0_xattn_bq': _L0_xattn_in['bq'], 'L0_xattn_Wk': _L0_xattn_in['Wk'], 'L0_xattn_bk': _L0_xattn_in['bk'], 'L0_xattn_Wv': _L0_xattn_in['Wv'], 'L0_xattn_bv': _L0_xattn_in['bv'], 'L0_xattn_Wo': _L0_xattn_in['Wo'], 'L0_xattn_bo': _L0_xattn_in['bo'], 'L0_xattn_q_norm_w': _L0_xattn_in['q_norm_w'], 'L0_xattn_k_norm_w': _L0_xattn_in['k_norm_w'], 'L0_ffn_w_gate': _L0_ffn_in['w_gate'], 'L0_ffn_w_up': _L0_ffn_in['w_up'], 'L0_ffn_w_down': _L0_ffn_in['w_down'], 'L1_ffn_gate_w': _L1_ffn_in['gate_w'], 'L1_ffn_w1': _L1_ffn_in['w1'], 'L1_ffn_w2': _L1_ffn_in['w2'], 'L1_ffn_w3': _L1_ffn_in['w3']}

def reference(x, ctx_1024, mask_BxS2_ik0, L0_xattn_Wq, L0_xattn_bq, L0_xattn_Wk, L0_xattn_bk, L0_xattn_Wv, L0_xattn_bv, L0_xattn_Wo, L0_xattn_bo, L0_xattn_q_norm_w, L0_xattn_k_norm_w, L0_ffn_w_gate, L0_ffn_w_up, L0_ffn_w_down, L1_ffn_gate_w, L1_ffn_w1, L1_ffn_w2, L1_ffn_w3):
    import jax
    import jax.numpy as jnp

    def _L0_xattn_ref(query, key, value, attention_mask, Wq, bq, Wk, bk, Wv, bv, Wo, bo, q_norm_w, k_norm_w):
        import jax, jax.numpy as jnp
        import numpy as np
        DIM = 128
        NUM_HEADS = 16
        HEAD_DIM = DIM // NUM_HEADS
        EPS = 1e-06
        SCALE = HEAD_DIM ** (-0.5)

        def _rmsnorm(x, w):
            dt = x.dtype
            xf = x.astype(jnp.float32)
            var = jnp.mean(xf * xf, axis=-1, keepdims=True)
            return w * (xf * jax.lax.rsqrt(var + EPS)).astype(dt)

        def _heads(x, B):
            return x.reshape(B, -1, NUM_HEADS, HEAD_DIM).transpose(0, 2, 1, 3)
        B, Lq, D = query.shape
        q = _heads(query @ Wq.T + bq, B)
        k = _heads(key @ Wk.T + bk, B)
        v = _heads(value @ Wv.T + bv, B)
        q = _rmsnorm(q, q_norm_w)
        k = _rmsnorm(k, k_norm_w)
        attn = jnp.einsum('bhqd,bhkd->bhqk', q, k) * SCALE
        mask = attention_mask[:, None, None, :] == 0
        attn = jnp.where(mask, -jnp.inf, attn)
        attn = jax.nn.softmax(attn, axis=-1)
        out = jnp.einsum('bhqk,bhkd->bhqd', attn, v)
        out = out.transpose(0, 2, 1, 3).reshape(B, Lq, D)
        return out @ Wo.T + bo

    def _L0_ffn_ref(x, w_gate, w_up, w_down):
        import jax, jax.numpy as jnp
        import numpy as np
        DIM = 128
        HIDDEN = 384
        SCALE = 1.0 / 127.0

        def _dequant(w_int, dtype):
            return w_int.astype(dtype) * jnp.asarray(SCALE, dtype)
        wg = _dequant(w_gate, x.dtype)
        wu = _dequant(w_up, x.dtype)
        wd = _dequant(w_down, x.dtype)
        gate = jnp.einsum('bsd,hd->bsh', x, wg)
        up = jnp.einsum('bsd,hd->bsh', x, wu)
        h = jax.nn.silu(gate) * up
        return jnp.einsum('bsh,dh->bsd', h, wd)

    def _L1_xattn_ref(teacher_features, student_features):
        import jax, jax.numpy as jnp
        import numpy as np
        from jax import lax
        BIG = jnp.float32(1e+30)

        def _pairwise_euclidean(a, b):
            aa = jnp.sum(a * a, axis=-1)[:, None]
            bb = jnp.sum(b * b, axis=-1)[None, :]
            ab = a @ b.T
            return jnp.sqrt(jnp.maximum(aa + bb - 2.0 * ab, 0.0))

        def _dtw_cost(D):
            row0 = jnp.cumsum(D[0])

            def row_step(prev_row, d_row):
                first = d_row[0] + prev_row[0]

                def col_step(left, inp):
                    d_ij, up, diag = inp
                    r = d_ij + jnp.minimum(jnp.minimum(up, left), diag)
                    return (r, r)
                _, rest = lax.scan(col_step, first, (d_row[1:], prev_row[1:], prev_row[:-1]))
                row = jnp.concatenate([first[None], rest])
                return (row, row)
            _, rows = lax.scan(row_step, row0, D[1:])
            return jnp.concatenate([row0[None], rows], axis=0)

        def _backtrack(R, T1, T2):
            L = T1 + T2 - 1

            def step(carry, _):
                i, j, done = carry
                valid = jnp.logical_not(done)
                cd = jnp.where((i > 0) & (j > 0), R[jnp.maximum(i - 1, 0), jnp.maximum(j - 1, 0)], BIG)
                cu = jnp.where(i > 0, R[jnp.maximum(i - 1, 0), j], BIG)
                cl = jnp.where(j > 0, R[i, jnp.maximum(j - 1, 0)], BIG)
                choice = jnp.argmin(jnp.stack([cd, cu, cl]))
                ni = jnp.where(choice <= 1, i - 1, i)
                nj = jnp.where((choice == 0) | (choice == 2), j - 1, j)
                at_origin = (i == 0) & (j == 0)
                ni = jnp.where(at_origin, 0, ni)
                nj = jnp.where(at_origin, 0, nj)
                return ((ni, nj, done | at_origin), (i, j, valid))
            init = (jnp.int32(T1 - 1), jnp.int32(T2 - 1), jnp.bool_(False))
            _, (i_idx, j_idx, valid) = lax.scan(step, init, None, length=L)
            return (i_idx, j_idx, valid)

        def _align_one(small, large):
            T_small, d = small.shape
            T_large = large.shape[0]
            D = _pairwise_euclidean(small, large)
            R = _dtw_cost(D)
            i_idx, j_idx, valid = _backtrack(R, T_small, T_large)
            contrib = small[i_idx] * valid[:, None].astype(small.dtype)
            expanded = jnp.zeros((T_large, d), dtype=small.dtype).at[j_idx].add(contrib)
            return expanded
        return jax.vmap(_align_one)(teacher_features, student_features)

    def _L1_ffn_ref(hidden_states, gate_w, w1, w2, w3):
        import jax, jax.numpy as jnp
        import numpy as np
        B, S, H = (1, 128, 128)
        E, I = (8, 256)
        JITTER_EPS = 0.01

        def _sparse_mixer_top2(scores, jitter_eps):
            vals, idx = jax.lax.top_k(scores, 2)
            neg_inf = jnp.array(-jnp.inf, scores.dtype)
            t1 = vals[:, :1]
            f1 = jnp.maximum(jnp.abs(scores), t1)
            m1 = (t1 - scores) / f1 > 2 * jitter_eps
            p1 = jax.nn.softmax(jnp.where(m1, neg_inf, scores), axis=-1)
            mult1 = jnp.take_along_axis(p1, idx[:, :1], axis=-1)
            t2 = vals[:, 1:2]
            f2 = jnp.maximum(jnp.abs(scores), t2)
            m2 = (t2 - scores) / f2 > 2 * jitter_eps
            rows = jnp.arange(scores.shape[0])[:, None]
            s2 = scores.at[rows, idx[:, :1]].set(neg_inf)
            p2 = jax.nn.softmax(jnp.where(m2, neg_inf, s2), axis=-1)
            mult2 = jnp.take_along_axis(p2, idx[:, 1:2], axis=-1)
            return (jnp.concatenate([mult1, mult2], axis=-1), idx)
        b, s, h = hidden_states.shape
        x = hidden_states.reshape(-1, h)
        T = x.shape[0]
        logits = x @ gate_w.T
        mult, sel = _sparse_mixer_top2(logits, JITTER_EPS)
        rows = jnp.arange(T)[:, None]
        dense_w = jnp.zeros((T, E), x.dtype).at[rows, sel].set(mult)
        h1 = jnp.einsum('th,eih->eti', x, w1)
        h3 = jnp.einsum('th,eih->eti', x, w3)
        act = jax.nn.silu(h1) * h3
        y = jnp.einsum('eti,ehi->eth', act, w2)
        out = jnp.einsum('eth,te->th', y, dense_w)
        return out.reshape(b, s, h)
    x = x + _L0_xattn_ref(_layernorm(x, axis=-1), ctx_1024, ctx_1024, mask_BxS2_ik0, L0_xattn_Wq, L0_xattn_bq, L0_xattn_Wk, L0_xattn_bk, L0_xattn_Wv, L0_xattn_bv, L0_xattn_Wo, L0_xattn_bo, L0_xattn_q_norm_w, L0_xattn_k_norm_w)
    x = x + _L0_ffn_ref(_layernorm(x, axis=-1), L0_ffn_w_gate, L0_ffn_w_up, L0_ffn_w_down)
    x = x + _L1_xattn_ref(ctx_1024, _layernorm(x, axis=-1))
    x = x + _L1_ffn_ref(_layernorm(x, axis=-1), L1_ffn_gate_w, L1_ffn_w1, L1_ffn_w2, L1_ffn_w3)
    return x

_drawn_inputs = setup_inputs


def setup_inputs(seed=0):
    import zlib

    import numpy as np

    out = dict(_drawn_inputs(seed))
    spreads = {'L0_xattn_bq': (0.0, 0.774),
     'L0_xattn_bk': (0.0, 0.8),
     'L0_xattn_bv': (0.0, 0.1),
     'L0_xattn_bo': (0.0, 0.1),
     'L0_xattn_q_norm_w': (1.0, 0.6),
     'L0_xattn_k_norm_w': (1.0, 0.6)}
    factors = {'L0_xattn_Wq': 3.027,
     'L0_xattn_Wk': 2.754,
     'L1_ffn_gate_w': 8.0,
     'L1_ffn_w1': 8.0,
     'L1_ffn_w2': 8.0,
     'L1_ffn_w3': 8.0}
    for name, (base, spread) in spreads.items():
        noise = np.random.default_rng([zlib.crc32(name.encode()), seed]).standard_normal(out[name].shape)
        drawn = base * np.exp(spread * noise) if base else spread * noise
        out[name] = jnp.asarray(drawn.astype(out[name].dtype))
    for name, factor in factors.items():
        out[name] = (out[name] * factor).astype(out[name].dtype)
    return out
```

```python
from contextlib import ExitStack

import concourse.bass as bass
from concourse import mybir

F32 = mybir.dt.float32
F16 = mybir.dt.float16
BF16 = mybir.dt.bfloat16
I32 = mybir.dt.int32
U32 = mybir.dt.uint32
ALU = mybir.AluOpType
ACT = mybir.ActivationFunctionType
AX = mybir.AxisListType.X

P = 128
BIG = 1.0e30
STAGE = "all"


class Steps:

    def __init__(self, eng, sem):
        self.eng, self.sem, self.n = eng, sem, 0

    def link(self, ins):
        ins.then_inc(self.sem, 1)
        self.n += 1
        self.eng.wait_ge(self.sem, self.n)

    def restart(self):
        self.eng.sem_clear(self.sem)
        self.n = 0


def peeled(eng, stop, body, count=None):
    body(0)
    with eng.Fori(1, stop - 1) as i:
        if count:
            count.restart()
        body(i)
    body(stop - 1)


def wait(eng, semaphore, value):
    if not isinstance(value, int) or value > 0:
        eng.wait_ge(semaphore, value)


def build(nc, x, ctx_dt, ctx_kd, mask, wqT, bq, wkT, bk, wvT, bv, woT, bo, qw, kw,
          wgT, wuT, wdT, gateT, w13T, w2T, out):
    BT, SL, D = x.shape[0], x.shape[1], x.shape[2]
    Q = SL // P
    NT = BT * Q
    KL = ctx_dt.shape[1] // BT
    HD = qw.shape[0]
    NH = D // HD
    SCALE = float(HD) ** -0.5
    HID = wgT.shape[1]
    FC = HID // P
    DQ = 1.0 / 127.0
    NE = gateT.shape[1]
    EI = w2T.shape[0] // NE
    EC = EI // P
    HK = NH * KL
    NC = -(-HK // P)
    HB = [(0, 6), (6, 12), (12, 16)]
    H0 = [min(c * P // KL, NH - 3) for c in range(NC)]
    CR = [min(P, HK - c * P) for c in range(NC)]
    VW = HD + 1

    RW = 3
    NI = -(-KL // RW)
    CB = 64
    NB = SL // CB
    NS = NB + NI - 1
    W = NS * CB
    WN = 4
    NWIN = -(-NS // WN)
    KR = NI * RW
    WD = CB + W
    JB = P // BT
    CC = SL // JB
    LN_EPS, Q_EPS = 1e-5, 1e-6

    ds = nc.dram_tensor("cost_skewed", (P, RW, WD), F32, kind="Internal").ap()
    rs = nc.dram_tensor("sums_skewed", (P, RW, WD), F32, kind="Internal").ap()

    with ExitStack() as ctx:
        def sb(name, shape, dt=F32):
            return ctx.enter_context(nc.sbuf_tensor(name, shape, dt))

        def sem(name):
            return ctx.enter_context(nc.semaphore(name))

        X = sb("X", [P, NT, D])
        XN = sb("XN", [P, Q, D])
        XNT = sb("XNT", [P, Q * P])
        space1 = sb("space1", [P, NT * D])
        space2 = sb("space2", [P, NT * D])
        space3 = sb("space3", [P, NT * P])
        space4 = sb("space4", [P, RW * W])
        space5 = sb("space5", [P, 2 * HK])
        space6 = sb("space6", [P, NC * P])
        space7 = sb("space7", [P, 2 * FC * Q * P])
        space8 = sb("space8", [P, 2 * 3 * HID])

        def part(t, shape, at=0):
            n = 1
            for d in shape[1:]:
                n *= d
            v = t[0:shape[0], at:at + n]
            if len(shape) == 3:
                return v.rearrange("p (a b) -> p a b", a=shape[1])
            if len(shape) == 4:
                return v.rearrange("p (a b c) -> p a b c", a=shape[1], b=shape[2])
            return v

        Qs = part(space1, [P, NT * D])
        SQ = part(space2, [P, NT * D])
        QN = sb("QN", [P, Q, D])
        QT = part(space3, [P, NT, P])
        QTb = sb("QTb", [P, 2, P])
        qss = sb("qss", [P, NT * NH])
        qrs = sb("qrs", [P, NT * NH])
        KQ = sb("KQ", [KL, BT * D])
        CSQ = sb("CSQ", [KR, BT * D])
        KSQ = CSQ[0:KL, :]
        kss = sb("kss", [KL, BT * NH])
        krs = sb("krs", [KL, BT * NH])
        KT = sb("KT", [P, BT * KL])
        KB = part(space4, [P, BT, HK])
        VX = sb("VX", [P, BT, NC * 3, VW])
        CT3 = sb("CT3", [P, BT, 3 * KL])
        CK = sb("CK", [KR, BT, D])
        WQ, WK, WV, WO = (sb(n, [P, D]) for n in ("WQ", "WK", "WV", "WO"))
        BQ, BK, BO, BIASO = (sb(n, [P, D]) for n in ("BQ", "BK", "BO", "BIASO"))
        bvc = sb("bvc", [P, 1])
        BVT = sb("BVT", [P, P])
        qwb = sb("qwb", [P, HD])
        kwb = sb("kwb", [P, HD])
        qkw = sb("qkw", [P, HD])
        mi = sb("mi", [P, BT, KL], I32)
        mz = sb("mz", [P, BT, KL])
        mrow = sb("mrow", [1, BT, NH, KL], BF16)
        ones_b = sb("ones_b", [1, P], BF16)
        cnt = sb("cnt", [P, BT])
        nanf = sb("nanf", [P, BT])
        mx = sb("mx", [P, NH])
        PR = part(space5, [P, 2, HK])
        PT = part(space6, [P, NC, P])
        rcp = sb("rcp", [P, NH])
        ON = sb("ON", [P, D])
        OT = sb("OT", [P, P])
        bst = sb("bst", [P, Q, 6])
        mv = sb("mv", [P, NT, 2])
        XS = sb("XS", [P, Q, D])
        mvs = sb("mvs", [P, Q, 2])
        std = sb("std", [P, NT])
        rstd = sb("rstd", [P, NT])
        epsl = sb("epsl", [P, 1])
        epsq = sb("epsq", [P, 1])
        wi = space8[:, 0:3 * HID].bitcast(I32)
        WG = part(space8, [P, HID], 3 * HID)
        WU = part(space8, [P, HID], 4 * HID)
        WD2 = part(space8, [P, FC, D], 5 * HID)
        HS = part(space7, [P, FC, Q * P])
        HT = part(space7, [P, FC, Q * P], FC * Q * P)
        ident = sb("ident", [P, P])
        HM = sb("HM", [P, NH])
        HMC = sb("HMC", [P, NC * 3])
        ones_f = sb("ones_f", [P, P])
        CN2 = sb("CN2", [P, BT, KR])
        aa = sb("aa", [KR, BT])
        XSQ = sb("XSQ", [P, Q * P])
        DSQ = part(space2, [KR, BT, SL])
        DSB = part(space1, [KR, BT, SL])
        DP = part(space4, [P, RW, W])
        WS = sb("WS", [P, 2, RW + 1, 1 + WN * CB])
        bigs = sb("bigs", [P, WD // 2])
        MM = sb("MM", [P, RW, CB])
        RI = part(space8, [KR, BT, SL + 1])
        UI = part(space5, [KR + 1, BT, SL + 1])
        T1 = part(space1, [KR, BT, SL])
        T2 = part(space2, [KR, BT, SL])
        JG = part(space7, [KR, BT, SL])
        FX = part(space3, [KR, BT * SL])
        FT = part(space6, [P, KR, CC])
        JH = sb("JH", [P, CC, 2])
        goff = sb("goff", [P, 1])
        blk1 = sb("blk1", [P, P], F16)
        hit = sb("hit", [P, CC, 2])
        hs = sb("hs", [P, 2], F16)
        last = sb("last", [P, 1])
        BS = sb("BS", [P, KR])
        lohi = sb("lohi", [KR, 2, BT])
        PA = sb("PA", [KR, SL])
        PM = sb("PM", [KR, SL])
        GW = sb("GW", [P, NE])
        XT4 = part(space3, [P, NT, P])
        LG = sb("LG", [P, NT, NE])
        M8 = sb("M8", [P, NT, 8])
        I8 = sb("I8", [P, NT, 8], U32)
        IF8 = sb("IF8", [P, NT, 2])
        JE = sb("JE", [P, NT, NE])
        OH = sb("OH", [P, 2, NT, NE])
        RA = sb("RA", [P, NT, NE])
        RB = sb("RB", [P, NT, NE])
        RC = sb("RC", [P, 2, NT, NE])
        ZS = sb("ZS", [P, 2, NT])
        GWT = sb("GWT", [P, NT, NE])
        W13 = sb("W13", [P, NE, 2 * EI])
        W2 = sb("W2", [P, NE, EC, D])
        XTb = sb("XTb", [P, 2, P])
        SI = sb("SI", [P, 2, EI])
        AC = sb("AC", [P, 2, EI])
        AT = sb("AT", [P, 2, EC, P])
        PS = ctx.enter_context(nc.psum_tensor("PS", [P, 8, 512], F32))

        ld_x = sem("ld_x")
        ld_ctx = sem("ld_ctx")
        ld_small = sem("ld_small")
        ld_ffn = sem("ld_ffn")
        ld_moe = sem("ld_moe")
        c_ident = sem("c_ident")
        c_step = sem("c_step")
        c_heads = sem("c_heads")
        c_all = sem("c_all")
        v_step = sem("v_step")
        k_ps = sem("k_ps")
        v_ps = sem("v_ps")
        kss_ok = sem("kss_ok")
        kst_ok = sem("kst_ok")
        kn_ok = sem("kn_ok")
        kT_ps = sem("kT_ps")
        kT_sb = sem("kT_sb")
        kb_ok = sem("kb_ok")
        vx_ok = sem("vx_ok")
        bvt_ok = sem("bvt_ok")
        bo_ps = sem("bo_ps")
        bo_ok = sem("bo_ok")
        var_ok = sem("var_ok")
        std_ok = sem("std_ok")
        xn_ok = sem("xn_ok")
        xT_ps = sem("xT_ps")
        xT_sb = sem("xT_sb")
        q_ps = sem("q_ps")
        q_sb = sem("q_sb")
        qss_ok = sem("qss_ok")
        qst_ok = sem("qst_ok")
        qn_ok = sem("qn_ok")
        qT_ps = sem("qT_ps")
        qT_sb = sem("qT_sb")
        qTb_ok = sem("qTb_ok")
        sc_ps = sem("sc_ps")
        sc_sub = sem("sc_sub")
        exp_ok = sem("exp_ok")
        pT_ps = sem("pT_ps")
        pT_sb = sem("pT_sb")
        pv_ps = sem("pv_ps")
        on_ok = sem("on_ok")
        oT_ps = sem("oT_ps")
        oT_sb = sem("oT_sb")
        wo_ps = sem("wo_ps")
        x1_ok = sem("x1_ok")
        wf_ok = sem("wf_ok")
        g_ps = sem("g_ps")
        u_ps = sem("u_ps")
        silu_ok = sem("silu_ok")
        h_ok = sem("h_ok")
        dn_ps = sem("dn_ps")
        x2_ok = sem("x2_ok")
        xsq_ok = sem("xsq_ok")
        d_ps = sem("d_ps")
        d_pos = sem("d_pos")
        d_ok = sem("d_ok")
        cn_ok = sem("cn_ok")
        bo_add = sem("bo_add")
        r1_ok = sem("r1_ok")
        xt4_ok = sem("xt4_ok")
        big_ok = sem("big_ok")
        dpre = sem("dpre")
        dst = sem("dst")
        dld = sem("dld")
        r_ok = sem("r_ok")
        xs_ok = sem("xs_ok")
        mvs_ok = sem("mvs_ok")
        ui_ok = sem("ui_ok")
        rpre = sem("rpre")
        rst = sem("rst")
        rld = sem("rld")
        f_ok = sem("f_ok")
        fT_ps = sem("fT_ps")
        hit_ok = sem("hit_ok")
        b_ps = sem("b_ps")
        bs_ok = sem("bs_ok")
        bT_ps = sem("bT_ps")
        pm_ok = sem("pm_ok")
        e_ps = sem("e_ps")
        x3_ok = sem("x3_ok")
        lg_ps = sem("lg_ps")
        lg_ok = sem("lg_ok")
        rsub_ok = sem("rsub_ok")
        rexp_ok = sem("rexp_ok")
        gate_ok = sem("gate_ok")
        xTb_ok = sem("xTb_ok")
        m1_ps = sem("m1_ps")
        si_ok = sem("si_ok")
        ac_ok = sem("ac_ok")
        aT_ps = sem("aT_ps")
        aT_sb = sem("aT_sb")
        y_ps = sem("y_ps")
        y_ok = sem("y_ok")
        st_out = sem("st_out")

        def bc(ap, shape):
            return ap.to_broadcast(shape)

        def steps3(t):
            return t.rearrange("p (h d) -> p h d", d=HD)

        block = ctx.enter_context(nc.Block())

        x_v = x.rearrange("b (q p) d -> b p q d", p=P)
        out_v = out.rearrange("b (q p) d -> b p q d", p=P)
        XV = X[:, :, :].rearrange("p (b q) d -> p b q d", b=BT)

        def skewed(t, b, shift, row, cols):
            ps = RW * WD
            return bass.AP(t.tensor, b * (P // BT) * ps + row * WD + CB + shift,
                           [[ps + CB, NI], [WD, RW], [1, cols]])

        N_CTX = 12

        @block.sync
        def _(sp):
            sp.dma_start(X[:, 0:Q, :], x_v[0]).then_inc(ld_x, 16)
            for t, v in ((WK, wkT), (WV, wvT), (WQ, wqT)):
                sp.dma_start(t[:, :], v).then_inc(ld_small, 16)
            for b in range(1, BT):
                sp.dma_start(X[:, b * Q:(b + 1) * Q, :], x_v[b]).then_inc(ld_x, 16)
            sp.dma_start(WO[:, :], woT).then_inc(ld_small, 16)
            sp.dma_start(wi[:, 0:HID], wgT).then_inc(ld_ffn, 16)
            sp.dma_start(wi[:, HID:2 * HID], wuT).then_inc(ld_ffn, 16)
            sp.dma_start(wi[:, 2 * HID:3 * HID].rearrange("p (c d) -> p c d", c=FC),
                         wdT.rearrange("(c p) d -> p c d", p=P)).then_inc(ld_ffn, 16)
            sp.wait_ge(big_ok, 1)
            for r in range(RW):
                for h in range(2):
                    sp.dma_start(ds[:, r, h * WD // 2:(h + 1) * WD // 2], bigs[:, :]).then_inc(dpre, 16)
                    sp.dma_start(rs[:, r, h * WD // 2:(h + 1) * WD // 2], bigs[:, :]).then_inc(rpre, 16)
            sp.dma_start(GW[:, :], gateT).then_inc(ld_moe, 16)
            sp.dma_start(W13[:, :, :].rearrange("p e n -> p (e n)"), w13T).then_inc(ld_moe, 16)
            sp.dma_start(W2[:, :, :, :].rearrange("p e c d -> p (e c) d"),
                         w2T.rearrange("(c p) d -> p c d", p=P)).then_inc(ld_moe, 16)
            sp.wait_ge(dpre, 16 * 2 * RW)
            for b in range(BT):
                sp.wait_ge(d_ok, b + 1)
                sp.dma_start(skewed(ds, b, 0, 0, SL), DSB[:, b, :]).then_inc(dst, 16)
            sp.wait_ge(dst, 16 * BT)
            for w in range(NWIN):
                a, z = w * WN * CB, min((w + 1) * WN, NS) * CB
                wait(sp, dld, 16 * w)
                sp.dma_start(DP[:, :, a:z], ds[:, :, CB + a:CB + z]).then_inc(dld, 16)
            sp.wait_ge(rpre, 16 * 2 * RW)
            for w in range(NWIN):
                a, z = w * WN * CB, min((w + 1) * WN, NS) * CB
                sp.wait_ge(r_ok, w + 1)
                wait(sp, rst, 16 * w)
                sp.dma_start(rs[:, :, CB + a:CB + z], WS[:, w % 2, 1:RW + 1, 1:1 + z - a]).then_inc(rst, 16)
            sp.wait_ge(rst, 16 * NWIN)
            sp.wait_ge(ui_ok, 1)
            for b in range(BT):
                sp.dma_start(RI[:, b, :], skewed(rs, b, -1, 0, SL + 1)).then_inc(rld, 16)
                sp.dma_start(UI[1:KR + 1, b, :], skewed(rs, b, -1, 0, SL + 1)).then_inc(rld, 16)
            for b in range(BT):
                sp.wait_ge(y_ok, NE * Q * (b + 1))
                sp.dma_start(out_v[b], X[:, b * Q:(b + 1) * Q, :]).then_inc(st_out, 16)
            sp.wait_ge(st_out, 16 * BT)

        @block.gpsimd
        def _(pool):
            step = Steps(pool, c_step)
            step.link(nc.gpsimd.memset(ident[:, :], 0.0))
            nc.gpsimd.affine_select(out=ident[:, :], in_=ident[:, :], compare_op=ALU.not_equal, fill=1.0, base=0,
                                    pattern=[[-1, P]], channel_multiplier=1).then_inc(c_ident, 1)
            step.link(nc.gpsimd.memset(HM[:, :], 1.0))
            step.link(nc.gpsimd.affine_select(out=HM[:, :], in_=HM[:, :], compare_op=ALU.is_ge, fill=0.0, base=0,
                                              pattern=[[-HD, NH]], channel_multiplier=1))
            step.link(nc.gpsimd.affine_select(out=HM[:, :], in_=HM[:, :], compare_op=ALU.is_ge, fill=0.0, base=HD - 1,
                                              pattern=[[HD, NH]], channel_multiplier=-1))
            step.link(nc.gpsimd.memset(HMC[:, :], 1.0))
            for c in range(NC):
                part = HMC[:, 3 * c:3 * c + 3]
                step.link(nc.gpsimd.affine_select(out=part, in_=part, compare_op=ALU.is_ge, fill=0.0,
                                                  base=P * c - KL * H0[c], pattern=[[-KL, 3]], channel_multiplier=1))
                step.link(nc.gpsimd.affine_select(out=part, in_=part, compare_op=ALU.is_ge, fill=0.0,
                                                  base=KL * (H0[c] + 1) - 1 - P * c, pattern=[[KL, 3]],
                                                  channel_multiplier=-1))
            for b in range(BT):
                ins = nc.gpsimd.tensor_copy(VX[:, b, :, HD], HMC[:, :])
            ins.then_inc(c_heads, 1)
            step.link(nc.gpsimd.memset(ones_f[:, :], 1.0))
            pool.wait_ge(ld_ctx, 16 * N_CTX)
            nc.gpsimd.tensor_scalar(CN2[:, :, :], CT3[:, :, 0:KR], -2.0, None, ALU.mult).then_inc(cn_ok, 1)
            nc.gpsimd.tensor_scalar(BVT[:, :], ones_f[:, :], bvc[:, :], None, ALU.mult).then_inc(bvt_ok, 1)
            nc.gpsimd.memset(ones_b[:, :], 1.0)
            nc.gpsimd.memset(epsl[:, :], LN_EPS)
            nc.gpsimd.memset(epsq[:, :], Q_EPS).then_inc(c_all, 1)
            nc.gpsimd.memset(bigs[:, :], BIG).then_inc(big_ok, 1)
            step.link(nc.gpsimd.memset(WS[:, :, :, :], BIG))
            for b in range(BT):
                step.link(nc.gpsimd.memset(WS[b * 32:b * 32 + 1, 0, 0, 0:1], 0.0))
            step.link(nc.gpsimd.memset(last[:, :], float(SL - 1)))
            step.link(nc.gpsimd.iota(JE[:, :, :], pattern=[[0, NT], [1, NE]], base=0, channel_multiplier=0,
                                     allow_small_or_imprecise_dtypes=True))
            for g in range(BT):
                step.link(nc.gpsimd.iota(JH[g * JB:(g + 1) * JB, :, 0], pattern=[[1, CC]], base=0, channel_multiplier=CC,
                                         allow_small_or_imprecise_dtypes=True))
                step.link(nc.gpsimd.memset(goff[g * JB:(g + 1) * JB, :], float(SL * g)))
            step.link(nc.gpsimd.memset(blk1[:, :], 0.0))
            for g in range(BT):
                step.link(nc.gpsimd.memset(blk1[g * JB:(g + 1) * JB, g * JB:(g + 1) * JB], 1.0))
            step.link(nc.gpsimd.memset(hs[:, :], 0.0))
            nc.gpsimd.tensor_scalar(JH[:, :, 1], JH[:, :, 0], 0.5, None, ALU.add).then_inc(c_all, 1)
            pool.wait_ge(ld_ffn, 48)
            nc.gpsimd.tensor_copy(WG[:, :], wi[:, 0:HID])
            nc.gpsimd.tensor_copy(WU[:, :], wi[:, HID:2 * HID])
            nc.gpsimd.tensor_copy(WD2[:, :, :].rearrange("p c d -> p (c d)"), wi[:, 2 * HID:3 * HID]).then_inc(wf_ok, 1)
            pool.wait_ge(bo_ok, 1)
            with pool.Fori(0, BT) as b:
                pool.wait_ge(xn_ok, b + 1)
                nc.gpsimd.tensor_tensor(X[:, bass.ds(b * Q, Q), :], X[:, bass.ds(b * Q, Q), :],
                                        bc(BIASO[:, :].unsqueeze(1), [P, Q, D]), ALU.add).then_inc(bo_add, 1)

            def store(t0, n, src, msrc, done, count):
                pool.wait_ge(mvs_ok, count)
                nc.gpsimd.tensor_copy(X[:, t0 if n == 1 else bass.ds(t0, n), :], src)
                nc.gpsimd.tensor_copy(mv[:, t0 if n == 1 else bass.ds(t0, n), :], msrc).then_inc(done, 1)

            def queries(b):
                for q in range(Q):
                    t = b * Q + q
                    pool.wait_ge(qT_sb, b + 1)
                    wait(pool, sc_ps, 3 * (t - 1))
                    nc.gpsimd.tensor_copy(QTb[:, q % 2, :], QT[:, t, :]).then_inc(qTb_ok, 1)
                    if not (isinstance(t, int) and t < 3):
                        store(t - 3, 1, XS[:, (q - 3) % Q, :], mvs[:, (q - 3) % Q, :], x1_ok, t - 2)

            peeled(pool, BT, queries)
            for t in range(NT - 3, NT):
                store(t, 1, XS[:, t % Q, :], mvs[:, t % Q, :], x1_ok, t + 1)
            with pool.Fori(0, BT) as b:
                store(b * Q, Q, XS[:, :, :], mvs[:, :, :], x2_ok, b + (NT + 1))

            pool.wait_ge(pT_ps, 3 * NT)
            step.link(nc.gpsimd.memset(UI[0:1, :, :], BIG))
            nc.gpsimd.memset(UI[0:1, :, 0:1], 0.0).then_inc(ui_ok, 1)
            pool.wait_ge(dn_ps, BT)
            nc.gpsimd.iota(JG[:, :, :], pattern=[[SL, BT], [1, SL]], base=0, channel_multiplier=0,
                           allow_small_or_imprecise_dtypes=True).then_inc(ui_ok, 1)

            with pool.Fori(0, BT) as b:
                store(b * Q, Q, XS[:, :, :], mvs[:, :, :], x3_ok, b + (NT + BT + 1))
            with pool.Fori(0, BT) as b:
                pool.wait_ge(xT_sb, 3 * BT + b + 1)
                nc.gpsimd.tensor_copy(XT4[:, bass.ds(b * Q, Q), :],
                                      XNT[:, :].rearrange("p (q c) -> p q c", q=Q)).then_inc(xt4_ok, 1)

            def expert_inputs(u):
                for j in range(2):
                    t = 2 * u + j
                    wait(pool, m1_ps, NE * (t - 1))
                    nc.gpsimd.tensor_copy(XTb[:, j, :], XT4[:, t, :]).then_inc(xTb_ok, 1)

            pool.wait_ge(xt4_ok, BT)
            expert_inputs(0)
            with pool.Fori(1, NT // 2) as u:
                expert_inputs(u)

        @block.scalar
        def _(act):
            for j in range(3):
                act.dma_start(CT3[:, :, j * KL:(j + 1) * KL], ctx_dt.rearrange("d (b k) -> d b k", b=BT)).then_inc(ld_ctx, 16)
            act.dma_start(CK[0:KL, :, :], ctx_kd.rearrange("b k d -> k b d")).then_inc(ld_ctx, 16)
            act.dma_start(CK[KL:KR, :, :], ctx_kd[:, 0:KR - KL, :].rearrange("b k d -> k b d")).then_inc(ld_ctx, 16)
            for t, v in ((BK, bk), (BQ, bq), (BO, bo), (qwb, qw), (kwb, kw)):
                act.dma_start(t[:, :], v.rearrange("(a d) -> a d", a=1).partition_broadcast(P)).then_inc(ld_ctx, 16)
            act.dma_start(bvc[:, :], bv.rearrange("(d a) -> d a", a=1)).then_inc(ld_ctx, 16)
            act.dma_start(mi[:, :, :].rearrange("p b k -> p (b k)"),
                          mask.rearrange("(a b) k -> a (b k)", a=1).partition_broadcast(P)).then_inc(ld_ctx, 16)

            def copy(out, in_):
                return nc.scalar.activation(out, in_, ACT.Copy)

            act.wait_ge(c_all, 1)
            act.wait_ge(kss_ok, 1)
            nc.scalar.activation(krs[:, :], kss[:, :], ACT.Sqrt, bias=epsq[0:KL, :], scale=1.0 / HD).then_inc(kst_ok, 1)

            def std_of(semaphore, value):
                act.wait_ge(semaphore, value)
                nc.scalar.activation(std[:, :], mv[:, :, 1], ACT.Sqrt, bias=epsl[:, :]).then_inc(std_ok, 1)

            def copy_xT(r):
                act.wait_ge(xT_ps, r + 1)
                copy(XNT[:, :], PS[:, 0, :]).then_inc(xT_sb, 1)

            std_of(var_ok, 1)

            def queries(b):
                wait(act, q_ps, b)
                copy_xT(b)

            queries(0)
            with act.Fori(1, BT) as b:
                queries(b)
            act.wait_ge(kT_ps, 1)
            copy(KT[:, :], PS[:, 2, 0:BT * KL]).then_inc(kT_sb, 1)
            act.wait_ge(qss_ok, 1)
            nc.scalar.activation(qrs[:, :], qss[:, :], ACT.Sqrt, bias=epsq[:, :], scale=1.0 / HD).then_inc(qst_ok, 1)
            with act.Fori(0, BT) as b:
                act.wait_ge(qT_ps, b + 1)
                copy(QT[:, bass.ds(b * Q, Q), :].rearrange("p q c -> p (q c)"), PS[:, 1, :]).then_inc(qT_sb, 1)

            groups = [(0, 4), (4, 8), (8, NC)]

            def exps(t, par):
                act.wait_ge(sc_sub, 2 * t + 2)
                nc.scalar.activation(PR[:, par, :], PR[:, par, :], ACT.Exp).then_inc(exp_ok, 1)

            def weights_T(t, g):
                c0, c1 = groups[g]
                act.wait_ge(pT_ps, 3 * t + g + 1)
                if g == 0:
                    wait(act, pv_ps, t)
                rows = P if g < 2 else CR[NC - 1]
                copy(PT[:, c0:NC - 1 if g == 2 else c1, :],
                     PS[:, 6, 0:((NC - 1 if g == 2 else c1) - c0) * P].rearrange("p (c k) -> p c k", k=P)
                     ).then_inc(pT_sb, 1)
                if g == 2:
                    copy(PT[0:rows, NC - 1, :], PS[0:rows, 6, (NC - 1 - c0) * P:(NC - c0) * P]).then_inc(pT_sb, 1)

            def out_T(t):
                act.wait_ge(oT_ps, t + 1)
                copy(OT[:, :], PS[:, 7, 256:384]).then_inc(oT_sb, 1)

            exps(0, 0)

            def attend(b):
                for q in range(Q):
                    t = b * Q + q
                    first, final = isinstance(t, int) and t == 0, isinstance(t, int) and t == NT - 1
                    weights_T(t, 0)
                    if not first:
                        out_T(t - 1)
                    weights_T(t, 1)
                    weights_T(t, 2)
                    if not final:
                        exps(t + 1, (q + 1) % 2)

            peeled(act, BT, attend)
            out_T(NT - 1)

            std_of(x1_ok, NT)
            act.wait_ge(xT_ps, BT + 1)
            copy_xT(BT)

            def ffn(b):
                for c in range(FC):
                    act.wait_ge(g_ps, FC * b + c + 1)
                    wait(act, h_ok, FC * (b - 1) + c + 1)
                    nc.scalar.activation(HS[:, c, :], PS[:, 1 + 2 * c, :], ACT.Silu, scale=DQ).then_inc(silu_ok, 1)
                if not (isinstance(b, int) and b == BT - 1):
                    act.wait_ge(u_ps, FC * (b + 1))
                    copy_xT(BT + b + 1)

            peeled(act, BT, ffn)

            std_of(x2_ok, BT)

            def squares(b):
                wait(act, d_ps, b)
                copy_xT(2 * BT + b)
                nc.scalar.activation(XSQ[:, :], PS[:, 0, :], ACT.Square).then_inc(xsq_ok, 1)

            def roots(b):
                act.wait_ge(d_pos, b + 1)
                nc.scalar.activation(DSB[:, b, :], DSQ[:, b, :], ACT.Sqrt).then_inc(d_ok, 1)

            squares(0)
            with act.Fori(0, BT - 1) as b:
                squares(b + 1)
                roots(b)
            roots(BT - 1)

            std_of(x3_ok, BT)

            def router(b):
                wait(act, lg_ps, b)
                wait(act, xt4_ok, b)
                copy_xT(3 * BT + b)

            router(0)
            with act.Fori(1, BT) as b:
                router(b)
            act.wait_ge(rsub_ok, 1)
            nc.scalar.activation(RC[:, :, :, :], RC[:, :, :, :], ACT.Exp).then_inc(rexp_ok, 1)

            def acts_T(n, par):
                act.wait_ge(aT_ps, n + 1)
                wait(act, y_ps, n - 1)
                copy(AT[:, par, :, :].rearrange("p c k -> p (c k)"), PS[:, 2 + par, 0:EI]).then_inc(aT_sb, 1)

            def experts(u):
                for k in range(2 * NE):
                    n = 2 * NE * u + k
                    act.wait_ge(m1_ps, n + 1)
                    wait(act, ac_ok, n - 1)
                    nc.scalar.activation(SI[:, k % 2, :], PS[:, k % 2, 0:EI], ACT.Silu).then_inc(si_ok, 1)
                    if not (isinstance(n, int) and n == 0):
                        acts_T(n - 1, (k - 1) % 2)

            experts(0)
            with act.Fori(1, NT // 2) as u:
                experts(u)
            acts_T(NT * NE - 1, 1)

        @block.vector
        def _(dve):
            step = Steps(dve, v_step)
            V = nc.vector

            def stats(src, dst):
                for q in range(Q):
                    ins = V.bn_stats(bst[:, q, :], src[:, q, :])
                step.link(ins)
                for q in range(Q):
                    ins = V.bn_aggr(dst[:, q, :], bst[:, q, :])
                return ins

            def rstd_of(run):
                dve.wait_ge(std_ok, run)
                step.link(V.reciprocal(rstd[:, :], std[:, :]))

            def normalise(r, b):
                wait(dve, xT_ps, r)
                for q in range(Q):
                    t = b * Q + q
                    ins = V.tensor_scalar(XN[:, q, :], X[:, t, :], mv[:, t, 0:1], rstd[:, t:t + 1] if isinstance(t, int)
                                          else rstd[:, bass.ds(t, 1)], ALU.subtract, ALU.mult)
                ins.then_inc(xn_ok, 1)

            dve.wait_ge(ld_ctx, 16 * N_CTX)
            dve.wait_ge(k_ps, 1)
            step.link(V.tensor_tensor(KQ[:, :].rearrange("k (b d) -> k b d", b=BT),
                                      PS[0:KL, 2, :].rearrange("k (b d) -> k b d", b=BT),
                                      bc(BK[0:KL, :].unsqueeze(1), [KL, BT, D]), ALU.add))
            step.link(V.tensor_tensor(KSQ[:, :], KQ[:, :], KQ[:, :], ALU.mult))
            V.tensor_reduce(kss[:, :], steps3(KSQ[:, :]), AX, ALU.add).then_inc(kss_ok, 1)
            dve.wait_ge(c_heads, 1)
            for b in range(BT):
                dve.wait_ge(v_ps, b + 1)
                ins = V.tensor_tensor(VX[:, b, :, 0:HD], PS[:, 4 + b, 0:NC * 3 * HD].rearrange("p (m d) -> p m d", d=HD),
                                      bc(HMC[:, :].unsqueeze(2), [P, NC * 3, HD]), ALU.mult)
            ins.then_inc(vx_ok, 1)
            dve.wait_ge(bo_ps, 1)
            V.tensor_tensor(BIASO[:, :], PS[:, 3, 0:D], BO[:, :], ALU.add).then_inc(bo_ok, 1)
            step.link(V.tensor_single_scalar(mz[:, :, :], mi[:, :, :], 0.0, ALU.is_equal))
            step.link(V.tensor_scalar(mrow[0:1, :, :, :], bc(mz[0:1, :, :].unsqueeze(2), [1, BT, NH, KL]), -BIG, None, ALU.mult))
            step.link(V.tensor_scalar(mz[:, :, :], mz[:, :, :], -1.0, 1.0, ALU.mult, ALU.add))
            step.link(V.tensor_reduce(cnt[:, :], mz[:, :, :], AX, ALU.add))
            step.link(V.reciprocal(nanf[:, :], cnt[:, :]))
            step.link(V.tensor_scalar(nanf[:, :], nanf[:, :], 0.0, None, ALU.mult))
            step.link(V.tensor_scalar(qkw[:, :], kwb[:, :], SCALE, None, ALU.mult))
            step.link(V.tensor_tensor(qkw[:, :], qkw[:, :], qwb[:, :], ALU.mult))
            dve.wait_ge(kst_ok, 1)
            step.link(V.reciprocal(krs[:, :], krs[:, :]))
            step.link(V.tensor_tensor(steps3(KQ[:, :]), steps3(KQ[:, :]), bc(krs[:, :].unsqueeze(2), [KL, BT * NH, HD]), ALU.mult))
            V.tensor_tensor(steps3(KQ[:, :]), steps3(KQ[:, :]), bc(qkw[0:KL, :].unsqueeze(1), [KL, BT * NH, HD]),
                            ALU.mult).then_inc(kn_ok, 1)
            step.link(V.tensor_tensor(CSQ[:, :], CK[:, :, :].rearrange("k b d -> k (b d)"), CK[:, :, :].rearrange("k b d -> k (b d)"), ALU.mult))
            step.link(V.tensor_reduce(aa[:, :], CSQ[:, :].rearrange("k (b d) -> k b d", b=BT), AX, ALU.add))

            dve.wait_ge(ld_x, 16 * BT)
            for b in range(BT):
                ins = stats(X[:, b * Q:(b + 1) * Q, :], mv[:, b * Q:(b + 1) * Q, :])
                if b < BT - 1:
                    step.link(ins)
            ins.then_inc(var_ok, 1)
            rstd_of(1)
            normalise(0, 0)

            def project(b):
                dve.wait_ge(q_ps, b + 1)
                V.tensor_tensor(Qs[:, bass.ds(b * Q * D, Q * D)].rearrange("p (q d) -> p q d", q=Q),
                                PS[:, 1, :].rearrange("p (q d) -> p q d", q=Q),
                                bc(BQ[:, :].unsqueeze(1), [P, Q, D]), ALU.add).then_inc(q_sb, 1)

            with dve.Fori(0, BT - 1) as b:
                normalise(b + 1, b + 1)
                project(b)
            project(BT - 1)
            dve.wait_ge(q_sb, BT)
            step.link(V.tensor_tensor(SQ[:, :], Qs[:, :], Qs[:, :], ALU.mult))
            V.tensor_reduce(qss[:, :], steps3(SQ[:, :]), AX, ALU.add).then_inc(qss_ok, 1)
            dve.wait_ge(kT_sb, 1)
            KBv = KB[:, :, :].rearrange("p b (h k) -> p b h k", h=NH)
            for h in range(NH):
                ins = V.tensor_scalar(KBv[:, :, h, :], KT[:, :].rearrange("p (b k) -> p b k", b=BT), HM[:, h:h + 1], None, ALU.mult)
            ins.then_inc(kb_ok, 1)
            dve.wait_ge(qst_ok, 1)
            step.link(V.reciprocal(qrs[:, :], qrs[:, :]))

            def scale_q(b):
                wait(dve, qT_ps, b)
                V.tensor_tensor(QN[:, :, :].rearrange("p q (h d) -> p (q h) d", d=HD),
                                steps3(Qs[:, bass.ds(b * Q * D, Q * D)]),
                                bc(qrs[:, bass.ds(b * Q * NH, Q * NH)].unsqueeze(2), [P, Q * NH, HD]), ALU.mult).then_inc(qn_ok, 1)

            scale_q(0)
            with dve.Fori(1, BT) as b:
                scale_q(b)

            def heads(t, par, h0, h1, bank, nb):
                n = (h1 - h0) // nb
                src = PS[:, 3 * par + bank:3 * par + bank + nb, 0:n * KL].rearrange("p a (h k) -> p a h k", k=KL)
                top = mx[:, h0:h1].rearrange("p (a h) -> p a h", a=nb)
                step.link(V.tensor_reduce(top, src, AX, ALU.max))
                V.tensor_tensor(PR[:, par, h0 * KL:h1 * KL].rearrange("p (a h k) -> p a h k", a=nb, k=KL), src,
                                bc(top.unsqueeze(3), [P, nb, n, KL]), ALU.subtract).then_inc(sc_sub, 1)

            def centre(t, par, part):
                dve.wait_ge(sc_ps, 3 * t + 2 + part)
                if part == 0:
                    wait(dve, pT_ps, 3 * (t - 1))
                    heads(t, par, 0, 12, 0, 2)
                else:
                    heads(t, par, 12, 16, 2, 1)

            def residual(t, b, q):
                dve.wait_ge(wo_ps, t + 1)
                wait(dve, x1_ok, t - Q + 1)
                V.scalar_tensor_tensor(XS[:, q, :], PS[:, 7, 384:512], nanf[:, b:b + 1] if isinstance(b, int) else nanf[:, bass.ds(b, 1)],
                                       X[:, t, :], ALU.add, ALU.add).then_inc(xs_ok, 1)
                dve.wait_ge(xs_ok, t + 1)
                step.link(V.bn_stats(bst[:, 0, :], XS[:, q, :]))
                V.bn_aggr(mvs[:, q, :], bst[:, 0, :]).then_inc(mvs_ok, 1)

            dve.wait_ge(bo_add, BT)
            centre(0, 0, 0)
            centre(0, 0, 1)

            def attend(b):
                for q in range(Q):
                    t = b * Q + q
                    first, final = isinstance(t, int) and t == 0, isinstance(t, int) and t == NT - 1
                    if not final:
                        centre(t + 1, (q + 1) % 2, 0)
                    if not first:
                        residual(t - 1, b if q else b - 1, (q - 1) % Q)
                    if not final:
                        centre(t + 1, (q + 1) % 2, 1)
                    dve.wait_ge(pv_ps, t + 1)
                    O = PS[:, 7, 0:NH * VW].rearrange("p (h w) -> p h w", w=VW)
                    step.link(V.reciprocal(rcp[:, :], O[:, :, HD]))
                    V.tensor_tensor(ON[:, :].rearrange("p (h d) -> p h d", d=HD), O[:, :, 0:HD],
                                    bc(rcp[:, :].unsqueeze(2), [P, NH, HD]), ALU.mult).then_inc(on_ok, 1)

            peeled(dve, BT, attend, step)
            residual(NT - 1, BT - 1, Q - 1)

            rstd_of(2)
            normalise(BT, 0)
            dve.wait_ge(wf_ok, 1)
            dve.wait_ge(x1_ok, NT)

            def ffn(b):
                if not (isinstance(b, int) and b == BT - 1):
                    normalise(BT + b + 1, b + 1)
                for c in range(FC):
                    dve.wait_ge(u_ps, FC * b + c + 1)
                    dve.wait_ge(silu_ok, FC * b + c + 1)
                    wait(dve, dn_ps, b)
                    V.scalar_tensor_tensor(HT[:, c, :], PS[:, 2 + 2 * c, :], DQ, HS[:, c, :], ALU.mult, ALU.mult).then_inc(h_ok, 1)
                dve.wait_ge(dn_ps, b + 1)
                wait(dve, x2_ok, b)
                V.scalar_tensor_tensor(XS[:, :, :].rearrange("p q d -> p (q d)"), PS[:, 7, :], DQ,
                                       X[:, bass.ds(b * Q, Q), :].rearrange("p q d -> p (q d)"), ALU.mult, ALU.add).then_inc(xs_ok, 1)
                dve.wait_ge(xs_ok, NT + b + 1)
                stats(XS, mvs).then_inc(mvs_ok, 1)

            peeled(dve, BT, ffn, step)

            rstd_of(3)
            normalise(2 * BT, 0)

            def clamp(b):
                dve.wait_ge(d_ps, b + 1)
                V.tensor_scalar(DSQ[:, b, :], PS[0:KR, 1 + b, :], aa[:, b:b + 1] if isinstance(b, int) else aa[:, bass.ds(b, 1)],
                                0.0, ALU.add, ALU.max).then_inc(d_pos, 1)

            with dve.Fori(0, BT - 1) as b:
                normalise(2 * BT + b + 1, b + 1)
                clamp(b)
            clamp(BT - 1)

            cost = DP[:, :, :].rearrange("p r (s c) -> p r s c", c=CB)
            down = [31] + list(range(31))

            def wave(s, k, par, go_on=True):
                at = k * CB
                for r in range(RW):
                    step.link(V.tensor_tensor(MM[:, r, :], WS[:, par, r, at:at + CB], WS[:, par, r, at + 1:at + 1 + CB], ALU.min))
                    ins = V.tensor_tensor_scan(WS[:, par, r + 1, at + 1:at + 1 + CB], MM[:, r, :], cost[:, r, s, :],
                                               WS[:, par, r + 1, at:at + 1], ALU.min, ALU.add)
                    if go_on or r < RW - 1:
                        step.link(ins)
                if not go_on:
                    ins.then_inc(r_ok, 1)
                    return
                if k == WN - 1:
                    V.tensor_copy(WS[:, 1 - par, :, 0:1], WS[:, par, :, at + CB:at + CB + 1]).then_inc(r_ok, 1)
                    step.link(V.stream_shuffle(WS[:, 1 - par, 0, 1:1 + CB], WS[:, par, RW, at + 1:at + 1 + CB], down))
                else:
                    step.link(V.stream_shuffle(WS[:, par, 0, at + CB + 1:at + 2 * CB + 1], WS[:, par, RW, at + 1:at + 1 + CB], down))

            def two_windows(v):
                for par in range(2):
                    w = v * 2 + par
                    dve.wait_ge(dld, w * 16 + 16)
                    wait(dve, rst, (w - 1) * 16)
                    for k in range(WN):
                        wave(w * WN + k, k, par)

            pairs = NS // (2 * WN)
            two_windows(0)
            with dve.Fori(1, pairs) as v:
                step.restart()
                two_windows(v)
            dve.wait_ge(dld, 16 * NWIN)
            dve.wait_ge(rst, 16 * (NWIN - 2))
            assert NS - 2 * WN * pairs == 1
            wave(NS - 1, 0, 0, False)

            dve.wait_ge(rld, 16 * 2 * BT)
            dve.wait_ge(ui_ok, 2)
            dg, up, lf = UI[0:KR, :, 0:SL], UI[0:KR, :, 1:SL + 1], RI[:, :, 0:SL]
            step.link(V.tensor_tensor(T1[:, :, :], dg, up, ALU.min))
            step.link(V.tensor_tensor(T2[:, :, :], lf, T1[:, :, :], ALU.is_ge))
            step.link(V.tensor_tensor(T1[:, :, :], dg, up, ALU.is_le))
            step.link(V.scalar_tensor_tensor(T1[:, :, :], T1[:, :, :], -0.5, JG[:, :, :], ALU.mult, ALU.add))
            step.link(V.tensor_tensor(T1[:, :, :], T1[:, :, :], T2[:, :, :], ALU.mult))
            v2 = T1[:, :, :].rearrange("k b j -> k (b j)")
            V.tensor_tensor_scan(FX[:, :], v2, v2, -1.0, ALU.max, ALU.max).then_inc(f_ok, 1)
            per = 6
            for g in range(3):
                c0, n = g * per, min(per, CC - g * per)
                dve.wait_ge(fT_ps, g + 1)
                ins = V.tensor_scalar(FT[:, :, c0:c0 + n].rearrange("p k c -> p c k"),
                                      PS[:, g, 0:n * 85].rearrange("p (c k) -> p c k", k=85)[:, :, 0:KR],
                                      goff[:, :], None, ALU.subtract)
            step.link(ins)

            def look(i, came, par):
                V.scalar_tensor_tensor(hit[:, :, :], JH[:, :, :], came, bc(FT[:, i, :].unsqueeze(2), [P, CC, 2]),
                                       ALU.is_equal, ALU.mult, accum_out=hs[:, par:par + 1]).then_inc(hit_ok, 1)

            with nc.allow_low_precision(reason="columns are multiples of one half below 1024, exact in float16"):
                look(KL - 1, last[:, :], 0)
                with dve.Fori(0, (KL - 1) // 4) as w:
                    for k in range(4):
                        i = w * (-4) + (KL - 2 - k)
                        dve.wait_ge(b_ps, w * 4 + k + 1)
                        look(i, PS[:, 5, bass.ds(i + 1, 1)], (k + 1) % 2)
            dve.wait_ge(b_ps, KL)
            V.memset(BS[:, KL:KR], float(SL - 1))
            V.tensor_copy(BS[:, 0:KL], PS[:, 5, 0:KL]).then_inc(bs_ok, 1)
            dve.wait_ge(bT_ps, 1)
            step.link(V.tensor_copy(lohi[0:KL, :, :],
                                    PS[0:KL, 6, 0:2 * P].rearrange("k (a b c) -> k a b c", a=2, b=BT)[:, :, :, 0]))
            jr = JG[0:KL, 0, :]

            def on_path(b):
                step.link(V.tensor_scalar(PA[0:KL, :], jr, lohi[0:KL, 0, bass.ds(b, 1)], None, ALU.is_ge))
                wait(dve, e_ps, b)
                V.scalar_tensor_tensor(PM[0:KL, :], jr, lohi[0:KL, 1, bass.ds(b, 1)], PA[0:KL, :], ALU.is_le, ALU.mult).then_inc(pm_ok, 1)
                dve.wait_ge(e_ps, b + 1)
                wait(dve, x3_ok, b)
                V.tensor_tensor(XS[:, :, :].rearrange("p q d -> p (q d)"), PS[:, 1, :],
                                X[:, bass.ds(b * Q, Q), :].rearrange("p q d -> p (q d)"), ALU.add).then_inc(xs_ok, 1)
                dve.wait_ge(xs_ok, NT + BT + b + 1)
                stats(XS, mvs).then_inc(mvs_ok, 1)

            peeled(dve, BT, on_path, step)
            rstd_of(4)
            normalise(3 * BT, 0)

            def logits(b):
                dve.wait_ge(lg_ps, b + 1)
                V.tensor_copy(LG[:, bass.ds(b * Q, Q), :].rearrange("p q e -> p (q e)"), PS[:, 2, 0:Q * NE]).then_inc(lg_ok, 1)

            with dve.Fori(0, BT - 1) as b:
                normalise(3 * BT + b + 1, b + 1)
                logits(b)
            logits(BT - 1)
            dve.wait_ge(lg_ok, BT)

            for t in range(NT):
                ins = V.max(M8[:, t, :], LG[:, t, :])
            step.link(ins)
            for t in range(NT):
                ins = V.max_index(I8[:, t, :], M8[:, t, :], LG[:, t, :])
            step.link(ins)
            step.link(V.tensor_copy(IF8[:, :, :], I8[:, :, 0:2]))
            for j in range(2):
                top = bc(M8[:, :, j:j + 1], [P, NT, NE])
                step.link(V.tensor_tensor(OH[:, j, :, :], JE[:, :, :], bc(IF8[:, :, j:j + 1], [P, NT, NE]), ALU.is_equal))
                step.link(V.tensor_scalar(RA[:, :, :], LG[:, :, :], -1.0, None, ALU.mult))
                step.link(V.tensor_tensor(RA[:, :, :], RA[:, :, :], LG[:, :, :], ALU.max))
                step.link(V.tensor_tensor(RA[:, :, :], RA[:, :, :], top, ALU.max))
                step.link(V.tensor_tensor(RB[:, :, :], top, LG[:, :, :], ALU.subtract))
                step.link(V.scalar_tensor_tensor(RA[:, :, :].rearrange("p t e -> p (t e)"), RA[:, :, :].rearrange("p t e -> p (t e)"), 0.02,
                                                 RB[:, :, :].rearrange("p t e -> p (t e)"), ALU.mult, ALU.is_ge))
                if j == 1:
                    step.link(V.tensor_tensor(RB[:, :, :], OH[:, 0, :, :], RA[:, :, :], ALU.mult))
                    step.link(V.tensor_tensor(RA[:, :, :], RA[:, :, :], RB[:, :, :], ALU.subtract))
                    step.link(V.tensor_tensor(RB[:, :, :], LG[:, :, :], top, ALU.subtract))
                    step.link(V.tensor_scalar(RC[:, j, :, :], RB[:, :, :], 0.0, None, ALU.min))
                    step.link(V.tensor_copy(AC[:, 0, 0:NT * NE], RA[:, :, :].rearrange("p t e -> p (t e)")))
                else:
                    step.link(V.tensor_scalar(RC[:, j, :, :], RB[:, :, :], -1.0, None, ALU.mult))
                    step.link(V.tensor_copy(AC[:, 1, 0:NT * NE], RA[:, :, :].rearrange("p t e -> p (t e)")))
            V.tensor_copy(rstd[:, :], std[:, :]).then_inc(rsub_ok, 1)
            dve.wait_ge(rexp_ok, 1)
            for j in range(2):
                keep = AC[:, 1 - j, 0:NT * NE].rearrange("p (t e) -> p t e", e=NE)
                step.link(V.tensor_tensor(RC[:, j, :, :], RC[:, j, :, :], keep, ALU.mult))
                step.link(V.tensor_reduce(ZS[:, j, :], RC[:, j, :, :], AX, ALU.add))
            step.link(V.reciprocal(ZS[:, :, :], ZS[:, :, :]))
            for j in range(2):
                step.link(V.tensor_tensor(OH[:, j, :, :], OH[:, j, :, :], bc(ZS[:, j, :].unsqueeze(2), [P, NT, NE]), ALU.mult))
            step.link(V.tensor_tensor(GWT[:, :, :], OH[:, 0, :, :], OH[:, 1, :, :], ALU.add))

            def add_out(n, u, m, par):
                dve.wait_ge(y_ps, n + 1)
                wait(dve, y_ok, n)
                t = 2 * u + m // NE
                V.scalar_tensor_tensor(X[:, t, :], PS[:, 4 + par, 0:D], GWT[:, t, m % NE:m % NE + 1], X[:, t, :],
                                       ALU.mult, ALU.add).then_inc(y_ok, 1)

            def experts(u):
                for k in range(2 * NE):
                    n = 2 * NE * u + k
                    dve.wait_ge(si_ok, n + 1)
                    wait(dve, aT_ps, n - 1)
                    V.tensor_tensor(AC[:, k % 2, :], PS[:, k % 2, EI:2 * EI], SI[:, k % 2, :], ALU.mult).then_inc(ac_ok, 1)
                    if not (isinstance(n, int) and n < 2):
                        add_out(n - 2, u, k - 2, k % 2)

            experts(0)
            with dve.Fori(1, NT // 2) as u:
                experts(u)
            for k in range(2):
                add_out(NT * NE - 2 + k, NT // 2 - 1, 2 * NE - 2 + k, k)

        @block.tensor
        def _(pe):
            def mm(o, l, r, start=True, stop=True, **kw):
                return nc.tensor.matmul(o, l, r, start=start, stop=stop, **kw)

            pe.wait_ge(ld_ctx, 16 * N_CTX)
            pe.wait_ge(ld_small, 16 * 4)
            for b in range(BT):
                ins = mm(PS[0:KL, 2, b * D:(b + 1) * D], CT3[:, b, 0:KL], WK[:, :])
            ins.then_inc(k_ps, 1)
            for b in range(BT):
                for c in range(NC):
                    s = c * P % KL
                    ins = mm(PS[:, 4 + b, c * 3 * HD:(c + 1) * 3 * HD], CT3[:, b, s:s + P],
                             WV[:, H0[c] * HD:(H0[c] + 3) * HD])
                ins.then_inc(v_ps, 1)
            pe.wait_ge(bvt_ok, 1)
            mm(PS[:, 3, 0:D], BVT[:, :], WO[:, :]).then_inc(bo_ps, 1)
            pe.wait_ge(c_ident, 1)

            def x_T(r):
                pe.wait_ge(xn_ok, r + 1)
                for q in range(Q):
                    ins = nc.tensor.transpose(PS[:, 0, q * P:(q + 1) * P], XN[:, q, :], ident[:, :])
                ins.then_inc(xT_ps, 1)

            def queries(b):
                wait(pe, xT_sb, b)
                x_T(b)
                pe.wait_ge(xT_sb, b + 1)
                wait(pe, q_sb, b)
                for q in range(Q):
                    ins = mm(PS[:, 1, q * P:(q + 1) * P], XNT[:, q * P:(q + 1) * P], WQ[:, :])
                ins.then_inc(q_ps, 1)

            queries(0)
            with pe.Fori(1, BT) as b:
                queries(b)
            pe.wait_ge(kn_ok, 1)
            for b in range(BT):
                ins = nc.tensor.transpose(PS[:, 2, b * KL:(b + 1) * KL], KQ[:, b * D:(b + 1) * D], ident[0:KL, 0:KL])
            ins.then_inc(kT_ps, 1)
            pe.wait_ge(q_sb, BT)

            def queries_T(b):
                wait(pe, qT_sb, b)
                pe.wait_ge(qn_ok, b + 1)
                for q in range(Q):
                    ins = nc.tensor.transpose(PS[:, 1, q * P:(q + 1) * P], QN[:, q, :], ident[:, :])
                ins.then_inc(qT_ps, 1)

            queries_T(0)
            with pe.Fori(1, BT) as b:
                queries_T(b)

            pe.wait_ge(kb_ok, 1)
            pe.wait_ge(vx_ok, 1)
            pe.wait_ge(bo_ok, 1)
            pe.wait_ge(qT_sb, BT)
            pe.wait_ge(kT_sb, 1)

            def scores(t, b, par, bank):
                h0, h1 = HB[bank]
                n = (h1 - h0) * KL
                o = PS[:, 3 * par + bank, 0:n]
                if bank == 0:
                    pe.wait_ge(qTb_ok, t + 1)
                    wait(pe, sc_sub, 2 * (t - 1))
                mm(o, QTb[:, par, :], KB[:, b, h0 * KL:h1 * KL], stop=False)
                mm(o, ones_b[:, :], mrow[0:1, b, h0:h1, :].rearrange("p h k -> p (h k)"), start=False).then_inc(sc_ps, 1)

            def weights_T(t, par, g):
                if g == 0:
                    pe.wait_ge(exp_ok, t + 1)
                wait(pe, pT_sb, 4 * t + g)
                for c in range(4 * g, min(4 * g + 4, NC)):
                    ins = nc.tensor.transpose(PS[0:CR[c], 6, (c - 4 * g) * P:(c - 4 * g + 1) * P],
                                              PR[:, par, c * P:c * P + CR[c]], ident[:, :])
                ins.then_inc(pT_ps, 1)

            def out_T(t):
                pe.wait_ge(on_ok, t + 1)
                nc.tensor.transpose(PS[:, 7, 256:384], ON[:, :], ident[:, :]).then_inc(oT_ps, 1)

            def out_proj(t):
                pe.wait_ge(oT_sb, t + 1)
                mm(PS[:, 7, 384:512], OT[:, :], WO[:, :]).then_inc(wo_ps, 1)

            for bank in range(3):
                scores(0, 0, 0, bank)

            def attend(b):
                for q in range(Q):
                    t, par = b * Q + q, q % 2
                    first, final = isinstance(t, int) and t == 0, isinstance(t, int) and t == NT - 1
                    for g in range(3):
                        weights_T(t, par, g)
                        if not final:
                            scores(t + 1, b if q < Q - 1 else b + 1, 1 - par, g)
                        if not first and g == 0:
                            out_T(t - 1)
                        if not first and g == 1:
                            out_proj(t - 1)
                    pe.wait_ge(pT_sb, 4 * t + 4)
                    wait(pe, xs_ok, t)
                    for c in range(NC):
                        ins = mm(PS[:, 7, H0[c] * VW:(H0[c] + 3) * VW], PT[0:CR[c], c, :],
                                 VX[0:CR[c], b, 3 * c:3 * c + 3, :].rearrange("p m w -> p (m w)"),
                                 start=c == 0, stop=c == NC - 1, skip_group_check=True)
                    ins.then_inc(pv_ps, 1)

            peeled(pe, BT, attend)
            out_T(NT - 1)
            out_proj(NT - 1)

            pe.wait_ge(wf_ok, 1)
            pe.wait_ge(xs_ok, NT)
            x_T(BT)

            def ffn(b):
                for c in range(FC):
                    if c == 0:
                        pe.wait_ge(xT_sb, BT + b + 1)
                    wait(pe, h_ok, FC * (b - 1) + c + 1)
                    mm(PS[:, 1 + 2 * c, :], WG[:, c * P:(c + 1) * P], XNT[:, :]).then_inc(g_ps, 1)
                    mm(PS[:, 2 + 2 * c, :], WU[:, c * P:(c + 1) * P], XNT[:, :]).then_inc(u_ps, 1)
                if not (isinstance(b, int) and b == BT - 1):
                    x_T(BT + b + 1)
                pe.wait_ge(h_ok, FC * (b + 1))
                pe.wait_ge(xs_ok, NT + b)
                for q in range(Q):
                    for c in range(FC):
                        ins = mm(PS[:, 7, q * D:(q + 1) * D], HT[:, c, q * P:(q + 1) * P], WD2[:, c, :],
                                 start=c == 0, stop=c == FC - 1)
                ins.then_inc(dn_ps, 1)

            peeled(pe, BT, ffn)

            pe.wait_ge(cn_ok, 1)
            pe.wait_ge(xs_ok, NT + BT)
            x_T(2 * BT)

            def distances(b, more):
                pe.wait_ge(xT_sb, 2 * BT + b + 1)
                pe.wait_ge(xsq_ok, b + 1)
                if more:
                    x_T(2 * BT + b + 1)
                o = PS[0:KR, 1 + b, :]
                return o

            for b in range(BT):
                o = distances(b, b < BT - 1)
                mm(o, CN2[:, b, :], XNT[:, :], stop=False)
                mm(o, ones_f[:, 0:KR], XSQ[:, :], start=False).then_inc(d_ps, 1)

            pe.wait_ge(d_pos, BT)
            pe.wait_ge(f_ok, 1)
            for c in range(CC):
                ins = nc.tensor.transpose(PS[:, c // 6, c % 6 * 85:c % 6 * 85 + KR], FX[:, c:BT * SL:CC], ident[0:KR, 0:KR])
                if c % 6 == 5 or c == CC - 1:
                    ins.then_inc(fT_ps, 1)

            pe.wait_ge(c_all, 2)
            pe.wait_ge(hit_ok, 1)
            mm(PS[:, 5, KL - 1:KL], blk1[:, :], hs[:, 0:1]).then_inc(b_ps, 1)
            with pe.Fori(0, (KL - 1) // 4) as w:
                for k in range(4):
                    pe.wait_ge(hit_ok, w * 4 + k + 2)
                    mm(PS[:, 5, bass.ds(w * (-4) + (KL - 2 - k), 1)], blk1[:, :], hs[:, (k + 1) % 2:(k + 1) % 2 + 1]).then_inc(b_ps, 1)
            pe.wait_ge(bs_ok, 1)
            for j in range(2):
                ins = nc.tensor.transpose(PS[0:KL, 6, j * P:(j + 1) * P], BS[:, j:j + KL], ident[:, :])
            ins.then_inc(bT_ps, 1)

            def aligned(b):
                pe.wait_ge(pm_ok, b + 1)
                pe.wait_ge(xs_ok, NT + BT + b)
                for q in range(Q):
                    ins = mm(PS[:, 1, q * D:(q + 1) * D], PM[0:KL, q * P:(q + 1) * P], CK[0:KL, b, :])
                ins.then_inc(e_ps, 1)

            aligned(0)
            with pe.Fori(1, BT) as b:
                aligned(b)

            def router(b):
                wait(pe, xT_sb, 3 * BT + b)
                x_T(3 * BT + b)
                pe.wait_ge(xT_sb, 3 * BT + b + 1)
                wait(pe, lg_ok, b)
                for q in range(Q):
                    ins = mm(PS[:, 2, q * NE:(q + 1) * NE], XNT[:, q * P:(q + 1) * P], GW[:, :])
                ins.then_inc(lg_ps, 1)

            pe.wait_ge(ld_moe, 16)
            with pe.Fori(0, BT) as b:
                router(b)

            pe.wait_ge(lg_ok, BT)
            pe.wait_ge(xs_ok, NT + 2 * BT)
            pe.wait_ge(ld_moe, 48)

            def acts_T(n, par):
                pe.wait_ge(ac_ok, n + 1)
                wait(pe, aT_sb, n - 1)
                for c in range(EC):
                    ins = nc.tensor.transpose(PS[:, 2 + par, c * P:(c + 1) * P], AC[:, par, c * P:(c + 1) * P], ident[:, :])
                ins.then_inc(aT_ps, 1)

            def second(n, m, par):
                pe.wait_ge(aT_sb, n + 1)
                wait(pe, y_ok, n - 1)
                for c in range(EC):
                    ins = mm(PS[:, 4 + par, 0:D], AT[:, par, c, :], W2[:, m % NE, c, :], start=c == 0, stop=c == EC - 1)
                ins.then_inc(y_ps, 1)

            def experts(u):
                for k in range(2 * NE):
                    n = 2 * NE * u + k
                    if k % NE == 0:
                        pe.wait_ge(xTb_ok, 2 * u + k // NE + 1)
                    wait(pe, ac_ok, n - 1)
                    mm(PS[:, k % 2, :], XTb[:, k // NE, :], W13[:, k % NE, :]).then_inc(m1_ps, 1)
                    if not (isinstance(n, int) and n < 1):
                        acts_T(n - 1, (k - 1) % 2)
                    if not (isinstance(n, int) and n < 2):
                        second(n - 2, k - 2, k % 2)

            experts(0)
            with pe.Fori(1, NT // 2) as u:
                experts(u)
            acts_T(NT * NE - 1, 1)
            for k in range(2):
                second(NT * NE - 2 + k, 2 * NE - 2 + k, k)


_OUTS = [((4, 512, 128), "float32")]


def kernel(**inputs):
    import numpy as _np
    import concourse.bacc as _bacc
    from concourse import mybir as _mybir
    from concourse.bass_utils import run_bass_kernel_spmd as _run

    g = {k: _np.asarray(v) for k, v in inputs.items()}
    ctx = g["ctx_1024"]
    w1, w3, w2 = g["L1_ffn_w1"], g["L1_ffn_w3"], g["L1_ffn_w2"]
    ne, ei, d = w1.shape
    w13 = _np.stack([w1, w3], axis=1).transpose(3, 0, 1, 2).reshape(d, ne * 2 * ei)
    named = [
        ("x", g["x"]), ("ctx_dt", ctx.transpose(2, 0, 1).reshape(d, -1)), ("ctx_kd", ctx),
        ("mask", g["mask_BxS2_ik0"]),
        ("wqT", g["L0_xattn_Wq"].T), ("bq", g["L0_xattn_bq"]), ("wkT", g["L0_xattn_Wk"].T), ("bk", g["L0_xattn_bk"]),
        ("wvT", g["L0_xattn_Wv"].T), ("bv", g["L0_xattn_bv"]), ("woT", g["L0_xattn_Wo"].T), ("bo", g["L0_xattn_bo"]),
        ("qw", g["L0_xattn_q_norm_w"]), ("kw", g["L0_xattn_k_norm_w"]),
        ("wgT", g["L0_ffn_w_gate"].T), ("wuT", g["L0_ffn_w_up"].T), ("wdT", g["L0_ffn_w_down"].T),
        ("gateT", g["L1_ffn_gate_w"].T), ("w13T", w13), ("w2T", w2.transpose(0, 2, 1).reshape(ne * ei, d)),
    ]
    nc = _bacc.Bacc("TRN2", target_bir_lowering=False, num_devices=1)
    arrays, args = {}, []
    for name, a in named:
        a = _np.ascontiguousarray(a)
        arrays[f"in_{name}_dram"] = a
        args.append(nc.dram_tensor(f"in_{name}_dram", a.shape, _mybir.dt.from_np(a.dtype), kind="ExternalInput").ap())
    for i, (shape, dtype) in enumerate(_OUTS):
        dt = _mybir.dt.from_np(_np.dtype(dtype))
        args.append(nc.dram_tensor(f"out_{i}_dram", shape, dt, kind="ExternalOutput").ap())
    build(nc, *args)
    r = _run(nc, [arrays], core_ids=[0])
    return r.results[0]["out_0_dram"]
```

```python
from contextlib import ExitStack

import concourse.bass as bass
from concourse import mybir

F32 = mybir.dt.float32
F32R = mybir.dt.float32r
F16 = mybir.dt.float16
BF16 = mybir.dt.bfloat16
I32 = mybir.dt.int32
U32 = mybir.dt.uint32
ALU = mybir.AluOpType
ACT = mybir.ActivationFunctionType
AX = mybir.AxisListType.X

P = 128
BIG = 1.0e30
STAGE = "all"


class Steps:

    def __init__(self, eng, sem):
        self.eng, self.sem, self.n = eng, sem, 0

    def link(self, ins):
        ins.then_inc(self.sem, 1)
        self.n += 1
        self.eng.wait_ge(self.sem, self.n)

    def restart(self):
        self.eng.sem_clear(self.sem)
        self.n = 0


def peeled(eng, stop, body, count=None):
    body(0)
    with eng.Fori(1, stop - 1) as i:
        if count:
            count.restart()
        body(i)
    body(stop - 1)


def wait(eng, semaphore, value):
    if not isinstance(value, int) or value > 0:
        eng.wait_ge(semaphore, value)


def build(nc, x, ctx_dt, ctx_kd, mask, wqT, bq, wkT, bk, wvT, bv, woT, bo, qw, kw,
          wgT, wuT, wdT, gateT, w13T, w2T, out):
    BT, SL, D = x.shape[0], x.shape[1], x.shape[2]
    Q = SL // P
    NT = BT * Q
    KL = ctx_dt.shape[1] // BT
    HD = qw.shape[0]
    NH = D // HD
    SCALE = float(HD) ** -0.5
    HID = wgT.shape[1]
    FC = HID // P
    DQ = 1.0 / 127.0
    NE = gateT.shape[1]
    EI = w2T.shape[0] // NE
    EC = EI // P
    HK = NH * KL
    NC = -(-HK // P)
    HB = [(0, 6), (6, 12), (12, 16)]
    H0 = [min(c * P // KL, NH - 3) for c in range(NC)]
    CR = [min(P, HK - c * P) for c in range(NC)]
    VW = HD + 1

    RW = 3
    NI = -(-KL // RW)
    CB = 64
    NB = SL // CB
    NS = NB + NI - 1
    W = NS * CB
    WN = 4
    NWIN = -(-NS // WN)
    KR = NI * RW
    WD = CB + W
    JB = P // BT
    CC = SL // JB
    LN_EPS, Q_EPS = 1e-5, 1e-6

    ds = nc.dram_tensor("cost_skewed", (P, RW, WD), F32, kind="Internal").ap()
    rs = nc.dram_tensor("sums_skewed", (P, RW, WD), F32, kind="Internal").ap()

    with ExitStack() as ctx:
        def sb(name, shape, dt=F32):
            return ctx.enter_context(nc.sbuf_tensor(name, shape, dt))

        def sem(name):
            return ctx.enter_context(nc.semaphore(name))

        X = sb("X", [P, NT, D])
        XN = sb("XN", [P, Q, D])
        XNT = sb("XNT", [P, Q * P])
        space1 = sb("space1", [P, NT * D])
        space2 = sb("space2", [P, NT * D])
        space3 = sb("space3", [P, NT * P])
        space4 = sb("space4", [P, BT * HK])
        space5 = sb("space5", [P, 2 * HK])
        space6 = sb("space6", [P, NC * P])
        space7 = sb("space7", [P, 2 * FC * Q * P])
        space8 = sb("space8", [P, 2 * 3 * HID])

        def part(t, shape, at=0):
            n = 1
            for d in shape[1:]:
                n *= d
            v = t[0:shape[0], at:at + n]
            if len(shape) == 3:
                return v.rearrange("p (a b) -> p a b", a=shape[1])
            if len(shape) == 4:
                return v.rearrange("p (a b c) -> p a b c", a=shape[1], b=shape[2])
            return v

        Qs = part(space1, [P, NT * D])
        SQ = part(space2, [P, NT * D])
        QN = sb("QN", [P, Q, D])
        QT = part(space3, [P, NT, P])
        QTb = sb("QTb", [P, 2, P])
        qss = sb("qss", [P, NT * NH])
        qrs = sb("qrs", [P, NT * NH])
        KQ = part(space7, [KL, BT * D], SL * 2)
        CSQ = part(space7, [KR, BT * D], BT * SL)
        KSQ = CSQ[0:KL, :]
        kss = sb("kss", [KL, BT * NH])
        krs = sb("krs", [KL, BT * NH])
        KT = sb("KT", [P, BT * KL])
        KB = part(space4, [P, BT, HK])
        VX = sb("VX", [P, BT, NC * 3, VW])
        CT3 = part(space7, [P, BT, 3 * KL])
        CK = sb("CK", [KR, BT, D])
        WQ, WK, WV, WO = (sb(n, [P, D]) for n in ("WQ", "WK", "WV", "WO"))
        BQ, BK, BO, BIASO = (sb(n, [P, D]) for n in ("BQ", "BK", "BO", "BIASO"))
        bvc = sb("bvc", [P, 1])
        BVT = sb("BVT", [P, P])
        qwb = sb("qwb", [P, HD])
        kwb = sb("kwb", [P, HD])
        qkw = sb("qkw", [P, HD])
        mi = sb("mi", [P, BT, KL], I32)
        mz = sb("mz", [P, BT, KL])
        mrow = sb("mrow", [1, BT, KL], BF16)
        ones_b = sb("ones_b", [1, P], BF16)
        cnt = sb("cnt", [P, BT])
        nanf = sb("nanf", [P, BT])
        mx = sb("mx", [P, NH])
        PR = part(space5, [P, 2, HK])
        PT = part(space6, [P, NC, P])
        rcp = sb("rcp", [P, NH])
        ON = sb("ON", [P, D])
        OT = sb("OT", [P, P])
        bst = sb("bst", [P, Q, 6])
        mv = sb("mv", [P, NT, 2])
        XS = sb("XS", [P, Q, D])
        mvs = sb("mvs", [P, Q, 2])
        std = sb("std", [P, NT])
        rstd = sb("rstd", [P, NT])
        epsl = sb("epsl", [P, 1])
        epsq = sb("epsq", [P, 1])
        wi = space8[:, 0:3 * HID].bitcast(I32)
        WG = part(space8, [P, HID], 3 * HID)
        WU = part(space8, [P, HID], 4 * HID)
        WD2 = part(space8, [P, FC, D], 5 * HID)
        HS = part(space7, [P, FC, Q * P])
        HT = part(space7, [P, FC, Q * P], FC * Q * P)
        ident = sb("ident", [P, P])
        HM = sb("HM", [P, NH])
        HMC = sb("HMC", [P, NC * 3])
        ones_f = sb("ones_f", [P, P])
        CN2 = sb("CN2", [P, BT, KR])
        aa = sb("aa", [KR, BT])
        XSQ = part(space6, [P, Q * P])
        DSQ = part(space2, [KR, BT, SL])
        DSB = part(space1, [KR, BT, SL])
        DP = part(space3, [P, 2, RW, WN * CB])
        WS = sb("WS", [P, 2, RW + 1, 1 + WN * CB])
        bigs = part(space6, [P, WD // 2])
        MM = sb("MM", [P, RW, CB])
        RI = part(space8, [KR, BT, SL + 1])
        UI = part(space5, [KR + 1, BT, SL + 1])
        T1 = part(space1, [KR, BT, SL])
        T2 = part(space2, [KR, BT, SL])
        JG = part(space7, [KR, BT, SL])
        FX = part(space3, [KR, BT * SL])
        FT = part(space6, [P, KR, CC])
        JH = sb("JH", [P, CC, 2])
        goff = sb("goff", [P, 1])
        blk1 = sb("blk1", [P, P], F16)
        hit = sb("hit", [P, CC, 2])
        hs = sb("hs", [P, 2], F16)
        last = sb("last", [P, 1])
        BS = sb("BS", [P, KR])
        lohi = sb("lohi", [KR, 2, BT])
        PA = part(space5, [KR, SL])
        PM = part(space5, [KR, SL], SL)
        GW = sb("GW", [P, NE])
        XT4 = part(space3, [P, NT * P])
        XTH = sb("XTH", [P, Q * P], F32R)
        XTL = sb("XTL", [P, Q * P], F32R)
        LG = sb("LG", [P, NT, NE])
        M8 = sb("M8", [P, NT, 8])
        I8 = sb("I8", [P, NT, 8], U32)
        IF8 = sb("IF8", [P, NT, 2])
        JE = sb("JE", [P, NT, NE])
        OH = sb("OH", [P, 2, NT, NE])
        RA = sb("RA", [P, NT, NE])
        RB = sb("RB", [P, NT, NE])
        RC = sb("RC", [P, 2, NT, NE])
        ZS = sb("ZS", [P, 2, NT])
        GWT = sb("GWT", [P, NT, NE])
        W13 = part(space4, [P, NE, 2 * EI])
        W2 = sb("W2", [P, NE * EC, D])
        W13H = sb("W13H", [P, NE, 2 * EI], F32R)
        W13L = sb("W13L", [P, NE, 2 * EI], F32R)
        KEEP = sb("KEEP", [P, 2, NT * NE])
        SI = part(space5, [P, EC, Q * P])
        HA = part(space4, [P, 2 * EC, Q * P])
        PS = ctx.enter_context(nc.psum_tensor("PS", [P, 8, 512], F32))

        ld_x = sem("ld_x")
        ld_q = sem("ld_q")
        ld_k = sem("ld_k")
        ld_v = sem("ld_v")
        ld_mask = sem("ld_mask")
        ld_ffn = sem("ld_ffn")
        ld_moe = sem("ld_moe")
        ld_gate = sem("ld_gate")
        xth_ok = sem("xth_ok")
        xtl_ok = sem("xtl_ok")
        c_ident = sem("c_ident")
        c_step = sem("c_step")
        c_heads = sem("c_heads")
        c_all = sem("c_all")
        v_step = sem("v_step")
        k_ps = sem("k_ps")
        v_ps = sem("v_ps")
        kss_ok = sem("kss_ok")
        kst_ok = sem("kst_ok")
        kn_ok = sem("kn_ok")
        kT_ps = sem("kT_ps")
        kT_sb = sem("kT_sb")
        kb_ok = sem("kb_ok")
        vx_ok = sem("vx_ok")
        bvt_ok = sem("bvt_ok")
        bo_ps = sem("bo_ps")
        bo_ok = sem("bo_ok")
        var_ok = sem("var_ok")
        std_ok = sem("std_ok")
        xn_ok = sem("xn_ok")
        xT_ps = sem("xT_ps")
        xT_sb = sem("xT_sb")
        q_ps = sem("q_ps")
        q_sb = sem("q_sb")
        qsq_ok = sem("qsq_ok")
        mask_ok = sem("mask_ok")
        qss_ok = sem("qss_ok")
        qst_ok = sem("qst_ok")
        qn_ok = sem("qn_ok")
        qT_ps = sem("qT_ps")
        qT_sb = sem("qT_sb")
        qTb_ok = sem("qTb_ok")
        sc_ps = sem("sc_ps")
        sc_sub = sem("sc_sub")
        exp_ok = sem("exp_ok")
        pT_ps = sem("pT_ps")
        pT_sb = sem("pT_sb")
        pv_ps = sem("pv_ps")
        on_ok = sem("on_ok")
        oT_ps = sem("oT_ps")
        oT_sb = sem("oT_sb")
        wo_ps = sem("wo_ps")
        x1_ok = sem("x1_ok")
        wf_ok = sem("wf_ok")
        g_ps = sem("g_ps")
        u_ps = sem("u_ps")
        silu_ok = sem("silu_ok")
        h_ok = sem("h_ok")
        dn_ps = sem("dn_ps")
        x2_ok = sem("x2_ok")
        xsq_ok = sem("xsq_ok")
        d_ps = sem("d_ps")
        d_pos = sem("d_pos")
        d_ok = sem("d_ok")
        cn_ok = sem("cn_ok")
        bo_add = sem("bo_add")
        r1_ok = sem("r1_ok")
        xt4_ok = sem("xt4_ok")
        big_ok = sem("big_ok")
        dpre = sem("dpre")
        dst = sem("dst")
        dld = sem("dld")
        r_ok = sem("r_ok")
        xs_ok = sem("xs_ok")
        mvs_ok = sem("mvs_ok")
        ui_ok = sem("ui_ok")
        rpre = sem("rpre")
        rst = sem("rst")
        rld = sem("rld")
        f_ok = sem("f_ok")
        fT_ps = sem("fT_ps")
        hit_ok = sem("hit_ok")
        b_ps = sem("b_ps")
        bs_ok = sem("bs_ok")
        bT_ps = sem("bT_ps")
        pm_ok = sem("pm_ok")
        e_ps = sem("e_ps")
        x3_ok = sem("x3_ok")
        lg_ps = sem("lg_ps")
        lg_ok = sem("lg_ok")
        rsub_ok = sem("rsub_ok")
        rexp_ok = sem("rexp_ok")
        gate_ok = sem("gate_ok")
        w_hi = sem("w_hi")
        w_lo = sem("w_lo")
        eg_ps = sem("eg_ps")
        eu_ps = sem("eu_ps")
        si_ok = sem("si_ok")
        ac_ok = sem("ac_ok")
        y_ps = sem("y_ps")
        y_ok = sem("y_ok")
        st_out = sem("st_out")

        def bc(ap, shape):
            return ap.to_broadcast(shape)

        def steps3(t):
            return t.rearrange("p (h d) -> p h d", d=HD)

        block = ctx.enter_context(nc.Block())

        x_v = x.rearrange("b (q p) d -> b p q d", p=P)
        out_v = out.rearrange("b (q p) d -> b p q d", p=P)
        XV = X[:, :, :].rearrange("p (b q) d -> p b q d", b=BT)

        def skewed(t, b, shift, row, cols):
            ps = RW * WD
            return bass.AP(t.tensor, b * (P // BT) * ps + row * WD + CB + shift,
                           [[ps + CB, NI], [WD, RW], [1, cols]])

        @block.sync
        def _(sp):
            for b in range(BT):
                sp.dma_start(X[:, b * Q:(b + 1) * Q, :], x_v[b]).then_inc(ld_x, 16)
            for j in range(3):
                sp.dma_start(CT3[:, :, j * KL:(j + 1) * KL], ctx_dt.rearrange("d (b k) -> d b k", b=BT)).then_inc(ld_k, 16)
            sp.dma_start(WV[:, :], wvT).then_inc(ld_v, 16)
            sp.dma_start(WO[:, :], woT).then_inc(ld_v, 16)
            sp.dma_start(bvc[:, :], bv.rearrange("(d a) -> d a", a=1)).then_inc(ld_v, 16)
            sp.dma_start(BO[:, :], bo.rearrange("(a d) -> a d", a=1).partition_broadcast(P)).then_inc(ld_v, 16)
            sp.dma_start(CK[0:KL, :, :], ctx_kd.rearrange("b k d -> k b d")).then_inc(ld_v, 16)
            sp.dma_start(CK[KL:KR, :, :], ctx_kd[:, 0:KR - KL, :].rearrange("b k d -> k b d")).then_inc(ld_v, 16)
            sp.dma_start(wi[:, 0:HID], wgT).then_inc(ld_ffn, 16)
            sp.dma_start(wi[:, HID:2 * HID], wuT).then_inc(ld_ffn, 16)
            sp.dma_start(wi[:, 2 * HID:3 * HID].rearrange("p (c d) -> p c d", c=FC),
                         wdT.rearrange("(c p) d -> p c d", p=P)).then_inc(ld_ffn, 16)
            sp.wait_ge(big_ok, 1)
            for r in range(RW):
                for h in range(2):
                    sp.dma_start(ds[:, r, h * WD // 2:(h + 1) * WD // 2], bigs[:, :]).then_inc(dpre, 16)
                    sp.dma_start(rs[:, r, h * WD // 2:(h + 1) * WD // 2], bigs[:, :]).then_inc(rpre, 16)
            sp.dma_start(GW[:, :], gateT).then_inc(ld_gate, 16)
            sp.wait_ge(dpre, 16 * 2 * RW)
            for b in range(BT):
                sp.wait_ge(d_ok, b + 1)
                sp.dma_start(skewed(ds, b, 0, 0, SL), DSB[:, b, :]).then_inc(dst, 16)
            sp.wait_ge(dst, 16 * BT)

            def costs(w):
                a, z = w * WN * CB, min((w + 1) * WN, NS) * CB
                wait(sp, dld, 16 * w)
                sp.dma_start(DP[:, w % 2, :, 0:z - a], ds[:, :, CB + a:CB + z]).then_inc(dld, 16)

            costs(0)
            costs(1)
            sp.wait_ge(rpre, 16 * 2 * RW)
            for w in range(NWIN):
                a, z = w * WN * CB, min((w + 1) * WN, NS) * CB
                sp.wait_ge(r_ok, w + 1)
                if w + 2 < NWIN:
                    costs(w + 2)
                wait(sp, rst, 16 * w)
                sp.dma_start(rs[:, :, CB + a:CB + z], WS[:, w % 2, 1:RW + 1, 1:1 + z - a]).then_inc(rst, 16)
            sp.wait_ge(rst, 16 * NWIN)
            sp.wait_ge(ui_ok, 1)
            for b in range(BT):
                sp.dma_start(RI[:, b, :], skewed(rs, b, -1, 0, SL + 1)).then_inc(rld, 16)
                sp.dma_start(UI[1:KR + 1, b, :], skewed(rs, b, -1, 0, SL + 1)).then_inc(rld, 16)
            for b in range(BT):
                sp.wait_ge(y_ok, NE * (b + 1))
                sp.dma_start(out_v[b], X[:, b * Q:(b + 1) * Q, :]).then_inc(st_out, 16)
            sp.wait_ge(st_out, 16 * BT)

        @block.gpsimd
        def _(pool):
            step = Steps(pool, c_step)
            nc.gpsimd.memset(epsl[:, :], LN_EPS)
            nc.gpsimd.memset(epsq[:, :], Q_EPS).then_inc(c_all, 1)
            step.link(nc.gpsimd.memset(ident[:, :], 0.0))
            nc.gpsimd.affine_select(out=ident[:, :], in_=ident[:, :], compare_op=ALU.not_equal, fill=1.0, base=0,
                                    pattern=[[-1, P]], channel_multiplier=1).then_inc(c_ident, 1)
            step.link(nc.gpsimd.memset(HM[:, :], 1.0))
            step.link(nc.gpsimd.affine_select(out=HM[:, :], in_=HM[:, :], compare_op=ALU.is_ge, fill=0.0, base=0,
                                              pattern=[[-HD, NH]], channel_multiplier=1))
            step.link(nc.gpsimd.affine_select(out=HM[:, :], in_=HM[:, :], compare_op=ALU.is_ge, fill=0.0, base=HD - 1,
                                              pattern=[[HD, NH]], channel_multiplier=-1))
            step.link(nc.gpsimd.memset(HMC[:, :], 1.0))
            for c in range(NC):
                part = HMC[:, 3 * c:3 * c + 3]
                step.link(nc.gpsimd.affine_select(out=part, in_=part, compare_op=ALU.is_ge, fill=0.0,
                                                  base=P * c - KL * H0[c], pattern=[[-KL, 3]], channel_multiplier=1))
                step.link(nc.gpsimd.affine_select(out=part, in_=part, compare_op=ALU.is_ge, fill=0.0,
                                                  base=KL * (H0[c] + 1) - 1 - P * c, pattern=[[KL, 3]],
                                                  channel_multiplier=-1))
            for b in range(BT):
                ins = nc.gpsimd.tensor_copy(VX[:, b, :, HD], HMC[:, :])
            ins.then_inc(c_heads, 1)
            step.link(nc.gpsimd.memset(ones_f[:, :], 1.0))
            pool.wait_ge(ld_v, 16 * 6)
            nc.gpsimd.tensor_scalar(BVT[:, :], ones_f[:, :], bvc[:, :], None, ALU.mult).then_inc(bvt_ok, 1)
            nc.gpsimd.memset(ones_b[:, :], 1.0)
            pool.wait_ge(ld_k, 16 * 7)
            nc.gpsimd.tensor_scalar(CN2[:, :, :], CT3[:, :, 0:KR], -2.0, None, ALU.mult).then_inc(cn_ok, 1)
            pool.wait_ge(bo_ok, 1)
            for b in range(BT):
                pool.wait_ge(xn_ok, b + 1)
                nc.gpsimd.tensor_tensor(X[:, b * Q:(b + 1) * Q, :], X[:, b * Q:(b + 1) * Q, :],
                                        bc(BIASO[:, :].unsqueeze(1), [P, Q, D]), ALU.add).then_inc(bo_add, 1)
            nc.gpsimd.memset(bigs[:, :], BIG).then_inc(big_ok, 1)
            step.link(nc.gpsimd.memset(WS[:, :, :, :], BIG))
            for b in range(BT):
                step.link(nc.gpsimd.memset(WS[b * 32:b * 32 + 1, 0, 0, 0:1], 0.0))
            step.link(nc.gpsimd.memset(last[:, :], float(SL - 1)))
            step.link(nc.gpsimd.iota(JE[:, :, :], pattern=[[0, NT], [1, NE]], base=0, channel_multiplier=0,
                                     allow_small_or_imprecise_dtypes=True))
            for g in range(BT):
                step.link(nc.gpsimd.iota(JH[g * JB:(g + 1) * JB, :, 0], pattern=[[1, CC]], base=0, channel_multiplier=CC,
                                         allow_small_or_imprecise_dtypes=True))
                step.link(nc.gpsimd.memset(goff[g * JB:(g + 1) * JB, :], float(SL * g)))
            step.link(nc.gpsimd.memset(blk1[:, :], 0.0))
            for g in range(BT):
                step.link(nc.gpsimd.memset(blk1[g * JB:(g + 1) * JB, g * JB:(g + 1) * JB], 1.0))
            step.link(nc.gpsimd.memset(hs[:, :], 0.0))
            nc.gpsimd.tensor_scalar(JH[:, :, 1], JH[:, :, 0], 0.5, None, ALU.add).then_inc(c_all, 1)

            pool.wait_ge(ld_ffn, 48)
            nc.gpsimd.tensor_copy(WG[:, :], wi[:, 0:HID])
            nc.gpsimd.tensor_copy(WU[:, :], wi[:, HID:2 * HID])
            nc.gpsimd.tensor_copy(WD2[:, :, :].rearrange("p c d -> p (c d)"), wi[:, 2 * HID:3 * HID]).then_inc(wf_ok, 1)

            def store(t0, n, src, msrc, done, count):
                pool.wait_ge(mvs_ok, count)
                nc.gpsimd.tensor_copy(X[:, t0 if n == 1 else bass.ds(t0, n), :], src)
                nc.gpsimd.tensor_copy(mv[:, t0 if n == 1 else bass.ds(t0, n), :], msrc).then_inc(done, 1)

            def queries(b):
                for q in range(Q):
                    t = b * Q + q
                    pool.wait_ge(qT_sb, b + 1)
                    wait(pool, sc_ps, 3 * (t - 1))
                    nc.gpsimd.tensor_copy(QTb[:, q % 2, :], QT[:, t, :]).then_inc(qTb_ok, 1)
                    if not (isinstance(t, int) and t < 3):
                        store(t - 3, 1, XS[:, (q - 3) % Q, :], mvs[:, (q - 3) % Q, :], x1_ok, t - 2)

            peeled(pool, BT, queries)
            for t in range(NT - 3, NT):
                store(t, 1, XS[:, t % Q, :], mvs[:, t % Q, :], x1_ok, t + 1)
            with pool.Fori(0, BT) as b:
                store(b * Q, Q, XS[:, :, :], mvs[:, :, :], x2_ok, b + (NT + 1))

            pool.wait_ge(pT_ps, 3 * NT)
            step.link(nc.gpsimd.memset(UI[0:1, :, :], BIG))
            nc.gpsimd.memset(UI[0:1, :, 0:1], 0.0).then_inc(ui_ok, 1)
            pool.wait_ge(dn_ps, BT)
            nc.gpsimd.iota(JG[:, :, :], pattern=[[SL, BT], [1, SL]], base=0, channel_multiplier=0,
                           allow_small_or_imprecise_dtypes=True).then_inc(ui_ok, 1)

            for e in range(NE):
                pool.wait_ge(w_hi, e + 1)
                nc.gpsimd.tensor_tensor(W13L[:, e, :], W13[:, e, :], W13H[:, e, :].bitcast(F32), ALU.subtract).then_inc(w_lo, 1)

            with pool.Fori(0, BT) as b:
                store(b * Q, Q, XS[:, :, :], mvs[:, :, :], x3_ok, b + (NT + BT + 1))
            with pool.Fori(0, BT) as b:
                pool.wait_ge(xT_sb, 3 * BT + b + 1)
                nc.gpsimd.tensor_copy(XT4[:, bass.ds(b * Q * P, Q * P)], XNT[:, :]).then_inc(xt4_ok, 1)

            def low_inputs(b):
                pool.wait_ge(xth_ok, b + 1)
                nc.gpsimd.tensor_tensor(XTL[:, :], XT4[:, b * Q * P:(b + 1) * Q * P] if isinstance(b, int) else XT4[:, bass.ds(b * Q * P, Q * P)],
                                        XTH[:, :].bitcast(F32), ALU.subtract).then_inc(xtl_ok, 1)

            low_inputs(0)
            with pool.Fori(1, BT) as b:
                low_inputs(b)

        @block.scalar
        def _(act):
            act.dma_start(WQ[:, :], wqT).then_inc(ld_q, 16)
            act.dma_start(BQ[:, :], bq.rearrange("(a d) -> a d", a=1).partition_broadcast(P)).then_inc(ld_q, 16)
            act.dma_start(WK[:, :], wkT).then_inc(ld_k, 16)
            for t, v in ((BK, bk), (qwb, qw), (kwb, kw)):
                act.dma_start(t[:, :], v.rearrange("(a d) -> a d", a=1).partition_broadcast(P)).then_inc(ld_k, 16)
            act.dma_start(mi[:, :, :].rearrange("p b k -> p (b k)"),
                          mask.rearrange("(a b) k -> a (b k)", a=1).partition_broadcast(P)).then_inc(ld_mask, 16)

            def copy(out, in_):
                return nc.scalar.activation(out, in_, ACT.Copy)

            act.wait_ge(c_all, 1)
            def std_of(semaphore, value):
                act.wait_ge(semaphore, value)
                nc.scalar.activation(std[:, :], mv[:, :, 1], ACT.Sqrt, bias=epsl[:, :]).then_inc(std_ok, 1)

            def copy_xT(r):
                act.wait_ge(xT_ps, r + 1)
                copy(XNT[:, :], PS[:, 0, :]).then_inc(xT_sb, 1)

            std_of(var_ok, 1)

            for b in range(BT + 1):
                if b < BT:
                    wait(act, q_ps, b)
                    copy_xT(b)
                if b == 1:
                    act.wait_ge(kss_ok, 1)
                    nc.scalar.activation(krs[:, :], kss[:, :], ACT.Sqrt, bias=epsq[0:KL, :], scale=1.0 / HD).then_inc(kst_ok, 1)
                if b == 2:
                    act.wait_ge(kT_ps, 1)
                    copy(KT[:, :], PS[:, 2, 0:BT * KL]).then_inc(kT_sb, 1)
                if b > 0:
                    act.wait_ge(qss_ok, b)
                    nc.scalar.activation(qrs[:, (b - 1) * Q * NH:b * Q * NH], qss[:, (b - 1) * Q * NH:b * Q * NH], ACT.Sqrt,
                                         bias=epsq[:, :], scale=1.0 / HD).then_inc(qst_ok, 1)
                if b < BT:
                    act.wait_ge(q_sb, b + 1)
                    nc.scalar.activation(SQ[:, b * Q * D:(b + 1) * Q * D], Qs[:, b * Q * D:(b + 1) * Q * D], ACT.Square).then_inc(qsq_ok, 1)
                if b > 0:
                    act.wait_ge(qT_ps, b)
                    copy(QT[:, (b - 1) * Q:b * Q, :].rearrange("p q c -> p (q c)"), PS[:, 3, :]).then_inc(qT_sb, 1)
            act.wait_ge(c_heads, 1)
            act.wait_ge(kT_sb, 1)
            KBv = KB[:, :, :].rearrange("p b (h k) -> p b h k", h=NH)
            for h in range(NH):
                ins = nc.scalar.activation(KBv[:, :, h, :], KT[:, :].rearrange("p (b k) -> p b k", b=BT), ACT.Copy, scale=HM[:, h:h + 1])
            ins.then_inc(kb_ok, 1)

            groups = [(0, 4), (4, 8), (8, NC)]

            def exps(t, par, part):
                c0, c1 = (0, 12 * KL) if part == 0 else (12 * KL, HK)
                act.wait_ge(sc_sub, 2 * t + 1 + part)
                nc.scalar.activation(PR[:, par, c0:c1], PR[:, par, c0:c1], ACT.Exp).then_inc(exp_ok, 1)

            def weights_T(t, g):
                c0, c1 = groups[g]
                act.wait_ge(pT_ps, 3 * t + g + 1)
                if g == 0:
                    wait(act, pv_ps, t)
                rows = P if g < 2 else CR[NC - 1]
                copy(PT[:, c0:NC - 1 if g == 2 else c1, :],
                     PS[:, 6, 0:((NC - 1 if g == 2 else c1) - c0) * P].rearrange("p (c k) -> p c k", k=P)
                     ).then_inc(pT_sb, 1)
                if g == 2:
                    copy(PT[0:rows, NC - 1, :], PS[0:rows, 6, (NC - 1 - c0) * P:(NC - c0) * P]).then_inc(pT_sb, 1)

            def out_T(t):
                act.wait_ge(oT_ps, t + 1)
                copy(OT[:, :], PS[:, 7, 256:384]).then_inc(oT_sb, 1)

            for part in range(2):
                exps(0, 0, part)
            act.wait_ge(dpre, 16 * 2 * RW)
            act.wait_ge(rpre, 16 * 2 * RW)

            def attend(b):
                for q in range(Q):
                    t = b * Q + q
                    first, final = isinstance(t, int) and t == 0, isinstance(t, int) and t == NT - 1
                    weights_T(t, 0)
                    if not first:
                        out_T(t - 1)
                    weights_T(t, 1)
                    if not final:
                        exps(t + 1, (q + 1) % 2, 0)
                    weights_T(t, 2)
                    if not final:
                        exps(t + 1, (q + 1) % 2, 1)

            peeled(act, BT, attend)
            out_T(NT - 1)

            std_of(x1_ok, NT)
            act.wait_ge(xT_ps, BT + 1)
            copy_xT(BT)

            def ffn(b):
                for c in range(FC):
                    act.wait_ge(g_ps, FC * b + c + 1)
                    wait(act, h_ok, FC * (b - 1) + c + 1)
                    nc.scalar.activation(HS[:, c, :], PS[:, 1 + 2 * c, :], ACT.Silu, scale=DQ).then_inc(silu_ok, 1)
                if not (isinstance(b, int) and b == BT - 1):
                    act.wait_ge(u_ps, FC * (b + 1))
                    copy_xT(BT + b + 1)

            peeled(act, BT, ffn)

            std_of(x2_ok, BT)

            def squares(b):
                wait(act, d_ps, b)
                copy_xT(2 * BT + b)
                nc.scalar.activation(XSQ[:, :], PS[:, 0, :], ACT.Square).then_inc(xsq_ok, 1)

            def roots(b):
                act.wait_ge(d_pos, b + 1)
                nc.scalar.activation(DSB[:, b, :], DSQ[:, b, :], ACT.Sqrt).then_inc(d_ok, 1)

            squares(0)
            with act.Fori(0, BT - 1) as b:
                squares(b + 1)
                roots(b)
            roots(BT - 1)

            act.wait_ge(sc_ps, 3 * NT)
            act.dma_start(W13[:, :, :].rearrange("p e n -> p (e n)"), w13T).then_inc(ld_moe, 16)
            act.dma_start(W2[:, :, :], w2T.rearrange("(c p) d -> p c d", p=P)).then_inc(ld_moe, 16)
            act.wait_ge(ld_moe, 32)
            for e in range(NE):
                copy(W13H[:, e, :], W13[:, e, :]).then_inc(w_hi, 1)

            std_of(x3_ok, BT)

            def router(b):
                wait(act, lg_ps, b)
                wait(act, xt4_ok, b)
                copy_xT(3 * BT + b)

            router(0)
            with act.Fori(1, BT) as b:
                router(b)
            act.wait_ge(xt4_ok, BT)
            act.wait_ge(rsub_ok, 1)
            nc.scalar.activation(RC[:, :, :, :], RC[:, :, :, :], ACT.Exp).then_inc(rexp_ok, 1)

            def inputs(b):
                wait(act, eu_ps, EC * NE * b)
                copy(XTH[:, :], XT4[:, b * Q * P:(b + 1) * Q * P] if isinstance(b, int) else XT4[:, bass.ds(b * Q * P, Q * P)]
                     ).then_inc(xth_ok, 1)

            def experts(b):
                for e in range(NE):
                    for c in range(EC):
                        n = NE * b + e
                        m = EC * n + c
                        act.wait_ge(eg_ps, m + 1)
                        wait(act, ac_ok, m - 1)
                        nc.scalar.activation(SI[:, c, :], PS[:, 2 * c, :], ACT.Silu).then_inc(si_ok, 1)

            inputs(0)
            experts(0)
            with act.Fori(1, BT) as b:
                inputs(b)
                experts(b)

        @block.vector
        def _(dve):
            step = Steps(dve, v_step)
            V = nc.vector

            def stats(src, dst):
                for q in range(Q):
                    ins = V.bn_stats(bst[:, q, :], src[:, q, :])
                step.link(ins)
                for q in range(Q):
                    ins = V.bn_aggr(dst[:, q, :], bst[:, q, :])
                return ins

            def rstd_of(run):
                dve.wait_ge(std_ok, run)
                step.link(V.reciprocal(rstd[:, :], std[:, :]))

            def normalise(r, b):
                wait(dve, xT_ps, r)
                for q in range(Q):
                    t = b * Q + q
                    ins = V.tensor_scalar(XN[:, q, :], X[:, t, :], mv[:, t, 0:1], rstd[:, t:t + 1] if isinstance(t, int)
                                          else rstd[:, bass.ds(t, 1)], ALU.subtract, ALU.mult)
                ins.then_inc(xn_ok, 1)

            for b in range(BT):
                dve.wait_ge(ld_x, 16 * BT)
                ins = stats(X[:, b * Q:(b + 1) * Q, :], mv[:, b * Q:(b + 1) * Q, :])
                if b < BT - 1:
                    step.link(ins)
            ins.then_inc(var_ok, 1)
            rstd_of(1)
            dve.wait_ge(ld_q, 32)

            def keys():
                dve.wait_ge(ld_k, 16 * 7)
                dve.wait_ge(k_ps, 1)
                step.link(V.tensor_tensor(KQ[:, :].rearrange("k (b d) -> k b d", b=BT),
                                          PS[0:KL, 2, :].rearrange("k (b d) -> k b d", b=BT),
                                          bc(BK[0:KL, :].unsqueeze(1), [KL, BT, D]), ALU.add))
                step.link(V.tensor_tensor(KSQ[:, :], KQ[:, :], KQ[:, :], ALU.mult))
                V.tensor_reduce(kss[:, :], steps3(KSQ[:, :]), AX, ALU.add).then_inc(kss_ok, 1)
                step.link(V.tensor_scalar(qkw[:, :], kwb[:, :], SCALE, None, ALU.mult))
                step.link(V.tensor_tensor(qkw[:, :], qkw[:, :], qwb[:, :], ALU.mult))

            def keys_normalised():
                dve.wait_ge(kst_ok, 1)
                step.link(V.reciprocal(krs[:, :], krs[:, :]))
                step.link(V.tensor_tensor(steps3(KQ[:, :]), steps3(KQ[:, :]), bc(krs[:, :].unsqueeze(2), [KL, BT * NH, HD]), ALU.mult))
                V.tensor_tensor(steps3(KQ[:, :]), steps3(KQ[:, :]), bc(qkw[0:KL, :].unsqueeze(1), [KL, BT * NH, HD]),
                                ALU.mult).then_inc(kn_ok, 1)

            def project(b):
                dve.wait_ge(q_ps, b + 1)
                V.tensor_tensor(Qs[:, b * Q * D:(b + 1) * Q * D].rearrange("p (q d) -> p q d", q=Q),
                                PS[:, 1, :].rearrange("p (q d) -> p q d", q=Q),
                                bc(BQ[:, :].unsqueeze(1), [P, Q, D]), ALU.add).then_inc(q_sb, 1)

            def squares_of(b):
                dve.wait_ge(qsq_ok, b + 1)
                V.tensor_reduce(qss[:, b * Q * NH:(b + 1) * Q * NH], steps3(SQ[:, b * Q * D:(b + 1) * Q * D]), AX, ALU.add).then_inc(qss_ok, 1)

            def scale_q(b):
                dve.wait_ge(qst_ok, b + 1)
                c0, c1 = b * Q * NH, (b + 1) * Q * NH
                step.link(V.reciprocal(qrs[:, c0:c1], qrs[:, c0:c1]))
                wait(dve, qT_ps, b)
                V.tensor_tensor(QN[:, :, :].rearrange("p q (h d) -> p (q h) d", d=HD), steps3(Qs[:, b * Q * D:(b + 1) * Q * D]),
                                bc(qrs[:, c0:c1].unsqueeze(2), [P, Q * NH, HD]), ALU.mult).then_inc(qn_ok, 1)

            for b in range(BT + 1):
                if b < BT:
                    normalise(b, b)
                if b == 0:
                    keys()
                if b > 0:
                    squares_of(b - 1)
                if b < BT:
                    project(b)
                if b > 0:
                    scale_q(b - 1)
                if b == 1:
                    keys_normalised()
                    dve.wait_ge(bo_ps, 1)
                    V.tensor_tensor(BIASO[:, :], PS[:, 7, 256:256 + D], BO[:, :], ALU.add).then_inc(bo_ok, 1)
            dve.wait_ge(ld_mask, 16)
            V.tensor_single_scalar(mz[:, :, :], mi[:, :, :], 0.0, ALU.is_equal).then_inc(mask_ok, 1)
            dve.wait_ge(mask_ok, 1)
            V.tensor_scalar(mrow[0:1, :, :], mz[0:1, :, :], -BIG, None, ALU.mult).then_inc(mask_ok, 1)
            dve.wait_ge(mask_ok, 2)
            step.link(V.tensor_scalar(mz[:, :, :], mz[:, :, :], -1.0, 1.0, ALU.mult, ALU.add))
            dve.wait_ge(c_heads, 1)
            for b in range(BT):
                dve.wait_ge(v_ps, b + 1)
                ins = V.tensor_tensor(VX[:, b, :, 0:HD], PS[:, 4 + b, 0:NC * 3 * HD].rearrange("p (m d) -> p m d", d=HD),
                                      bc(HMC[:, :].unsqueeze(2), [P, NC * 3, HD]), ALU.mult)
            ins.then_inc(vx_ok, 1)
            step.link(V.tensor_reduce(cnt[:, :], mz[:, :, :], AX, ALU.add))
            step.link(V.reciprocal(nanf[:, :], cnt[:, :]))
            step.link(V.tensor_scalar(nanf[:, :], nanf[:, :], 0.0, None, ALU.mult))

            def heads(t, par, h0, h1, bank, nb):
                n = (h1 - h0) // nb
                src = PS[:, 3 * par + bank:3 * par + bank + nb, 0:n * KL].rearrange("p a (h k) -> p a h k", k=KL)
                top = mx[:, h0:h1].rearrange("p (a h) -> p a h", a=nb)
                step.link(V.tensor_reduce(top, src, AX, ALU.max))
                V.tensor_tensor(PR[:, par, h0 * KL:h1 * KL].rearrange("p (a h k) -> p a h k", a=nb, k=KL), src,
                                bc(top.unsqueeze(3), [P, nb, n, KL]), ALU.subtract).then_inc(sc_sub, 1)

            def centre(t, par, part):
                dve.wait_ge(sc_ps, 3 * t + 2 + part)
                if part == 0:
                    wait(dve, pT_ps, 3 * (t - 1))
                    heads(t, par, 0, 12, 0, 2)
                else:
                    heads(t, par, 12, 16, 2, 1)

            def residual(t, b, q):
                dve.wait_ge(wo_ps, t + 1)
                wait(dve, x1_ok, t - Q + 1)
                V.scalar_tensor_tensor(XS[:, q, :], PS[:, 7, 384:512], nanf[:, b:b + 1] if isinstance(b, int) else nanf[:, bass.ds(b, 1)],
                                       X[:, t, :], ALU.add, ALU.add).then_inc(xs_ok, 1)
                dve.wait_ge(xs_ok, t + 1)
                step.link(V.bn_stats(bst[:, 0, :], XS[:, q, :]))
                V.bn_aggr(mvs[:, q, :], bst[:, 0, :]).then_inc(mvs_ok, 1)

            centre(0, 0, 0)
            centre(0, 0, 1)
            dve.wait_ge(bo_add, BT)

            def attend(b):
                for q in range(Q):
                    t = b * Q + q
                    first, final = isinstance(t, int) and t == 0, isinstance(t, int) and t == NT - 1
                    if not final:
                        centre(t + 1, (q + 1) % 2, 0)
                    if not first:
                        residual(t - 1, b if q else b - 1, (q - 1) % Q)
                    if not final:
                        centre(t + 1, (q + 1) % 2, 1)
                    dve.wait_ge(pv_ps, t + 1)
                    O = PS[:, 7, 0:NH * VW].rearrange("p (h w) -> p h w", w=VW)
                    step.link(V.reciprocal(rcp[:, :], O[:, :, HD]))
                    V.tensor_tensor(ON[:, :].rearrange("p (h d) -> p h d", d=HD), O[:, :, 0:HD],
                                    bc(rcp[:, :].unsqueeze(2), [P, NH, HD]), ALU.mult).then_inc(on_ok, 1)

            peeled(dve, BT, attend, step)
            residual(NT - 1, BT - 1, Q - 1)

            rstd_of(2)
            normalise(BT, 0)
            dve.wait_ge(wf_ok, 1)
            dve.wait_ge(x1_ok, NT)

            def ffn(b):
                if not (isinstance(b, int) and b == BT - 1):
                    normalise(BT + b + 1, b + 1)
                for c in range(FC):
                    dve.wait_ge(u_ps, FC * b + c + 1)
                    dve.wait_ge(silu_ok, FC * b + c + 1)
                    wait(dve, dn_ps, b)
                    V.scalar_tensor_tensor(HT[:, c, :], PS[:, 2 + 2 * c, :], DQ, HS[:, c, :], ALU.mult, ALU.mult).then_inc(h_ok, 1)
                dve.wait_ge(dn_ps, b + 1)
                wait(dve, x2_ok, b)
                V.scalar_tensor_tensor(XS[:, :, :].rearrange("p q d -> p (q d)"), PS[:, 7, :], DQ,
                                       X[:, bass.ds(b * Q, Q), :].rearrange("p q d -> p (q d)"), ALU.mult, ALU.add).then_inc(xs_ok, 1)
                dve.wait_ge(xs_ok, NT + b + 1)
                stats(XS, mvs).then_inc(mvs_ok, 1)

            peeled(dve, BT, ffn, step)

            step.link(V.tensor_tensor(CSQ[:, :], CK[:, :, :].rearrange("k b d -> k (b d)"), CK[:, :, :].rearrange("k b d -> k (b d)"), ALU.mult))
            step.link(V.tensor_reduce(aa[:, :], CSQ[:, :].rearrange("k (b d) -> k b d", b=BT), AX, ALU.add))
            rstd_of(3)
            normalise(2 * BT, 0)

            def clamp(b):
                dve.wait_ge(d_ps, b + 1)
                V.tensor_scalar(DSQ[:, b, :], PS[0:KR, 1 + b, :], aa[:, b:b + 1] if isinstance(b, int) else aa[:, bass.ds(b, 1)],
                                0.0, ALU.add, ALU.max).then_inc(d_pos, 1)

            with dve.Fori(0, BT - 1) as b:
                normalise(2 * BT + b + 1, b + 1)
                clamp(b)
            clamp(BT - 1)

            down = [31] + list(range(31))

            def wave(k, par, go_on=True):
                at = k * CB
                for r in range(RW):
                    step.link(V.tensor_tensor(MM[:, r, :], WS[:, par, r, at:at + CB], WS[:, par, r, at + 1:at + 1 + CB], ALU.min))
                    ins = V.tensor_tensor_scan(WS[:, par, r + 1, at + 1:at + 1 + CB], MM[:, r, :], DP[:, par, r, at:at + CB],
                                               WS[:, par, r + 1, at:at + 1], ALU.min, ALU.add)
                    if go_on or r < RW - 1:
                        step.link(ins)
                if not go_on:
                    ins.then_inc(r_ok, 1)
                    return
                if k == WN - 1:
                    V.tensor_copy(WS[:, 1 - par, :, 0:1], WS[:, par, :, at + CB:at + CB + 1]).then_inc(r_ok, 1)
                    step.link(V.stream_shuffle(WS[:, 1 - par, 0, 1:1 + CB], WS[:, par, RW, at + 1:at + 1 + CB], down))
                else:
                    step.link(V.stream_shuffle(WS[:, par, 0, at + CB + 1:at + 2 * CB + 1], WS[:, par, RW, at + 1:at + 1 + CB], down))

            def two_windows(v):
                for par in range(2):
                    w = v * 2 + par
                    dve.wait_ge(dld, w * 16 + 16)
                    wait(dve, rst, (w - 1) * 16)
                    for k in range(WN):
                        wave(k, par)

            pairs = NS // (2 * WN)
            two_windows(0)
            with dve.Fori(1, pairs) as v:
                step.restart()
                two_windows(v)
            dve.wait_ge(dld, 16 * NWIN)
            dve.wait_ge(rst, 16 * (NWIN - 2))
            assert NS - 2 * WN * pairs == 1
            wave(0, 0, False)

            dve.wait_ge(rld, 16 * 2 * BT)
            dve.wait_ge(ui_ok, 2)
            dg, up, lf = UI[0:KR, :, 0:SL], UI[0:KR, :, 1:SL + 1], RI[:, :, 0:SL]
            step.link(V.tensor_tensor(T1[:, :, :], dg, up, ALU.min))
            step.link(V.tensor_tensor(T2[:, :, :], lf, T1[:, :, :], ALU.is_ge))
            step.link(V.tensor_tensor(T1[:, :, :], dg, up, ALU.is_le))
            step.link(V.scalar_tensor_tensor(T1[:, :, :], T1[:, :, :], -0.5, JG[:, :, :], ALU.mult, ALU.add))
            step.link(V.tensor_tensor(T1[:, :, :], T1[:, :, :], T2[:, :, :], ALU.mult))
            v2 = T1[:, :, :].rearrange("k b j -> k (b j)")
            V.tensor_tensor_scan(FX[:, :], v2, v2, -1.0, ALU.max, ALU.max).then_inc(f_ok, 1)
            per = 6
            for g in range(3):
                c0, n = g * per, min(per, CC - g * per)
                dve.wait_ge(fT_ps, g + 1)
                ins = V.tensor_scalar(FT[:, :, c0:c0 + n].rearrange("p k c -> p c k"),
                                      PS[:, g, 0:n * 85].rearrange("p (c k) -> p c k", k=85)[:, :, 0:KR],
                                      goff[:, :], None, ALU.subtract)
            step.link(ins)

            def look(i, came, par):
                V.scalar_tensor_tensor(hit[:, :, :], JH[:, :, :], came, bc(FT[:, i, :].unsqueeze(2), [P, CC, 2]),
                                       ALU.is_equal, ALU.mult, accum_out=hs[:, par:par + 1]).then_inc(hit_ok, 1)

            with nc.allow_low_precision(reason="columns are multiples of one half below 1024, exact in float16"):
                look(KL - 1, last[:, :], 0)
                for i in range(KL - 2, -1, -1):
                    dve.wait_ge(b_ps, KL - 1 - i)
                    look(i, PS[:, 5, i + 1:i + 2], (KL - 1 - i) % 2)
            dve.wait_ge(b_ps, KL)
            V.memset(BS[:, KL:KR], float(SL - 1))
            V.tensor_copy(BS[:, 0:KL], PS[:, 5, 0:KL]).then_inc(bs_ok, 1)
            dve.wait_ge(bT_ps, 1)
            step.link(V.tensor_copy(lohi[0:KL, :, :],
                                    PS[0:KL, 6, 0:2 * P].rearrange("k (a b c) -> k a b c", a=2, b=BT)[:, :, :, 0]))
            jr = JG[0:KL, 0, :]

            def on_path(b):
                step.link(V.tensor_scalar(PA[0:KL, :], jr, lohi[0:KL, 0, bass.ds(b, 1)], None, ALU.is_ge))
                wait(dve, e_ps, b)
                V.scalar_tensor_tensor(PM[0:KL, :], jr, lohi[0:KL, 1, bass.ds(b, 1)], PA[0:KL, :], ALU.is_le, ALU.mult).then_inc(pm_ok, 1)
                dve.wait_ge(e_ps, b + 1)
                wait(dve, x3_ok, b)
                V.tensor_tensor(XS[:, :, :].rearrange("p q d -> p (q d)"), PS[:, 1, :],
                                X[:, bass.ds(b * Q, Q), :].rearrange("p q d -> p (q d)"), ALU.add).then_inc(xs_ok, 1)
                dve.wait_ge(xs_ok, NT + BT + b + 1)
                stats(XS, mvs).then_inc(mvs_ok, 1)

            peeled(dve, BT, on_path, step)
            rstd_of(4)
            normalise(3 * BT, 0)

            def logits(b):
                dve.wait_ge(lg_ps, b + 1)
                V.tensor_copy(LG[:, bass.ds(b * Q, Q), :].rearrange("p q e -> p (q e)"), PS[:, 2, 0:Q * NE]).then_inc(lg_ok, 1)

            with dve.Fori(0, BT - 1) as b:
                normalise(3 * BT + b + 1, b + 1)
                logits(b)
            logits(BT - 1)
            dve.wait_ge(lg_ok, BT)

            for t in range(NT):
                ins = V.max(M8[:, t, :], LG[:, t, :])
            step.link(ins)
            for t in range(NT):
                ins = V.max_index(I8[:, t, :], M8[:, t, :], LG[:, t, :])
            step.link(ins)
            step.link(V.tensor_copy(IF8[:, :, :], I8[:, :, 0:2]))
            for j in range(2):
                top = bc(M8[:, :, j:j + 1], [P, NT, NE])
                step.link(V.tensor_tensor(OH[:, j, :, :], JE[:, :, :], bc(IF8[:, :, j:j + 1], [P, NT, NE]), ALU.is_equal))
                step.link(V.tensor_scalar(RA[:, :, :], LG[:, :, :], -1.0, None, ALU.mult))
                step.link(V.tensor_tensor(RA[:, :, :], RA[:, :, :], LG[:, :, :], ALU.max))
                step.link(V.tensor_tensor(RA[:, :, :], RA[:, :, :], top, ALU.max))
                step.link(V.tensor_tensor(RB[:, :, :], top, LG[:, :, :], ALU.subtract))
                step.link(V.scalar_tensor_tensor(RA[:, :, :].rearrange("p t e -> p (t e)"), RA[:, :, :].rearrange("p t e -> p (t e)"), 0.02,
                                                 RB[:, :, :].rearrange("p t e -> p (t e)"), ALU.mult, ALU.is_ge))
                if j == 1:
                    step.link(V.tensor_tensor(RB[:, :, :], OH[:, 0, :, :], RA[:, :, :], ALU.mult))
                    step.link(V.tensor_tensor(RA[:, :, :], RA[:, :, :], RB[:, :, :], ALU.subtract))
                    step.link(V.tensor_tensor(RB[:, :, :], LG[:, :, :], top, ALU.subtract))
                    step.link(V.tensor_scalar(RC[:, j, :, :], RB[:, :, :], 0.0, None, ALU.min))
                    step.link(V.tensor_copy(KEEP[:, 0, :], RA[:, :, :].rearrange("p t e -> p (t e)")))
                else:
                    step.link(V.tensor_scalar(RC[:, j, :, :], RB[:, :, :], -1.0, None, ALU.mult))
                    step.link(V.tensor_copy(KEEP[:, 1, :], RA[:, :, :].rearrange("p t e -> p (t e)")))
            V.tensor_copy(rstd[:, :], std[:, :]).then_inc(rsub_ok, 1)
            dve.wait_ge(rexp_ok, 1)
            for j in range(2):
                keep = KEEP[:, 1 - j, :].rearrange("p (t e) -> p t e", e=NE)
                step.link(V.tensor_tensor(RC[:, j, :, :], RC[:, j, :, :], keep, ALU.mult))
                step.link(V.tensor_reduce(ZS[:, j, :], RC[:, j, :, :], AX, ALU.add))
            step.link(V.reciprocal(ZS[:, :, :], ZS[:, :, :]))
            for j in range(2):
                step.link(V.tensor_tensor(OH[:, j, :, :], OH[:, j, :, :], bc(ZS[:, j, :].unsqueeze(2), [P, NT, NE]), ALU.mult))
            step.link(V.tensor_tensor(GWT[:, :, :], OH[:, 0, :, :], OH[:, 1, :, :], ALU.add))

            def add_out(n, b, e):
                dve.wait_ge(y_ps, n + 1)
                wait(dve, y_ok, n)
                for q in range(Q):
                    t = b * Q + q
                    ins = V.scalar_tensor_tensor(X[:, t, :], PS[:, 4 + e % 2, q * D:(q + 1) * D], GWT[:, t, e:e + 1], X[:, t, :],
                                                 ALU.mult, ALU.add)
                ins.then_inc(y_ok, 1)

            def experts(b):
                for e in range(NE):
                    n = NE * b + e
                    for c in range(EC):
                        m = EC * n + c
                        dve.wait_ge(eu_ps, m + 1)
                        dve.wait_ge(si_ok, m + 1)
                        wait(dve, y_ps, n - 1)
                        V.tensor_tensor(HA[:, e % 2 * EC + c, :], PS[:, 2 * c + 1, :], SI[:, c, :], ALU.mult).then_inc(ac_ok, 1)
                    if not (isinstance(n, int) and n == 0):
                        add_out(n - 1, b if e else b - 1, (e - 1) % NE)

            dve.wait_ge(w_lo, NE)
            experts(0)
            with dve.Fori(1, BT) as b:
                experts(b)
            add_out(NE * BT - 1, BT - 1, NE - 1)

        @block.tensor
        def _(pe):
            def mm(o, l, r, start=True, stop=True, **kw):
                return nc.tensor.matmul(o, l, r, start=start, stop=stop, **kw)

            pe.wait_ge(c_ident, 1)

            def x_T(r):
                pe.wait_ge(xn_ok, r + 1)
                for q in range(Q):
                    ins = nc.tensor.transpose(PS[:, 0, q * P:(q + 1) * P], XN[:, q, :], ident[:, :])
                ins.then_inc(xT_ps, 1)

            def queries(b):
                wait(pe, xT_sb, b)
                x_T(b)
                pe.wait_ge(xT_sb, b + 1)
                wait(pe, q_sb, b)
                for q in range(Q):
                    ins = mm(PS[:, 1, q * P:(q + 1) * P], XNT[:, q * P:(q + 1) * P], WQ[:, :])
                ins.then_inc(q_ps, 1)

            def queries_T(b):
                wait(pe, qT_sb, b)
                pe.wait_ge(qn_ok, b + 1)
                for q in range(Q):
                    ins = nc.tensor.transpose(PS[:, 3, q * P:(q + 1) * P], QN[:, q, :], ident[:, :])
                ins.then_inc(qT_ps, 1)

            def values(b):
                for c in range(NC):
                    s = c * P % KL
                    ins = mm(PS[:, 4 + b, c * 3 * HD:(c + 1) * 3 * HD], CT3[:, b, s:s + P],
                             WV[:, H0[c] * HD:(H0[c] + 3) * HD])
                ins.then_inc(v_ps, 1)

            pe.wait_ge(ld_q, 32)
            pe.wait_ge(ld_k, 16 * 7)
            for b in range(BT):
                ins = mm(PS[0:KL, 2, b * D:(b + 1) * D], CT3[:, b, 0:KL], WK[:, :])
            ins.then_inc(k_ps, 1)
            for b in range(BT + 1):
                if b < BT:
                    queries(b)
                if b == 2:
                    pe.wait_ge(kn_ok, 1)
                    for c in range(BT):
                        ins = nc.tensor.transpose(PS[:, 2, c * KL:(c + 1) * KL], KQ[:, c * D:(c + 1) * D], ident[0:KL, 0:KL])
                    ins.then_inc(kT_ps, 1)
                if b > 0:
                    queries_T(b - 1)
                if b == 0:
                    pe.wait_ge(ld_v, 16 * 6)
                    pe.wait_ge(bvt_ok, 1)
                    mm(PS[:, 7, 256:256 + D], BVT[:, :], WO[:, :]).then_inc(bo_ps, 1)
                if b > 0:
                    if b == BT:
                        pe.wait_ge(bo_ok, 1)
                    values(b - 1)
            pe.wait_ge(kb_ok, 1)
            pe.wait_ge(vx_ok, 1)
            pe.wait_ge(bo_ok, 1)
            pe.wait_ge(mask_ok, 2)
            pe.wait_ge(qT_sb, BT)
            pe.wait_ge(kT_sb, 1)

            def scores(t, b, par, bank):
                h0, h1 = HB[bank]
                n = (h1 - h0) * KL
                o = PS[:, 3 * par + bank, 0:n]
                if bank == 0:
                    pe.wait_ge(qTb_ok, t + 1)
                    wait(pe, sc_sub, 2 * (t - 1))
                mm(o, QTb[:, par, :], KB[:, b, h0 * KL:h1 * KL], stop=False)
                mm(o.rearrange("p (h k) -> p h k", k=KL), ones_b[:, :], bc(mrow[0:1, b, :].unsqueeze(1), [1, h1 - h0, KL]), start=False).then_inc(sc_ps, 1)

            def weights_T(t, par, g):
                if g < 2:
                    pe.wait_ge(exp_ok, 2 * t + 1 + g)
                wait(pe, pT_sb, 4 * t + g)
                for c in range(4 * g, min(4 * g + 4, NC)):
                    ins = nc.tensor.transpose(PS[0:CR[c], 6, (c - 4 * g) * P:(c - 4 * g + 1) * P],
                                              PR[:, par, c * P:c * P + CR[c]], ident[:, :])
                ins.then_inc(pT_ps, 1)

            def out_T(t):
                pe.wait_ge(on_ok, t + 1)
                nc.tensor.transpose(PS[:, 7, 256:384], ON[:, :], ident[:, :]).then_inc(oT_ps, 1)

            def out_proj(t):
                pe.wait_ge(oT_sb, t + 1)
                mm(PS[:, 7, 384:512], OT[:, :], WO[:, :]).then_inc(wo_ps, 1)

            for t in range(2):
                for bank in range(3):
                    scores(t, 0, t, bank)

            def attend(b):
                for q in range(Q):
                    t, par = b * Q + q, q % 2
                    first = isinstance(t, int) and t == 0
                    for g in range(3):
                        weights_T(t, par, g)
                        if not first and g == 0:
                            out_T(t - 1)
                        if not (isinstance(t, int) and t >= NT - 2):
                            scores(t + 2, b if q < Q - 2 else b + 1, par, g)
                        if not first and g == 0:
                            out_proj(t - 1)
                    pe.wait_ge(pT_sb, 4 * t + 4)
                    wait(pe, xs_ok, t)
                    for c in range(NC):
                        ins = mm(PS[:, 7, H0[c] * VW:(H0[c] + 3) * VW], PT[0:CR[c], c, :],
                                 VX[0:CR[c], b, 3 * c:3 * c + 3, :].rearrange("p m w -> p (m w)"),
                                 start=c == 0, stop=c == NC - 1, skip_group_check=True)
                    ins.then_inc(pv_ps, 1)

            peeled(pe, BT, attend)
            out_T(NT - 1)
            out_proj(NT - 1)

            pe.wait_ge(wf_ok, 1)
            pe.wait_ge(xs_ok, NT)
            x_T(BT)

            def ffn(b):
                for c in range(FC):
                    if c == 0:
                        pe.wait_ge(xT_sb, BT + b + 1)
                    wait(pe, h_ok, FC * (b - 1) + c + 1)
                    mm(PS[:, 1 + 2 * c, :], WG[:, c * P:(c + 1) * P], XNT[:, :]).then_inc(g_ps, 1)
                    mm(PS[:, 2 + 2 * c, :], WU[:, c * P:(c + 1) * P], XNT[:, :]).then_inc(u_ps, 1)
                if not (isinstance(b, int) and b == BT - 1):
                    x_T(BT + b + 1)
                pe.wait_ge(h_ok, FC * (b + 1))
                pe.wait_ge(xs_ok, NT + b)
                for q in range(Q):
                    for c in range(FC):
                        ins = mm(PS[:, 7, q * D:(q + 1) * D], HT[:, c, q * P:(q + 1) * P], WD2[:, c, :],
                                 start=c == 0, stop=c == FC - 1)
                ins.then_inc(dn_ps, 1)

            peeled(pe, BT, ffn)

            pe.wait_ge(cn_ok, 1)
            pe.wait_ge(xs_ok, NT + BT)
            x_T(2 * BT)

            def distances(b, more):
                pe.wait_ge(xT_sb, 2 * BT + b + 1)
                pe.wait_ge(xsq_ok, b + 1)
                if more:
                    x_T(2 * BT + b + 1)
                o = PS[0:KR, 1 + b, :]
                return o

            for b in range(BT):
                o = distances(b, b < BT - 1)
                mm(o, CN2[:, b, :], XNT[:, :], stop=False)
                mm(o, ones_f[:, 0:KR], XSQ[:, :], start=False).then_inc(d_ps, 1)

            pe.wait_ge(d_pos, BT)
            pe.wait_ge(f_ok, 1)
            for c in range(CC):
                ins = nc.tensor.transpose(PS[:, c // 6, c % 6 * 85:c % 6 * 85 + KR], FX[:, c:BT * SL:CC], ident[0:KR, 0:KR])
                if c % 6 == 5 or c == CC - 1:
                    ins.then_inc(fT_ps, 1)

            pe.wait_ge(c_all, 2)
            for i in range(KL - 1, -1, -1):
                pe.wait_ge(hit_ok, KL - i)
                mm(PS[:, 5, i:i + 1], blk1[:, :], hs[:, (KL - 1 - i) % 2:(KL - 1 - i) % 2 + 1]).then_inc(b_ps, 1)
            pe.wait_ge(bs_ok, 1)
            for j in range(2):
                ins = nc.tensor.transpose(PS[0:KL, 6, j * P:(j + 1) * P], BS[:, j:j + KL], ident[:, :])
            ins.then_inc(bT_ps, 1)

            def aligned(b):
                pe.wait_ge(pm_ok, b + 1)
                pe.wait_ge(xs_ok, NT + BT + b)
                for q in range(Q):
                    ins = mm(PS[:, 1, q * D:(q + 1) * D], PM[0:KL, q * P:(q + 1) * P], CK[0:KL, b, :])
                ins.then_inc(e_ps, 1)

            aligned(0)
            with pe.Fori(1, BT) as b:
                aligned(b)

            def router(b):
                wait(pe, xT_sb, 3 * BT + b)
                x_T(3 * BT + b)
                pe.wait_ge(xT_sb, 3 * BT + b + 1)
                wait(pe, lg_ok, b)
                for q in range(Q):
                    ins = mm(PS[:, 2, q * NE:(q + 1) * NE], XNT[:, q * P:(q + 1) * P], GW[:, :])
                ins.then_inc(lg_ps, 1)

            pe.wait_ge(ld_gate, 16)
            with pe.Fori(0, BT) as b:
                router(b)

            pe.wait_ge(lg_ok, BT)
            pe.wait_ge(xs_ok, NT + 2 * BT)
            pe.wait_ge(w_lo, NE)
            pe.wait_ge(ld_moe, 32)

            def first(m, b, e, c):
                wait(pe, ac_ok, m - 1)
                xh, xl = XTH[:, :], XTL[:, :]
                for j, done in ((0, eg_ps), (1, eu_ps)):
                    c0 = j * EI + c * P
                    o = PS[:, 2 * c + j, :]
                    mm(o, W13H[:, e, c0:c0 + P], xh, stop=False)
                    mm(o, W13H[:, e, c0:c0 + P], xl, start=False, stop=False)
                    mm(o, W13L[:, e, c0:c0 + P], xh, start=False).then_inc(done, 1)

            def second(n, e):
                pe.wait_ge(ac_ok, EC * n + EC)
                wait(pe, y_ok, n - 1)
                for q in range(Q):
                    for c in range(EC):
                        ins = mm(PS[:, 4 + e % 2, q * D:(q + 1) * D], HA[:, e % 2 * EC + c, q * P:(q + 1) * P], W2[:, EC * e + c, :],
                                 start=c == 0, stop=c == EC - 1)
                ins.then_inc(y_ps, 1)

            def experts(b):
                pe.wait_ge(xtl_ok, b + 1)
                for e in range(NE):
                    n = NE * b + e
                    for c in range(EC):
                        first(EC * n + c, b, e, c)
                    if not (isinstance(n, int) and n == 0):
                        second(n - 1, (e - 1) % NE)

            experts(0)
            with pe.Fori(1, BT) as b:
                experts(b)
            second(NE * BT - 1, NE - 1)


_OUTS = [((4, 512, 128), "float32")]


def kernel(**inputs):
    import numpy as _np
    import concourse.bacc as _bacc
    from concourse import mybir as _mybir
    from concourse.bass_utils import run_bass_kernel_spmd as _run

    g = {k: _np.asarray(v) for k, v in inputs.items()}
    ctx = g["ctx_1024"]
    w1, w3, w2 = g["L1_ffn_w1"], g["L1_ffn_w3"], g["L1_ffn_w2"]
    ne, ei, d = w1.shape
    w13 = _np.stack([w1, w3], axis=1).transpose(3, 0, 1, 2).reshape(d, ne * 2 * ei)
    named = [
        ("x", g["x"]), ("ctx_dt", ctx.transpose(2, 0, 1).reshape(d, -1)), ("ctx_kd", ctx),
        ("mask", g["mask_BxS2_ik0"]),
        ("wqT", g["L0_xattn_Wq"].T), ("bq", g["L0_xattn_bq"]), ("wkT", g["L0_xattn_Wk"].T), ("bk", g["L0_xattn_bk"]),
        ("wvT", g["L0_xattn_Wv"].T), ("bv", g["L0_xattn_bv"]), ("woT", g["L0_xattn_Wo"].T), ("bo", g["L0_xattn_bo"]),
        ("qw", g["L0_xattn_q_norm_w"]), ("kw", g["L0_xattn_k_norm_w"]),
        ("wgT", g["L0_ffn_w_gate"].T), ("wuT", g["L0_ffn_w_up"].T), ("wdT", g["L0_ffn_w_down"].T),
        ("gateT", g["L1_ffn_gate_w"].T), ("w13T", w13), ("w2T", w2.transpose(0, 2, 1).reshape(ne * ei, d)),
    ]
    nc = _bacc.Bacc("TRN2", target_bir_lowering=False, num_devices=1)
    arrays, args = {}, []
    for name, a in named:
        a = _np.ascontiguousarray(a)
        arrays[f"in_{name}_dram"] = a
        args.append(nc.dram_tensor(f"in_{name}_dram", a.shape, _mybir.dt.from_np(a.dtype), kind="ExternalInput").ap())
    for i, (shape, dtype) in enumerate(_OUTS):
        dt = _mybir.dt.from_np(_np.dtype(dtype))
        args.append(nc.dram_tensor(f"out_{i}_dram", shape, dt, kind="ExternalOutput").ap())
    build(nc, *args)
    r = _run(nc, [arrays], core_ids=[0])
    return r.results[0]["out_0_dram"]
```

```python
from contextlib import ExitStack

import concourse.bass as bass
from concourse import mybir

F32 = mybir.dt.float32
F32R = mybir.dt.float32r
F16 = mybir.dt.float16
BF16 = mybir.dt.bfloat16
I32 = mybir.dt.int32
U32 = mybir.dt.uint32
ALU = mybir.AluOpType
ACT = mybir.ActivationFunctionType
AX = mybir.AxisListType.X

P = 128
BIG = 1.0e30
STAGE = "all"


class Steps:

    def __init__(self, eng, sem):
        self.eng, self.sem, self.n = eng, sem, 0

    def link(self, ins):
        ins.then_inc(self.sem, 1)
        self.n += 1
        self.eng.wait_ge(self.sem, self.n)

    def restart(self):
        self.eng.sem_clear(self.sem)
        self.n = 0


def peeled(eng, stop, body, count=None):
    body(0)
    with eng.Fori(1, stop - 1) as i:
        if count:
            count.restart()
        body(i)
    body(stop - 1)


def wait(eng, semaphore, value):
    if not isinstance(value, int) or value > 0:
        eng.wait_ge(semaphore, value)


def build(nc, x, ctx_dt, ctx_kd, mask, wqT, bq, wkT, bk, wvT, bv, woT, bo, qw, kw,
          wgT, wuT, wdT, gateT, w13T, w2T, out):
    BT, SL, D = x.shape[0], x.shape[1], x.shape[2]
    Q = SL // P
    NT = BT * Q
    KL = ctx_dt.shape[1] // BT
    HD = qw.shape[0]
    NH = D // HD
    SCALE = float(HD) ** -0.5
    HID = wgT.shape[1]
    FC = HID // P
    DQ = 1.0 / 127.0
    NE = gateT.shape[1]
    EI = w2T.shape[0] // NE
    EC = EI // P
    HK = NH * KL
    NC = -(-HK // P)
    HB = [(0, 6), (6, 12), (12, 16)]
    H0 = [min(c * P // KL, NH - 3) for c in range(NC)]
    CR = [min(P, HK - c * P) for c in range(NC)]
    VW = HD + 1

    RW = 3
    NI = -(-KL // RW)
    CB = 64
    NB = SL // CB
    NS = NB + NI - 1
    W = NS * CB
    WN = 4
    NWIN = -(-NS // WN)
    KR = NI * RW
    WD = CB + W
    JB = P // BT
    CC = SL // JB
    LN_EPS, Q_EPS = 1e-5, 1e-6
    HB2 = BT // 2

    ds = nc.dram_tensor("cost_skewed", (P, RW, WD), F32, kind="Internal").ap()
    rs = nc.dram_tensor("sums_skewed", (P, RW, WD), F32, kind="Internal").ap()

    with ExitStack() as ctx:
        def sb(name, shape, dt=F32):
            return ctx.enter_context(nc.sbuf_tensor(name, shape, dt))

        def sem(name):
            return ctx.enter_context(nc.semaphore(name))

        X = sb("X", [P, NT, D])
        XN = sb("XN", [P, 2, Q, D])
        XNT = sb("XNT", [P, 2, Q * P])
        space1 = sb("space1", [P, NT * D])
        space2 = sb("space2", [P, NT * D])
        space3 = sb("space3", [P, NT * P])
        space4 = sb("space4", [P, BT * HK])
        space5 = sb("space5", [P, 2 * HK])
        space6 = sb("space6", [P, NC * P])
        space7 = sb("space7", [P, 2 * FC * Q * P])
        space8 = sb("space8", [P, 2 * 3 * HID])

        def part(t, shape, at=0):
            n = 1
            for d in shape[1:]:
                n *= d
            v = t[0:shape[0], at:at + n]
            if len(shape) == 3:
                return v.rearrange("p (a b) -> p a b", a=shape[1])
            if len(shape) == 4:
                return v.rearrange("p (a b c) -> p a b c", a=shape[1], b=shape[2])
            return v

        Qs = part(space1, [P, NT * D])
        SQ = part(space2, [P, NT * D])
        QN = sb("QN", [P, Q, D])
        QT = part(space3, [P, NT, P])
        QTb = sb("QTb", [P, 2, P])
        qss = sb("qss", [P, NT * NH])
        qrs = sb("qrs", [P, NT * NH])
        KQ = part(space7, [KL, BT * D], SL * 2)
        CSQ = part(space7, [KR, BT * D], BT * SL)
        KSQ = CSQ[0:KL, :]
        kss = sb("kss", [KL, BT * NH])
        krs = sb("krs", [KL, BT * NH])
        KT = sb("KT", [P, BT * KL])
        KB = part(space4, [P, BT, HK])
        VX = sb("VX", [P, BT, NC * 3, VW])
        CT3 = part(space7, [P, BT, 3 * KL])
        CK = sb("CK", [KR, BT, D])
        WQ, WK, WV, WO = (sb(n, [P, D]) for n in ("WQ", "WK", "WV", "WO"))
        BQ, BK, BO, BIASO = (sb(n, [P, D]) for n in ("BQ", "BK", "BO", "BIASO"))
        bvc = sb("bvc", [P, 1])
        BVT = sb("BVT", [P, P])
        qwb = sb("qwb", [P, HD])
        kwb = sb("kwb", [P, HD])
        qkw = sb("qkw", [P, HD])
        mi = sb("mi", [P, BT, KL], I32)
        mz = sb("mz", [P, BT, KL])
        mrow = sb("mrow", [1, BT, KL], BF16)
        ones_b = sb("ones_b", [1, P], BF16)
        cnt = sb("cnt", [P, BT])
        nanf = sb("nanf", [P, BT])
        mx = sb("mx", [P, NH])
        PR = part(space5, [P, 2, HK])
        PT = part(space6, [P, NC, P])
        rcp = sb("rcp", [P, NH])
        ON = sb("ON", [P, D])
        OT = sb("OT", [P, P])
        bst = sb("bst", [P, Q, 6])
        mv = sb("mv", [P, NT, 2])
        XS = sb("XS", [P, Q, D])
        mvs = sb("mvs", [P, Q, 2])
        std = sb("std", [P, NT])
        shift = sb("shift", [P, NT])
        rstd = sb("rstd", [P, NT])
        epsl = sb("epsl", [P, 1])
        epsq = sb("epsq", [P, 1])
        wi = space8[:, 0:3 * HID].bitcast(I32)
        WG = sb("WG", [P, HID], F32R)
        WU = sb("WU", [P, HID], F32R)
        WD2 = part(space8, [P, FC, D], 3 * HID)
        HS = part(space7, [P, FC, Q * P])
        HT = (part(space7, [P, FC, Q * P], FC * Q * P), part(space5, [P, FC, Q * P]))
        ident = sb("ident", [P, P])
        HM = sb("HM", [P, NH])
        HMC = sb("HMC", [P, NC * 3])
        ones_f = sb("ones_f", [P, P])
        CN2 = sb("CN2", [P, BT, KR])
        aa = sb("aa", [KR, BT])
        XSQ = part(space6, [P, 2, Q * P])
        DSQ = part(space2, [KR, BT, SL])
        DSB = part(space1, [KR, BT, SL])
        DP = part(space3, [P, 2, RW, WN * CB])
        WS = sb("WS", [P, 2, RW + 1, 1 + WN * CB])
        bigs = part(space6, [P, WD // 2])
        MM = sb("MM", [P, RW, CB])
        RI = part(space8, [KR, BT, SL + 1])
        UI = part(space5, [KR + 1, BT, SL + 1])
        T1 = part(space1, [KR, BT, SL])
        T2 = part(space2, [KR, BT, SL])
        JG = part(space7, [KR, BT, SL])
        FX = part(space3, [KR, BT * SL])
        FT = part(space6, [P, KR, CC])
        JH = sb("JH", [P, CC, 2])
        goff = sb("goff", [P, 1])
        blk1 = sb("blk1", [P, P], F16)
        hit = sb("hit", [P, CC, 2])
        hs = sb("hs", [P, 2], F16)
        last = sb("last", [P, 1])
        BS = sb("BS", [P, KR])
        lohi = sb("lohi", [KR, 2, BT])
        PA = part(space5, [KR, SL])
        PM = part(space5, [KR, 2, SL], SL)
        GW = sb("GW", [P, NE])
        XT4 = part(space3, [P, NT * P])
        XTHs = sb("XTHs", [P, 2, Q * P], F32R)
        XTLs = sb("XTLs", [P, 2, Q * P], F32R)
        LG = sb("LG", [P, NT, NE])
        M8 = sb("M8", [P, NT, 8])
        I8 = sb("I8", [P, NT, 8], U32)
        IF8 = sb("IF8", [P, NT, 2])
        JE = sb("JE", [P, NT, NE])
        OH = sb("OH", [P, 2, NT, NE])
        AB = sb("AB", [P, NT, NE])
        RA = sb("RA", [P, 2, NT, NE])
        RB = sb("RB", [P, 2, NT, NE])
        RC = sb("RC", [P, 2, NT, NE])
        ZS = sb("ZS", [P, 2, NT])
        GWT = sb("GWT", [P, NT, NE])
        W13 = part(space4, [P, NE, 2 * EI])
        W2 = sb("W2", [P, NE * EC, D])
        W13H = sb("W13H", [P, NE, 2 * EI], F32R)
        W13L = sb("W13L", [P, NE, 2 * EI], F32R)
        SI = part(space5, [P, EC, Q * P])
        HA = part(space4, [P, 2 * EC, Q * P])
        PS = ctx.enter_context(nc.psum_tensor("PS", [P, 8, 512], F32))

        ld_x = [sem(f"ld_x{b}") for b in range(BT)]
        ld_q = sem("ld_q")
        ld_k = sem("ld_k")
        ld_v = sem("ld_v")
        ld_mask = sem("ld_mask")
        ld_ffn = sem("ld_ffn")
        ld_moe = sem("ld_moe")
        ld_gate = sem("ld_gate")
        xth_ok = sem("xth_ok")
        xtl_ok = sem("xtl_ok")
        c_ident = sem("c_ident")
        c_step = sem("c_step")
        c_heads = sem("c_heads")
        c_all = sem("c_all")
        v_step = sem("v_step")
        k_ps = sem("k_ps")
        v_ps = sem("v_ps")
        kss_ok = sem("kss_ok")
        kst_ok = sem("kst_ok")
        kn_ok = sem("kn_ok")
        kT_ps = sem("kT_ps")
        kT_sb = sem("kT_sb")
        kb_ok = sem("kb_ok")
        vx_ok = sem("vx_ok")
        bvt_ok = sem("bvt_ok")
        bo_ps = sem("bo_ps")
        bo_ok = sem("bo_ok")
        var_ok = sem("var_ok")
        std_ok = sem("std_ok")
        xn_ok = sem("xn_ok")
        xT_ps = sem("xT_ps")
        xT_sb = sem("xT_sb")
        q_ps = sem("q_ps")
        q_sb = sem("q_sb")
        qsq_ok = sem("qsq_ok")
        mask_ok = sem("mask_ok")
        qss_ok = sem("qss_ok")
        qst_ok = sem("qst_ok")
        qn_ok = sem("qn_ok")
        qT_ps = sem("qT_ps")
        qT_sb = sem("qT_sb")
        qTb_ok = sem("qTb_ok")
        sc_ps = sem("sc_ps")
        sc_sub = sem("sc_sub")
        exp_ok = sem("exp_ok")
        pT_ps = sem("pT_ps")
        pT_sb = sem("pT_sb")
        pv_ps = sem("pv_ps")
        on_ok = sem("on_ok")
        oT_ps = sem("oT_ps")
        oT_sb = sem("oT_sb")
        wo_ps = sem("wo_ps")
        x1_ok = sem("x1_ok")
        wf_ok = sem("wf_ok")
        g_ps = sem("g_ps")
        u_ps = sem("u_ps")
        silu_ok = sem("silu_ok")
        h_ok = sem("h_ok")
        dn_ps = sem("dn_ps")
        x2_add = sem("x2_add")
        x2_ok = sem("x2_ok")
        xsq_ok = sem("xsq_ok")
        d_ps = sem("d_ps")
        d_pos = sem("d_pos")
        d_ok = sem("d_ok")
        cn_ok = sem("cn_ok")
        bo_add = sem("bo_add")
        r1_ok = sem("r1_ok")
        xt4_ok = sem("xt4_ok")
        big_ok = sem("big_ok")
        dpre = sem("dpre")
        dst = sem("dst")
        dld = sem("dld")
        r_ok = sem("r_ok")
        xs_ok = sem("xs_ok")
        mvs_ok = sem("mvs_ok")
        ui_ok = sem("ui_ok")
        rpre = sem("rpre")
        rst = sem("rst")
        rld_last = sem("rld_last")
        rld = [sem(f"rld_{h}") for h in range(2)]
        f_ok = sem("f_ok")
        fT_ps = sem("fT_ps")
        hit_ok = sem("hit_ok")
        b_ps = sem("b_ps")
        bs_ok = sem("bs_ok")
        bT_ps = sem("bT_ps")
        pm_ok = sem("pm_ok")
        e_ps = sem("e_ps")
        x3_ok = sem("x3_ok")
        lg_ps = sem("lg_ps")
        rsub_ok = sem("rsub_ok")
        rexp_ok = sem("rexp_ok")
        norm_ok = sem("norm_ok")
        lg_sb = sem("lg_sb")
        gate_ok = sem("gate_ok")
        w_hi = sem("w_hi")
        w_lo = sem("w_lo")
        eg_ps = sem("eg_ps")
        eu_ps = sem("eu_ps")
        si_ok = sem("si_ok")
        ac_ok = sem("ac_ok")
        y_ps = sem("y_ps")
        y_ok = sem("y_ok")
        st_out = sem("st_out")

        def bc(ap, shape):
            return ap.to_broadcast(shape)

        def steps3(t):
            return t.rearrange("p (h d) -> p h d", d=HD)

        block = ctx.enter_context(nc.Block())

        x_v = x.rearrange("b (q p) d -> b p q d", p=P)
        out_v = out.rearrange("b (q p) d -> b p q d", p=P)
        XV = X[:, :, :].rearrange("p (b q) d -> p b q d", b=BT)

        def skewed(t, b, shift, cols, groups=NI):
            ps = RW * WD
            return bass.AP(t.tensor, b * (P // BT) * ps + CB + shift,
                           [[ps + CB, groups], [WD, RW], [1, cols]])

        @block.sync
        def _(sp):
            for b in range(BT):
                sp.dma_start(X[:, b * Q:(b + 1) * Q, :], x_v[b]).then_inc(ld_x[b], 16)
            for j in range(3):
                sp.dma_start(CT3[:, :, j * KL:(j + 1) * KL], ctx_dt.rearrange("d (b k) -> d b k", b=BT)).then_inc(ld_k, 16)
            sp.dma_start(WV[:, :], wvT).then_inc(ld_v, 16)
            sp.dma_start(WO[:, :], woT).then_inc(ld_v, 16)
            sp.dma_start(bvc[:, :], bv.rearrange("(d a) -> d a", a=1)).then_inc(ld_v, 16)
            sp.dma_start(BO[:, :], bo.rearrange("(a d) -> a d", a=1).partition_broadcast(P)).then_inc(ld_v, 16)
            sp.dma_start(CK[0:KL, :, :], ctx_kd.rearrange("b k d -> k b d")).then_inc(ld_v, 16)
            sp.dma_start(CK[KL:KR, :, :], ctx_kd[:, 0:KR - KL, :].rearrange("b k d -> k b d")).then_inc(ld_v, 16)
            sp.dma_start(wi[:, 0:HID], wgT).then_inc(ld_ffn, 16)
            sp.dma_start(wi[:, HID:2 * HID], wuT).then_inc(ld_ffn, 16)
            sp.dma_start(wi[:, 2 * HID:3 * HID].rearrange("p (c d) -> p c d", c=FC),
                         wdT.rearrange("(c p) d -> p c d", p=P)).then_inc(ld_ffn, 16)
            sp.wait_ge(big_ok, 1)
            for r in range(RW):
                for h in range(2):
                    sp.dma_start(ds[:, r, h * WD // 2:(h + 1) * WD // 2], bigs[:, :]).then_inc(dpre, 16)
                    sp.dma_start(rs[:, r, h * WD // 2:(h + 1) * WD // 2], bigs[:, :]).then_inc(rpre, 16)
            sp.dma_start(GW[:, :], gateT).then_inc(ld_gate, 16)
            sp.wait_ge(dpre, 16 * 2 * RW)
            for b in range(BT):
                sp.wait_ge(d_ok, b + 1)
                sp.dma_start(skewed(ds, b, 0, SL), DSB[:, b, :]).then_inc(dst, 16)
            sp.wait_ge(dst, 16 * BT)

            def costs(w):
                a, z = w * WN * CB, min((w + 1) * WN, NS) * CB
                wait(sp, dld, 16 * w)
                sp.dma_start(DP[:, w % 2, :, 0:z - a], ds[:, :, CB + a:CB + z]).then_inc(dld, 16)

            costs(0)
            costs(1)
            sp.wait_ge(rpre, 16 * 2 * RW)
            for w in range(NWIN):
                a, z = w * WN * CB, min((w + 1) * WN, NS) * CB
                sp.wait_ge(r_ok, w + 1)
                if w + 2 < NWIN:
                    costs(w + 2)
                wait(sp, rst, 16 * w)
                sp.dma_start(rs[:, :, CB + a:CB + z], WS[:, w % 2, 1:RW + 1, 1:1 + z - a]).then_inc(rst, 16)
            sp.wait_ge(rst, 16 * NWIN)
            for tile, row in ((RI, KR - RW), (UI, KR - RW + 1)):
                ps = RW * WD
                sp.dma_start(tile[row:row + RW, :, :], bass.AP(rs.tensor, (NI - 1) * (ps + CB) + CB - 1,
                                                               [[WD, RW], [(P // BT) * ps, BT], [1, SL + 1]])).then_inc(rld_last, 16)
            for b in range(BT):
                sp.wait_ge(y_ok, NE * (b + 1))
                sp.dma_start(out_v[b], X[:, b * Q:(b + 1) * Q, :]).then_inc(st_out, 16)
            sp.wait_ge(st_out, 16 * BT)

        @block.gpsimd
        def _(pool):
            step = Steps(pool, c_step)
            nc.gpsimd.memset(epsl[:, :], LN_EPS)
            nc.gpsimd.memset(epsq[:, :], Q_EPS).then_inc(c_all, 1)
            step.link(nc.gpsimd.memset(ident[:, :], 0.0))
            nc.gpsimd.affine_select(out=ident[:, :], in_=ident[:, :], compare_op=ALU.not_equal, fill=1.0, base=0,
                                    pattern=[[-1, P]], channel_multiplier=1).then_inc(c_ident, 1)
            step.link(nc.gpsimd.memset(HM[:, :], 1.0))
            step.link(nc.gpsimd.affine_select(out=HM[:, :], in_=HM[:, :], compare_op=ALU.is_ge, fill=0.0, base=0,
                                              pattern=[[-HD, NH]], channel_multiplier=1))
            step.link(nc.gpsimd.affine_select(out=HM[:, :], in_=HM[:, :], compare_op=ALU.is_ge, fill=0.0, base=HD - 1,
                                              pattern=[[HD, NH]], channel_multiplier=-1))
            step.link(nc.gpsimd.memset(HMC[:, :], 1.0))
            for c in range(NC):
                part = HMC[:, 3 * c:3 * c + 3]
                step.link(nc.gpsimd.affine_select(out=part, in_=part, compare_op=ALU.is_ge, fill=0.0,
                                                  base=P * c - KL * H0[c], pattern=[[-KL, 3]], channel_multiplier=1))
                step.link(nc.gpsimd.affine_select(out=part, in_=part, compare_op=ALU.is_ge, fill=0.0,
                                                  base=KL * (H0[c] + 1) - 1 - P * c, pattern=[[KL, 3]],
                                                  channel_multiplier=-1))
            for b in range(BT):
                ins = nc.gpsimd.tensor_copy(VX[:, b, :, HD], HMC[:, :])
            ins.then_inc(c_heads, 1)
            step.link(nc.gpsimd.memset(ones_f[:, :], 1.0))
            pool.wait_ge(ld_v, 16 * 6)
            nc.gpsimd.tensor_scalar(BVT[:, :], ones_f[:, :], bvc[:, :], None, ALU.mult).then_inc(bvt_ok, 1)
            nc.gpsimd.memset(ones_b[:, :], 1.0)
            pool.wait_ge(ld_k, 16 * 7)
            nc.gpsimd.tensor_scalar(CN2[:, :, :], CT3[:, :, 0:KR], -2.0, None, ALU.mult).then_inc(cn_ok, 1)
            pool.wait_ge(bo_ok, 1)
            for b in range(BT):
                pool.wait_ge(xn_ok, b + 1)
                nc.gpsimd.tensor_tensor(X[:, b * Q:(b + 1) * Q, :], X[:, b * Q:(b + 1) * Q, :],
                                        bc(BIASO[:, :].unsqueeze(1), [P, Q, D]), ALU.add).then_inc(bo_add, 1)
            nc.gpsimd.memset(bigs[:, :], BIG).then_inc(big_ok, 1)
            step.link(nc.gpsimd.memset(WS[:, :, :, :], BIG))
            for b in range(BT):
                step.link(nc.gpsimd.memset(WS[b * 32:b * 32 + 1, 0, 0, 0:1], 0.0))
            step.link(nc.gpsimd.memset(last[:, :], float(SL - 1)))
            step.link(nc.gpsimd.iota(JE[:, :, :], pattern=[[0, NT], [1, NE]], base=0, channel_multiplier=0,
                                     allow_small_or_imprecise_dtypes=True))
            for g in range(BT):
                step.link(nc.gpsimd.iota(JH[g * JB:(g + 1) * JB, :, 0], pattern=[[1, CC]], base=0, channel_multiplier=CC,
                                         allow_small_or_imprecise_dtypes=True))
                step.link(nc.gpsimd.memset(goff[g * JB:(g + 1) * JB, :], float(SL * g)))
            step.link(nc.gpsimd.memset(blk1[:, :], 0.0))
            for g in range(BT):
                step.link(nc.gpsimd.memset(blk1[g * JB:(g + 1) * JB, g * JB:(g + 1) * JB], 1.0))
            step.link(nc.gpsimd.memset(hs[:, :], 0.0))
            nc.gpsimd.tensor_scalar(JH[:, :, 1], JH[:, :, 0], 0.5, None, ALU.add).then_inc(c_all, 1)

            pool.wait_ge(ld_ffn, 48)
            nc.gpsimd.tensor_copy(WG[:, :], wi[:, 0:HID])
            nc.gpsimd.tensor_copy(WU[:, :], wi[:, HID:2 * HID])
            nc.gpsimd.tensor_copy(WD2[:, :, :].rearrange("p c d -> p (c d)"), wi[:, 2 * HID:3 * HID]).then_inc(wf_ok, 1)

            def store(t0, n, src, msrc, done, count):
                pool.wait_ge(mvs_ok, count)
                nc.gpsimd.tensor_copy(X[:, t0 if n == 1 else bass.ds(t0, n), :], src)
                nc.gpsimd.tensor_copy(mv[:, t0 if n == 1 else bass.ds(t0, n), :], msrc).then_inc(done, 1)

            def queries(b):
                for q in range(Q):
                    t = b * Q + q
                    pool.wait_ge(qT_sb, b + 1)
                    wait(pool, sc_ps, 3 * (t - 1))
                    nc.gpsimd.tensor_copy(QTb[:, q % 2, :], QT[:, t, :]).then_inc(qTb_ok, 1)
                    if not (isinstance(t, int) and t < 3):
                        store(t - 3, 1, XS[:, (q - 3) % Q, :], mvs[:, (q - 3) % Q, :], x1_ok, t - 2)

            peeled(pool, BT, queries)
            def low_ffn(b):
                pool.wait_ge(xth_ok, b + 1)
                wait(pool, u_ps, FC * (b - 1))
                nc.gpsimd.tensor_tensor(XTLs[:, b % 2, :], XNT[:, b % 2, :], XTHs[:, b % 2, :].bitcast(F32), ALU.subtract).then_inc(xtl_ok, 1)

            for t in range(NT - 3, NT):
                store(t, 1, XS[:, t % Q, :], mvs[:, t % Q, :], x1_ok, t + 1)
                if t == NT - 3:
                    low_ffn(0)
            for b in range(1, BT):
                low_ffn(b)

            pool.wait_ge(dn_ps, BT)
            step.link(nc.gpsimd.memset(UI[0:1, :, :], BIG))
            nc.gpsimd.memset(UI[0:1, :, 0:1], 0.0).then_inc(ui_ok, 1)
            nc.gpsimd.iota(JG[:, :, :], pattern=[[SL, BT], [1, SL]], base=0, channel_multiplier=0,
                           allow_small_or_imprecise_dtypes=True).then_inc(ui_ok, 1)

            for e in range(NE):
                pool.wait_ge(w_hi, e + 1)
                nc.gpsimd.tensor_tensor(W13L[:, e, :], W13[:, e, :], W13H[:, e, :].bitcast(F32), ALU.subtract).then_inc(w_lo, 1)

            for b in range(BT):
                pool.wait_ge(xT_sb, 3 * BT + b + 1)
                nc.gpsimd.tensor_copy(XT4[:, b * Q * P:(b + 1) * Q * P], XNT[:, b % 2, :]).then_inc(xt4_ok, 1)

            def low_inputs(b):
                pool.wait_ge(xth_ok, BT + b + 1)
                nc.gpsimd.tensor_tensor(XTLs[:, b % 2, :], XT4[:, b * Q * P:(b + 1) * Q * P],
                                        XTHs[:, b % 2, :].bitcast(F32), ALU.subtract).then_inc(xtl_ok, 1)

            for b in range(BT):
                low_inputs(b)

        @block.scalar
        def _(act):
            act.dma_start(WQ[:, :], wqT).then_inc(ld_q, 16)
            act.dma_start(BQ[:, :], bq.rearrange("(a d) -> a d", a=1).partition_broadcast(P)).then_inc(ld_q, 16)
            act.dma_start(WK[:, :], wkT).then_inc(ld_k, 16)
            for t, v in ((BK, bk), (qwb, qw), (kwb, kw)):
                act.dma_start(t[:, :], v.rearrange("(a d) -> a d", a=1).partition_broadcast(P)).then_inc(ld_k, 16)
            act.dma_start(mi[:, :, :].rearrange("p b k -> p (b k)"),
                          mask.rearrange("(a b) k -> a (b k)", a=1).partition_broadcast(P)).then_inc(ld_mask, 16)

            def copy(out, in_):
                return nc.scalar.activation(out, in_, ACT.Copy)

            act.wait_ge(c_all, 1)
            def std_of(semaphore, value, b0=0, b1=BT):
                act.wait_ge(semaphore, value)
                nc.scalar.activation(std[:, b0 * Q:b1 * Q], mv[:, b0 * Q:b1 * Q, 1], ACT.Sqrt, bias=epsl[:, :]).then_inc(std_ok, 1)

            def copy_xT(r, bank=0):
                act.wait_ge(xT_ps, r + 1)
                copy(XNT[:, r % 2, :], PS[:, bank, :]).then_inc(xT_sb, 1)

            std_of(var_ok, 1, 0, 1)
            std_of(var_ok, 2, 1, 2)

            copy_xT(0)
            std_of(var_ok, 3, 2, 3)
            std_of(var_ok, 4, 3, 4)
            for b in range(BT):
                act.wait_ge(q_sb, b + 1)
                nc.scalar.activation(SQ[:, b * Q * D:(b + 1) * Q * D], Qs[:, b * Q * D:(b + 1) * Q * D], ACT.Square).then_inc(qsq_ok, 1)
                if b + 1 < BT:
                    wait(act, q_ps, b)
                    copy_xT(b + 1)
                act.wait_ge(qss_ok, b + 1)
                nc.scalar.activation(qrs[:, b * Q * NH:(b + 1) * Q * NH], qss[:, b * Q * NH:(b + 1) * Q * NH], ACT.Sqrt,
                                     bias=epsq[:, :], scale=1.0 / HD).then_inc(qst_ok, 1)
                if b == 0:
                    act.wait_ge(kss_ok, 1)
                    nc.scalar.activation(krs[:, :], kss[:, :], ACT.Sqrt, bias=epsq[0:KL, :], scale=1.0 / HD).then_inc(kst_ok, 1)
                act.wait_ge(qT_ps, b + 1)
                copy(QT[:, b * Q:(b + 1) * Q, :].rearrange("p q c -> p (q c)"), PS[:, 3, :]).then_inc(qT_sb, 1)
                if b == 1:
                    act.wait_ge(kT_ps, 1)
                    copy(KT[:, :], PS[:, 2, 0:BT * KL]).then_inc(kT_sb, 1)
                    act.wait_ge(c_heads, 1)
                    act.wait_ge(kT_sb, 1)
                if b in (1, 2):
                    for h in range((b - 1) * NH // 3, b * NH // 3):
                        ins = nc.scalar.activation(KB[:, :, h * KL:(h + 1) * KL], KT[:, :].rearrange("p (b k) -> p b k", b=BT),
                                                   ACT.Copy, scale=HM[:, h:h + 1])
                    ins.then_inc(kb_ok, 1)

            groups = [(0, 4), (4, 8), (8, NC)]

            def exps(t, par, part):
                c0, c1 = (0, 12 * KL) if part == 0 else (12 * KL, HK)
                act.wait_ge(sc_sub, 2 * t + 1 + part)
                nc.scalar.activation(PR[:, par, c0:c1], PR[:, par, c0:c1], ACT.Exp).then_inc(exp_ok, 1)

            def weights_T(t, g):
                c0, c1 = groups[g]
                act.wait_ge(pT_ps, 3 * t + g + 1)
                if g == 0:
                    wait(act, pv_ps, t)
                rows = P if g < 2 else CR[NC - 1]
                copy(PT[:, c0:NC - 1 if g == 2 else c1, :],
                     PS[:, 6, 0:((NC - 1 if g == 2 else c1) - c0) * P].rearrange("p (c k) -> p c k", k=P)
                     ).then_inc(pT_sb, 1)
                if g == 2:
                    copy(PT[0:rows, NC - 1, :], PS[0:rows, 6, (NC - 1 - c0) * P:(NC - c0) * P]).then_inc(pT_sb, 1)

            def out_T(t):
                act.wait_ge(oT_ps, t + 1)
                copy(OT[:, :], PS[:, 7, 256:384]).then_inc(oT_sb, 1)

            for part in range(2):
                exps(0, 0, part)
            act.wait_ge(dpre, 16 * 2 * RW)
            act.wait_ge(rpre, 16 * 2 * RW)

            def ffn_inputs(b):
                wait(act, xtl_ok, b - 1)
                copy_xT(BT + b)
                wait(act, u_ps, FC * (b - 1))
                copy(XTHs[:, b % 2, :], PS[:, 0, :]).then_inc(xth_ok, 1)

            def attend(b):
                for q in range(Q):
                    t = b * Q + q
                    first, final = isinstance(t, int) and t == 0, isinstance(t, int) and t == NT - 1
                    weights_T(t, 0)
                    if not first:
                        out_T(t - 1)
                    weights_T(t, 1)
                    if not final:
                        exps(t + 1, (q + 1) % 2, 0)
                    weights_T(t, 2)
                    if not final:
                        exps(t + 1, (q + 1) % 2, 1)
                    if isinstance(t, int) and t == NT - 2:
                        std_of(x1_ok, NT - Q, 0, BT - 1)

            peeled(act, BT, attend)
            ffn_inputs(0)
            out_T(NT - 1)

            std_of(x1_ok, NT, BT - 1, BT)
            for b in range(BT):
                for c in range(FC):
                    act.wait_ge(g_ps, FC * b + c + 1)
                    wait(act, h_ok, FC * (b - 1) + c + 1)
                    nc.scalar.activation(HS[:, c, :], PS[:, 1 + 2 * c, :], ACT.Silu, scale=DQ).then_inc(silu_ok, 1)
                    if b < BT - 1 and c == 0:
                        ffn_inputs(b + 1)

            std_of(x2_ok, BT - 1, 0, BT - 1)

            def squares(b):
                wait(act, d_ps, b - 1)
                copy_xT(2 * BT + b, 7 * (b % 2))
                nc.scalar.activation(XSQ[:, b % 2, :], PS[:, 7 * (b % 2), :], ACT.Square).then_inc(xsq_ok, 1)

            squares(0)
            std_of(x2_ok, BT, BT - 1, BT)
            squares(1)
            for b in range(BT):
                act.wait_ge(d_pos, b + 1)
                nc.scalar.activation(DSB[:, b, :], DSQ[:, b, :], ACT.Sqrt).then_inc(d_ok, 1)
                if b + 2 < BT:
                    squares(b + 2)

            act.wait_ge(dld, 32)
            act.dma_start(W13[:, :, :].rearrange("p e n -> p (e n)"), w13T).then_inc(ld_moe, 16)
            act.dma_start(W2[:, :, :], w2T.rearrange("(c p) d -> p c d", p=P)).then_inc(ld_moe, 16)
            act.wait_ge(ld_moe, 32)
            for e in range(NE):
                copy(W13H[:, e, :], W13[:, e, :]).then_inc(w_hi, 1)

            act.wait_ge(ui_ok, 1)
            act.wait_ge(rst, 16 * (NWIN - 1))
            for b in range(BT):
                for tile, row in ((RI, 0), (UI, 1)):
                    act.dma_start(tile[row:row + KR - RW, b, :], skewed(rs, b, -1, SL + 1, NI - 1)).then_inc(rld[b // HB2], 16)

            for b in range(BT + 2):
                if b < BT:
                    std_of(x3_ok, b + 1, b, b + 1)
                if 0 < b <= BT:
                    act.wait_ge(norm_ok, b)
                    wait(act, xT_ps, 3 * BT + b - 2)
                    for q in range(Q):
                        t = (b - 1) * Q + q
                        ins = nc.scalar.activation(XN[:, (b - 1) % 2, q, :], X[:, t, :], ACT.Identity, bias=shift[:, t:t + 1],
                                                   scale=rstd[:, t:t + 1])
                    ins.then_inc(xn_ok, 1)
                if b > 1:
                    wait(act, lg_ps, b - 3)
                    wait(act, xt4_ok, b - 3)
                    copy_xT(3 * BT + b - 2, 7 * (b % 2))

            def inputs(b):
                copy(XTHs[:, b % 2, :],
                     XT4[:, b * Q * P:(b + 1) * Q * P] if isinstance(b, int) else XT4[:, bass.ds(b * Q * P, Q * P)]
                     ).then_inc(xth_ok, 1)

            act.wait_ge(xt4_ok, BT)
            inputs(0)
            act.wait_ge(rsub_ok, 1)
            nc.scalar.activation(RC[:, :, :, :], RC[:, :, :, :], ACT.Exp).then_inc(rexp_ok, 1)

            def experts(b):
                for e in range(NE):
                    for c in range(EC):
                        n = NE * b + e
                        m = EC * n + c
                        act.wait_ge(eg_ps, m + 1)
                        wait(act, ac_ok, m - 1)
                        nc.scalar.activation(SI[:, c, :], PS[:, 2 * c, :], ACT.Silu).then_inc(si_ok, 1)
                    if e == 0 and not (isinstance(b, int) and b == BT - 1):
                        inputs(b + 1)

            peeled(act, BT, experts)

        @block.vector
        def _(dve):
            step = Steps(dve, v_step)
            V = nc.vector

            def stats(src, dst):
                for q in range(Q):
                    ins = V.bn_stats(bst[:, q, :], src[:, q, :])
                step.link(ins)
                for q in range(Q):
                    ins = V.bn_aggr(dst[:, q, :], bst[:, q, :])
                return ins

            def rstd_of(run, b0=0, b1=BT):
                dve.wait_ge(std_ok, run)
                step.link(V.reciprocal(rstd[:, b0 * Q:b1 * Q], std[:, b0 * Q:b1 * Q]))

            def normalise(r, b):
                wait(dve, xT_ps, r - 1)
                for q in range(Q):
                    t = b * Q + q
                    ins = V.tensor_scalar(XN[:, r % 2, q, :], X[:, t, :], mv[:, t, 0:1], rstd[:, t:t + 1], ALU.subtract, ALU.mult)
                ins.then_inc(xn_ok, 1)

            def first_stats(b):
                dve.wait_ge(ld_x[b], 16)
                stats(X[:, b * Q:(b + 1) * Q, :], mv[:, b * Q:(b + 1) * Q, :]).then_inc(var_ok, 1)
                dve.wait_ge(var_ok, b + 1)

            first_stats(0)
            first_stats(1)
            for b in range(2):
                rstd_of(b + 1, b, b + 1)
                normalise(b, b)
            first_stats(2)
            first_stats(3)
            dve.wait_ge(ld_q, 32)

            def keys():
                dve.wait_ge(ld_k, 16 * 7)
                dve.wait_ge(k_ps, 1)
                step.link(V.tensor_tensor(KQ[:, :].rearrange("k (b d) -> k b d", b=BT),
                                          PS[0:KL, 2, :].rearrange("k (b d) -> k b d", b=BT),
                                          bc(BK[0:KL, :].unsqueeze(1), [KL, BT, D]), ALU.add))
                step.link(V.tensor_tensor(KSQ[:, :], KQ[:, :], KQ[:, :], ALU.mult))
                V.tensor_reduce(kss[:, :], steps3(KSQ[:, :]), AX, ALU.add).then_inc(kss_ok, 1)
                step.link(V.tensor_scalar(qkw[:, :], kwb[:, :], SCALE, None, ALU.mult))
                step.link(V.tensor_tensor(qkw[:, :], qkw[:, :], qwb[:, :], ALU.mult))

            def keys_normalised():
                dve.wait_ge(kst_ok, 1)
                step.link(V.reciprocal(krs[:, :], krs[:, :]))
                step.link(V.tensor_tensor(steps3(KQ[:, :]), steps3(KQ[:, :]), bc(krs[:, :].unsqueeze(2), [KL, BT * NH, HD]), ALU.mult))
                V.tensor_tensor(steps3(KQ[:, :]), steps3(KQ[:, :]), bc(qkw[0:KL, :].unsqueeze(1), [KL, BT * NH, HD]),
                                ALU.mult).then_inc(kn_ok, 1)

            def project(b):
                dve.wait_ge(q_ps, b + 1)
                V.tensor_tensor(Qs[:, b * Q * D:(b + 1) * Q * D].rearrange("p (q d) -> p q d", q=Q),
                                PS[:, 1, :].rearrange("p (q d) -> p q d", q=Q),
                                bc(BQ[:, :].unsqueeze(1), [P, Q, D]), ALU.add).then_inc(q_sb, 1)

            def squares_of(b):
                dve.wait_ge(qsq_ok, b + 1)
                V.tensor_reduce(qss[:, b * Q * NH:(b + 1) * Q * NH], steps3(SQ[:, b * Q * D:(b + 1) * Q * D]), AX, ALU.add).then_inc(qss_ok, 1)

            def scale_q(b):
                dve.wait_ge(qst_ok, b + 1)
                c0, c1 = b * Q * NH, (b + 1) * Q * NH
                step.link(V.reciprocal(qrs[:, c0:c1], qrs[:, c0:c1]))
                wait(dve, qT_ps, b)
                V.tensor_tensor(QN[:, :, :].rearrange("p q (h d) -> p (q h) d", d=HD), steps3(Qs[:, b * Q * D:(b + 1) * Q * D]),
                                bc(qrs[:, c0:c1].unsqueeze(2), [P, Q * NH, HD]), ALU.mult).then_inc(qn_ok, 1)

            keys()
            for b in range(BT):
                project(b)
                if b + 2 < BT:
                    rstd_of(b + 3, b + 2, b + 3)
                    normalise(b + 2, b + 2)
                squares_of(b)
                if b == 1:
                    keys_normalised()
                scale_q(b)
                if b == 1:
                    dve.wait_ge(bo_ps, 1)
                    V.tensor_tensor(BIASO[:, :], PS[:, 7, 256:256 + D], BO[:, :], ALU.add).then_inc(bo_ok, 1)
            dve.wait_ge(ld_v, 16 * 6)
            dve.wait_ge(kn_ok, 1)
            step.link(V.tensor_tensor(CSQ[:, :], CK[:, :, :].rearrange("k b d -> k (b d)"), CK[:, :, :].rearrange("k b d -> k (b d)"), ALU.mult))
            step.link(V.tensor_reduce(aa[:, :], CSQ[:, :].rearrange("k (b d) -> k b d", b=BT), AX, ALU.add))
            dve.wait_ge(c_heads, 1)
            dve.wait_ge(kT_sb, 1)
            for h in range(2 * NH // 3, NH):
                ins = V.tensor_scalar(KB[:, :, h * KL:(h + 1) * KL], KT[:, :].rearrange("p (b k) -> p b k", b=BT), HM[:, h:h + 1],
                                      None, ALU.mult)
            ins.then_inc(kb_ok, 1)
            dve.wait_ge(ld_mask, 16)
            V.tensor_single_scalar(mz[:, :, :], mi[:, :, :], 0.0, ALU.is_equal).then_inc(mask_ok, 1)
            dve.wait_ge(mask_ok, 1)
            V.tensor_scalar(mrow[0:1, :, :], mz[0:1, :, :], -BIG, None, ALU.mult).then_inc(mask_ok, 1)
            dve.wait_ge(mask_ok, 2)
            step.link(V.tensor_scalar(mz[:, :, :], mz[:, :, :], -1.0, 1.0, ALU.mult, ALU.add))
            for b in range(BT):
                dve.wait_ge(v_ps, b + 1)
                ins = V.tensor_tensor(VX[:, b, :, 0:HD], PS[:, 4 + b, 0:NC * 3 * HD].rearrange("p (m d) -> p m d", d=HD),
                                      bc(HMC[:, :].unsqueeze(2), [P, NC * 3, HD]), ALU.mult)
            ins.then_inc(vx_ok, 1)
            step.link(V.tensor_reduce(cnt[:, :], mz[:, :, :], AX, ALU.add))
            step.link(V.reciprocal(nanf[:, :], cnt[:, :]))
            step.link(V.tensor_scalar(nanf[:, :], nanf[:, :], 0.0, None, ALU.mult))

            def heads(t, par, h0, h1, bank, nb):
                n = (h1 - h0) // nb
                src = PS[:, 3 * par + bank:3 * par + bank + nb, 0:n * KL].rearrange("p a (h k) -> p a h k", k=KL)
                top = mx[:, h0:h1].rearrange("p (a h) -> p a h", a=nb)
                step.link(V.tensor_reduce(top, src, AX, ALU.max))
                V.tensor_tensor(PR[:, par, h0 * KL:h1 * KL].rearrange("p (a h k) -> p a h k", a=nb, k=KL), src,
                                bc(top.unsqueeze(3), [P, nb, n, KL]), ALU.subtract).then_inc(sc_sub, 1)

            def centre(t, par, part):
                dve.wait_ge(sc_ps, 3 * t + 2 + part)
                if part == 0:
                    wait(dve, pT_ps, 3 * (t - 1))
                    heads(t, par, 0, 12, 0, 2)
                else:
                    heads(t, par, 12, 16, 2, 1)

            def residual(t, b, q):
                dve.wait_ge(wo_ps, t + 1)
                wait(dve, x1_ok, t - Q + 1)
                V.scalar_tensor_tensor(XS[:, q, :], PS[:, 7, 384:512], nanf[:, b:b + 1] if isinstance(b, int) else nanf[:, bass.ds(b, 1)],
                                       X[:, t, :], ALU.add, ALU.add).then_inc(xs_ok, 1)
                dve.wait_ge(xs_ok, t + 1)
                step.link(V.bn_stats(bst[:, 0, :], XS[:, q, :]))
                V.bn_aggr(mvs[:, q, :], bst[:, 0, :]).then_inc(mvs_ok, 1)

            centre(0, 0, 0)
            centre(0, 0, 1)
            dve.wait_ge(bo_add, BT)

            def attend(b):
                for q in range(Q):
                    t = b * Q + q
                    first, final = isinstance(t, int) and t == 0, isinstance(t, int) and t == NT - 1
                    if not final:
                        centre(t + 1, (q + 1) % 2, 0)
                    if not first:
                        residual(t - 1, b if q else b - 1, (q - 1) % Q)
                    if not final:
                        centre(t + 1, (q + 1) % 2, 1)
                    if final:
                        rstd_of(5, 0, BT - 1)
                        normalise(BT, 0)
                    dve.wait_ge(pv_ps, t + 1)
                    O = PS[:, 7, 0:NH * VW].rearrange("p (h w) -> p h w", w=VW)
                    step.link(V.reciprocal(rcp[:, :], O[:, :, HD]))
                    V.tensor_tensor(ON[:, :].rearrange("p (h d) -> p h d", d=HD), O[:, :, 0:HD],
                                    bc(rcp[:, :].unsqueeze(2), [P, NH, HD]), ALU.mult).then_inc(on_ok, 1)

            peeled(dve, BT, attend, step)
            residual(NT - 1, BT - 1, Q - 1)

            def hidden(b):
                for c in range(FC):
                    dve.wait_ge(u_ps, FC * b + c + 1)
                    dve.wait_ge(silu_ok, FC * b + c + 1)
                    wait(dve, dn_ps, b - 1)
                    V.scalar_tensor_tensor(HT[b % 2][:, c, :], PS[:, 2 + 2 * c, :], DQ, HS[:, c, :], ALU.mult, ALU.mult).then_inc(h_ok, 1)

            normalise(BT + 1, 1)
            hidden(0)
            rstd_of(6, BT - 1, BT)
            dve.wait_ge(x1_ok, NT)
            for b in range(BT):
                if b + 2 < BT:
                    normalise(BT + b + 2, b + 2)
                if b + 1 < BT:
                    hidden(b + 1)
                if b == BT - 1:
                    rstd_of(7, 0, BT - 1)
                    normalise(2 * BT, 0)
                    normalise(2 * BT + 1, 1)
                dve.wait_ge(dn_ps, b + 1)
                xb = X[:, b * Q:(b + 1) * Q, :]
                V.scalar_tensor_tensor(xb.rearrange("p q d -> p (q d)"), PS[:, 7, :], DQ, xb.rearrange("p q d -> p (q d)"),
                                       ALU.mult, ALU.add).then_inc(x2_add, 1)
                dve.wait_ge(x2_add, b + 1)
                stats(xb, mv[:, b * Q:(b + 1) * Q, :]).then_inc(x2_ok, 1)
                dve.wait_ge(x2_ok, b + 1)

            rstd_of(8, BT - 1, BT)
            for b in range(BT):
                if b + 2 < BT:
                    normalise(2 * BT + b + 2, b + 2)
                dve.wait_ge(d_ps, b + 1)
                V.tensor_scalar(DSQ[:, b, :], PS[0:KR, 1 + b, :], aa[:, b:b + 1], 0.0, ALU.add, ALU.max).then_inc(d_pos, 1)

            down = [31] + list(range(31))

            def wave(k, par, go_on=True):
                at = k * CB
                for r in range(RW):
                    step.link(V.tensor_tensor(MM[:, r, :], WS[:, par, r, at:at + CB], WS[:, par, r, at + 1:at + 1 + CB], ALU.min))
                    ins = V.tensor_tensor_scan(WS[:, par, r + 1, at + 1:at + 1 + CB], MM[:, r, :], DP[:, par, r, at:at + CB],
                                               WS[:, par, r + 1, at:at + 1], ALU.min, ALU.add)
                    if go_on or r < RW - 1:
                        step.link(ins)
                if not go_on:
                    ins.then_inc(r_ok, 1)
                    return
                if k == WN - 1:
                    V.tensor_copy(WS[:, 1 - par, :, 0:1], WS[:, par, :, at + CB:at + CB + 1]).then_inc(r_ok, 1)
                    step.link(V.stream_shuffle(WS[:, 1 - par, 0, 1:1 + CB], WS[:, par, RW, at + 1:at + 1 + CB], down))
                else:
                    step.link(V.stream_shuffle(WS[:, par, 0, at + CB + 1:at + 2 * CB + 1], WS[:, par, RW, at + 1:at + 1 + CB], down))

            def two_windows(v):
                for par in range(2):
                    w = v * 2 + par
                    dve.wait_ge(dld, w * 16 + 16)
                    wait(dve, rst, (w - 1) * 16)
                    for k in range(WN):
                        wave(k, par)

            pairs = NS // (2 * WN)
            two_windows(0)
            with dve.Fori(1, pairs) as v:
                step.restart()
                two_windows(v)
            dve.wait_ge(dld, 16 * NWIN)
            dve.wait_ge(rst, 16 * (NWIN - 2))
            assert NS - 2 * WN * pairs == 1
            wave(0, 0, False)

            dve.wait_ge(rld_last, 32)
            dve.wait_ge(ui_ok, 2)
            for h in range(2):
                dve.wait_ge(rld[h], 16 * 2 * HB2)
                bs = slice(h * HB2, (h + 1) * HB2)
                dg, up, lf = UI[0:KR, bs, 0:SL], UI[0:KR, bs, 1:SL + 1], RI[:, bs, 0:SL]
                step.link(V.tensor_tensor(T1[:, bs, :], dg, up, ALU.min))
                step.link(V.tensor_tensor(T2[:, bs, :], lf, T1[:, bs, :], ALU.is_ge))
                step.link(V.tensor_tensor(T1[:, bs, :], dg, up, ALU.is_le))
                step.link(V.scalar_tensor_tensor(T1[:, bs, :], T1[:, bs, :], -0.5, JG[:, bs, :], ALU.mult, ALU.add))
                step.link(V.tensor_tensor(T1[:, bs, :], T1[:, bs, :], T2[:, bs, :], ALU.mult))
                v2 = T1[:, bs, :].rearrange("k b j -> k (b j)")
                V.tensor_tensor_scan(FX[:, h * HB2 * SL:(h + 1) * HB2 * SL], v2, v2, -1.0, ALU.max, ALU.max).then_inc(f_ok, 1)
            per = 6
            for g in range(3):
                c0, n = g * per, min(per, CC - g * per)
                dve.wait_ge(fT_ps, g + 1)
                ins = V.tensor_scalar(FT[:, :, c0:c0 + n].rearrange("p k c -> p c k"),
                                      PS[:, g, 0:n * 85].rearrange("p (c k) -> p c k", k=85)[:, :, 0:KR],
                                      goff[:, :], None, ALU.subtract)
            step.link(ins)

            def look(i, came, par):
                V.scalar_tensor_tensor(hit[:, :, :], JH[:, :, :], came, bc(FT[:, i, :].unsqueeze(2), [P, CC, 2]),
                                       ALU.is_equal, ALU.mult, accum_out=hs[:, par:par + 1]).then_inc(hit_ok, 1)

            with nc.allow_low_precision(reason="columns are multiples of one half below 1024, exact in float16"):
                look(KL - 1, last[:, :], 0)
                for i in range(KL - 2, -1, -1):
                    dve.wait_ge(b_ps, KL - 1 - i)
                    look(i, PS[:, 5, i + 1:i + 2], (KL - 1 - i) % 2)
            dve.wait_ge(b_ps, KL)
            V.memset(BS[:, KL:KR], float(SL - 1))
            V.tensor_copy(BS[:, 0:KL], PS[:, 5, 0:KL]).then_inc(bs_ok, 1)
            dve.wait_ge(bT_ps, 1)
            step.link(V.tensor_copy(lohi[0:KL, :, :],
                                    PS[0:KL, 6, 0:2 * P].rearrange("k (a b c) -> k a b c", a=2, b=BT)[:, :, :, 0]))
            jr = JG[0:KL, 0, :]

            def on_path(b):
                step.link(V.tensor_scalar(PA[0:KL, :], jr, lohi[0:KL, 0, b:b + 1], None, ALU.is_ge))
                wait(dve, e_ps, b - 1)
                V.scalar_tensor_tensor(PM[0:KL, b % 2, :], jr, lohi[0:KL, 1, b:b + 1], PA[0:KL, :], ALU.is_le, ALU.mult).then_inc(pm_ok, 1)
                dve.wait_ge(pm_ok, b + 1)

            on_path(0)
            for b in range(BT + 1):
                if b + 1 < BT:
                    on_path(b + 1)
                if b < BT:
                    dve.wait_ge(e_ps, b + 1)
                    xb = X[:, b * Q:(b + 1) * Q, :]
                    step.link(V.tensor_tensor(xb.rearrange("p q d -> p (q d)"), PS[:, 1 + b, :], xb.rearrange("p q d -> p (q d)"), ALU.add))
                    stats(xb, mv[:, b * Q:(b + 1) * Q, :]).then_inc(x3_ok, 1)
                    dve.wait_ge(x3_ok, b + 1)
                if b > 0:
                    rstd_of(8 + b, b - 1, b)
                    c = slice((b - 1) * Q, b * Q)
                    V.scalar_tensor_tensor(shift[:, c], mv[:, c, 0], -1.0, rstd[:, c], ALU.mult, ALU.mult).then_inc(norm_ok, 1)

            for b in range(BT):
                dve.wait_ge(lg_ps, b + 1)
                c = slice(b * Q, (b + 1) * Q)
                V.tensor_copy(LG[:, c, :].rearrange("p t e -> p (t e)"), PS[:, 5 + b % 2, 256:256 + Q * NE]).then_inc(lg_sb, 1)
                dve.wait_ge(lg_sb, b + 1)
                for t in range(b * Q, (b + 1) * Q):
                    ins = V.max(M8[:, t, :], LG[:, t, :])
                step.link(ins)
                for t in range(b * Q, (b + 1) * Q):
                    ins = V.max_index(I8[:, t, :], M8[:, t, :], LG[:, t, :])
            step.link(ins)
            step.link(V.tensor_copy(IF8[:, :, :], I8[:, :, 0:2]))
            full = [P, 2, NT, NE]
            flat = "p j t e -> p (j t e)"
            best = bc(M8[:, :, 0:2].rearrange("p t j -> p j t").unsqueeze(3), full)
            lg = bc(LG[:, :, :].unsqueeze(1), full)
            step.link(V.tensor_tensor(OH[:, :, :, :], bc(JE[:, :, :].unsqueeze(1), full),
                                      bc(IF8[:, :, :].rearrange("p t j -> p j t").unsqueeze(3), full), ALU.is_equal))
            step.link(V.tensor_scalar(AB[:, :, :], LG[:, :, :], -1.0, None, ALU.mult))
            step.link(V.tensor_tensor(AB[:, :, :], AB[:, :, :], LG[:, :, :], ALU.max))
            step.link(V.tensor_tensor(RA[:, :, :, :], bc(AB[:, :, :].unsqueeze(1), full), best, ALU.max))
            step.link(V.tensor_tensor(RB[:, :, :, :], best, lg, ALU.subtract))
            step.link(V.scalar_tensor_tensor(RA[:, :, :, :].rearrange(flat), RA[:, :, :, :].rearrange(flat), 0.02,
                                             RB[:, :, :, :].rearrange(flat), ALU.mult, ALU.is_ge))
            V.tensor_scalar(RC[:, :, :, :], RB[:, :, :, :], -1.0, 0.0, ALU.mult, ALU.min).then_inc(rsub_ok, 1)
            step.link(V.tensor_tensor(AB[:, :, :], OH[:, 0, :, :], RA[:, 1, :, :], ALU.mult))
            step.link(V.tensor_tensor(RA[:, 1, :, :], RA[:, 1, :, :], AB[:, :, :], ALU.subtract))
            dve.wait_ge(rexp_ok, 1)
            step.link(V.tensor_tensor(RC[:, :, :, :], RC[:, :, :, :], RA[:, :, :, :], ALU.mult))
            step.link(V.tensor_reduce(ZS[:, :, :], RC[:, :, :, :], AX, ALU.add))
            step.link(V.reciprocal(ZS[:, :, :], ZS[:, :, :]))
            step.link(V.tensor_tensor(OH[:, :, :, :], OH[:, :, :, :], bc(ZS[:, :, :].unsqueeze(3), full), ALU.mult))
            step.link(V.tensor_tensor(GWT[:, :, :], OH[:, 0, :, :], OH[:, 1, :, :], ALU.add))

            def add_out(n, b, e):
                dve.wait_ge(y_ps, n + 1)
                wait(dve, y_ok, n)
                for q in range(Q):
                    t = b * Q + q
                    ins = V.scalar_tensor_tensor(X[:, t, :], PS[:, 4 + e % 2, q * D:(q + 1) * D], GWT[:, t, e:e + 1], X[:, t, :],
                                                 ALU.mult, ALU.add)
                ins.then_inc(y_ok, 1)

            def experts(b):
                for e in range(NE):
                    n = NE * b + e
                    for c in range(EC):
                        m = EC * n + c
                        dve.wait_ge(eu_ps, m + 1)
                        dve.wait_ge(si_ok, m + 1)
                        wait(dve, y_ps, n - 1)
                        V.tensor_tensor(HA[:, e % 2 * EC + c, :], PS[:, 2 * c + 1, :], SI[:, c, :], ALU.mult).then_inc(ac_ok, 1)
                    if not (isinstance(n, int) and n == 0):
                        add_out(n - 1, b if e else b - 1, (e - 1) % NE)

            dve.wait_ge(w_lo, NE)
            experts(0)
            with dve.Fori(1, BT) as b:
                experts(b)
            add_out(NE * BT - 1, BT - 1, NE - 1)

        @block.tensor
        def _(pe):
            def mm(o, l, r, start=True, stop=True, **kw):
                return nc.tensor.matmul(o, l, r, start=start, stop=stop, **kw)

            pe.wait_ge(c_ident, 1)

            def x_T(r, bank=0):
                pe.wait_ge(xn_ok, r + 1)
                for q in range(Q):
                    ins = nc.tensor.transpose(PS[:, bank, q * P:(q + 1) * P], XN[:, r % 2, q, :], ident[:, :])
                ins.then_inc(xT_ps, 1)

            def queries(b):
                wait(pe, xT_sb, b)
                x_T(b)
                pe.wait_ge(xT_sb, b + 1)
                wait(pe, q_sb, b)
                for q in range(Q):
                    ins = mm(PS[:, 1, q * P:(q + 1) * P], XNT[:, b % 2, q * P:(q + 1) * P], WQ[:, :])
                ins.then_inc(q_ps, 1)

            def queries_T(b):
                wait(pe, qT_sb, b)
                pe.wait_ge(qn_ok, b + 1)
                for q in range(Q):
                    ins = nc.tensor.transpose(PS[:, 3, q * P:(q + 1) * P], QN[:, q, :], ident[:, :])
                ins.then_inc(qT_ps, 1)

            def values(b):
                for c in range(NC):
                    s = c * P % KL
                    ins = mm(PS[:, 4 + b, c * 3 * HD:(c + 1) * 3 * HD], CT3[:, b, s:s + P],
                             WV[:, H0[c] * HD:(H0[c] + 3) * HD])
                ins.then_inc(v_ps, 1)

            pe.wait_ge(ld_q, 32)
            queries(0)
            pe.wait_ge(ld_k, 16 * 7)
            for b in range(BT):
                ins = mm(PS[0:KL, 2, b * D:(b + 1) * D], CT3[:, b, 0:KL], WK[:, :])
            ins.then_inc(k_ps, 1)
            for b in range(BT):
                if b + 1 < BT:
                    queries(b + 1)
                if b == 0:
                    pe.wait_ge(ld_v, 16 * 6)
                    pe.wait_ge(bvt_ok, 1)
                    mm(PS[:, 7, 256:256 + D], BVT[:, :], WO[:, :]).then_inc(bo_ps, 1)
                if b == 1:
                    pe.wait_ge(kn_ok, 1)
                    for c in range(BT):
                        ins = nc.tensor.transpose(PS[:, 2, c * KL:(c + 1) * KL], KQ[:, c * D:(c + 1) * D], ident[0:KL, 0:KL])
                    ins.then_inc(kT_ps, 1)
                queries_T(b)
                if b == BT - 1:
                    pe.wait_ge(bo_ok, 1)
                values(b)

            pe.wait_ge(kb_ok, BT - 1)
            pe.wait_ge(vx_ok, 1)
            pe.wait_ge(bo_ok, 1)
            pe.wait_ge(mask_ok, 2)
            pe.wait_ge(qT_sb, BT)
            pe.wait_ge(kT_sb, 1)

            def scores(t, b, par, bank):
                h0, h1 = HB[bank]
                n = (h1 - h0) * KL
                o = PS[:, 3 * par + bank, 0:n]
                if bank == 0:
                    pe.wait_ge(qTb_ok, t + 1)
                    wait(pe, sc_sub, 2 * (t - 1))
                mm(o, QTb[:, par, :], KB[:, b, h0 * KL:h1 * KL], stop=False)
                mm(o.rearrange("p (h k) -> p h k", k=KL), ones_b[:, :], bc(mrow[0:1, b, :].unsqueeze(1), [1, h1 - h0, KL]), start=False).then_inc(sc_ps, 1)

            def weights_T(t, par, g):
                if g < 2:
                    pe.wait_ge(exp_ok, 2 * t + 1 + g)
                wait(pe, pT_sb, 4 * t + g)
                for c in range(4 * g, min(4 * g + 4, NC)):
                    ins = nc.tensor.transpose(PS[0:CR[c], 6, (c - 4 * g) * P:(c - 4 * g + 1) * P],
                                              PR[:, par, c * P:c * P + CR[c]], ident[:, :])
                ins.then_inc(pT_ps, 1)

            def out_T(t):
                pe.wait_ge(on_ok, t + 1)
                nc.tensor.transpose(PS[:, 7, 256:384], ON[:, :], ident[:, :]).then_inc(oT_ps, 1)

            def out_proj(t):
                pe.wait_ge(oT_sb, t + 1)
                mm(PS[:, 7, 384:512], OT[:, :], WO[:, :]).then_inc(wo_ps, 1)

            for t in range(2):
                for bank in range(3):
                    scores(t, 0, t, bank)

            def ahead(t, b, q, bank):
                if not (isinstance(t, int) and t >= NT - 2):
                    scores(t + 2, b if q < Q - 2 else b + 1, q % 2, bank)

            def values_of(t, b, c0, c1):
                pe.wait_ge(pT_sb, 4 * t + (4 if c1 == NC else c1 // 4))
                if c0 == 0:
                    wait(pe, xs_ok, t)
                for c in range(c0, c1):
                    ins = mm(PS[:, 7, H0[c] * VW:(H0[c] + 3) * VW], PT[0:CR[c], c, :],
                             VX[0:CR[c], b, 3 * c:3 * c + 3, :].rearrange("p m w -> p (m w)"),
                             start=c == 0, stop=c == NC - 1, skip_group_check=True)
                if c1 == NC:
                    ins.then_inc(pv_ps, 1)

            def attend(b):
                for q in range(Q):
                    t, par = b * Q + q, q % 2
                    first = isinstance(t, int) and t == 0
                    weights_T(t, par, 0)
                    ahead(t, b, q, 0)
                    if not first:
                        out_T(t - 1)
                    weights_T(t, par, 1)
                    if not first:
                        out_proj(t - 1)
                    ahead(t, b, q, 1)
                    weights_T(t, par, 2)
                    ahead(t, b, q, 2)
                    values_of(t, b, 0, 4)
                    values_of(t, b, 4, 8)
                    values_of(t, b, 8, NC)
                    if isinstance(t, int) and t == NT - 1:
                        pe.wait_ge(sc_sub, 2 * NT)
                        x_T(BT)

            peeled(pe, BT, attend)
            out_T(NT - 1)
            out_proj(NT - 1)

            pe.wait_ge(wf_ok, 1)

            def gates(b):
                pe.wait_ge(xtl_ok, b + 1)
                for c in range(FC):
                    wait(pe, h_ok, FC * (b - 1) + c + 1)
                    for w, bank, done in ((WG, 1 + 2 * c, g_ps), (WU, 2 + 2 * c, u_ps)):
                        mm(PS[:, bank, :], w[:, c * P:(c + 1) * P], XTHs[:, b % 2, :], stop=False)
                        mm(PS[:, bank, :], w[:, c * P:(c + 1) * P], XTLs[:, b % 2, :], start=False).then_inc(done, 1)
                    if c == 0 and b + 1 < BT:
                        x_T(BT + b + 1)

            gates(0)
            for b in range(BT):
                if b + 1 < BT:
                    gates(b + 1)
                pe.wait_ge(h_ok, FC * (b + 1))
                pe.wait_ge(xs_ok, NT)
                wait(pe, x2_add, b)
                for q in range(Q):
                    for c in range(FC):
                        ins = mm(PS[:, 7, q * D:(q + 1) * D], HT[b % 2][:, c, q * P:(q + 1) * P], WD2[:, c, :],
                                 start=c == 0, stop=c == FC - 1)
                ins.then_inc(dn_ps, 1)

            pe.wait_ge(cn_ok, 1)
            pe.wait_ge(x2_add, BT)
            x_T(2 * BT, 0)
            x_T(2 * BT + 1, 7)
            for b in range(BT):
                pe.wait_ge(xT_sb, 2 * BT + b + 1)
                mm(PS[0:KR, 1 + b, :], CN2[:, b, :], XNT[:, b % 2, :], stop=False)
                pe.wait_ge(xsq_ok, b + 1)
                mm(PS[0:KR, 1 + b, :], ones_f[:, 0:KR], XSQ[:, b % 2, :], start=False).then_inc(d_ps, 1)
                if b + 2 < BT:
                    x_T(2 * BT + b + 2, 7 * (b % 2))

            pe.wait_ge(d_pos, BT)
            pe.wait_ge(f_ok, 2)
            for c in range(CC):
                ins = nc.tensor.transpose(PS[:, c // 6, c % 6 * 85:c % 6 * 85 + KR], FX[:, c:BT * SL:CC], ident[0:KR, 0:KR])
                if c % 6 == 5 or c == CC - 1:
                    ins.then_inc(fT_ps, 1)

            pe.wait_ge(c_all, 2)
            for i in range(KL - 1, -1, -1):
                pe.wait_ge(hit_ok, KL - i)
                mm(PS[:, 5, i:i + 1], blk1[:, :], hs[:, (KL - 1 - i) % 2:(KL - 1 - i) % 2 + 1]).then_inc(b_ps, 1)
            pe.wait_ge(bs_ok, 1)
            for j in range(2):
                ins = nc.tensor.transpose(PS[0:KL, 6, j * P:(j + 1) * P], BS[:, j:j + KL], ident[:, :])
            ins.then_inc(bT_ps, 1)

            for b in range(BT):
                pe.wait_ge(pm_ok, b + 1)
                for q in range(Q):
                    ins = mm(PS[:, 1 + b, q * D:(q + 1) * D], PM[0:KL, b % 2, q * P:(q + 1) * P], CK[0:KL, b, :])
                ins.then_inc(e_ps, 1)

            pe.wait_ge(ld_gate, 16)
            for b in range(BT + 1):
                if b < BT:
                    wait(pe, xT_sb, 3 * BT + b - 1)
                    x_T(3 * BT + b, 7 * (b % 2))
                if b > 0:
                    pe.wait_ge(xT_sb, 3 * BT + b)
                    wait(pe, lg_sb, b - 2)
                    for q in range(Q):
                        ins = mm(PS[:, 5 + (b - 1) % 2, 256 + q * NE:256 + (q + 1) * NE], XNT[:, (b - 1) % 2, q * P:(q + 1) * P], GW[:, :])
                    ins.then_inc(lg_ps, 1)

            pe.wait_ge(x3_ok, BT)
            pe.wait_ge(lg_sb, BT)
            pe.wait_ge(xT_sb, 4 * BT)
            pe.wait_ge(w_lo, NE)
            pe.wait_ge(ld_moe, 32)

            def first(m, b, e, c):
                wait(pe, ac_ok, m - 1)
                xh, xl = XTHs[:, b % 2, :], XTLs[:, b % 2, :]
                for j, done in ((0, eg_ps), (1, eu_ps)):
                    c0 = j * EI + c * P
                    o = PS[:, 2 * c + j, :]
                    mm(o, W13H[:, e, c0:c0 + P], xh, stop=False)
                    mm(o, W13H[:, e, c0:c0 + P], xl, start=False, stop=False)
                    mm(o, W13L[:, e, c0:c0 + P], xh, start=False).then_inc(done, 1)

            def second(n, e):
                pe.wait_ge(ac_ok, EC * n + EC)
                wait(pe, y_ok, n - 1)
                for q in range(Q):
                    for c in range(EC):
                        ins = mm(PS[:, 4 + e % 2, q * D:(q + 1) * D], HA[:, e % 2 * EC + c, q * P:(q + 1) * P], W2[:, EC * e + c, :],
                                 start=c == 0, stop=c == EC - 1)
                ins.then_inc(y_ps, 1)

            def experts(b):
                pe.wait_ge(xtl_ok, b + (BT + 1))
                for e in range(NE):
                    n = NE * b + e
                    for c in range(EC):
                        first(EC * n + c, b, e, c)
                    if not (isinstance(n, int) and n == 0):
                        second(n - 1, (e - 1) % NE)

            experts(0)
            with pe.Fori(1, BT) as b:
                experts(b)
            second(NE * BT - 1, NE - 1)


_OUTS = [((4, 512, 128), "float32")]


def kernel(**inputs):
    import numpy as _np
    import concourse.bacc as _bacc
    from concourse import mybir as _mybir
    from concourse.bass_utils import run_bass_kernel_spmd as _run

    g = {k: _np.asarray(v) for k, v in inputs.items()}
    ctx = g["ctx_1024"]
    w1, w3, w2 = g["L1_ffn_w1"], g["L1_ffn_w3"], g["L1_ffn_w2"]
    ne, ei, d = w1.shape
    w13 = _np.stack([w1, w3], axis=1).transpose(3, 0, 1, 2).reshape(d, ne * 2 * ei)
    named = [
        ("x", g["x"]), ("ctx_dt", ctx.transpose(2, 0, 1).reshape(d, -1)), ("ctx_kd", ctx),
        ("mask", g["mask_BxS2_ik0"]),
        ("wqT", g["L0_xattn_Wq"].T), ("bq", g["L0_xattn_bq"]), ("wkT", g["L0_xattn_Wk"].T), ("bk", g["L0_xattn_bk"]),
        ("wvT", g["L0_xattn_Wv"].T), ("bv", g["L0_xattn_bv"]), ("woT", g["L0_xattn_Wo"].T), ("bo", g["L0_xattn_bo"]),
        ("qw", g["L0_xattn_q_norm_w"]), ("kw", g["L0_xattn_k_norm_w"]),
        ("wgT", g["L0_ffn_w_gate"].T), ("wuT", g["L0_ffn_w_up"].T), ("wdT", g["L0_ffn_w_down"].T),
        ("gateT", g["L1_ffn_gate_w"].T), ("w13T", w13), ("w2T", w2.transpose(0, 2, 1).reshape(ne * ei, d)),
    ]
    nc = _bacc.Bacc("TRN2", target_bir_lowering=False, num_devices=1)
    arrays, args = {}, []
    for name, a in named:
        a = _np.ascontiguousarray(a)
        arrays[f"in_{name}_dram"] = a
        args.append(nc.dram_tensor(f"in_{name}_dram", a.shape, _mybir.dt.from_np(a.dtype), kind="ExternalInput").ap())
    for i, (shape, dtype) in enumerate(_OUTS):
        dt = _mybir.dt.from_np(_np.dtype(dtype))
        args.append(nc.dram_tensor(f"out_{i}_dram", shape, dt, kind="ExternalOutput").ap())
    build(nc, *args)
    r = _run(nc, [arrays], core_ids=[0])
    return r.results[0]["out_0_dram"]
```
